# Optimizing a Trainium2 kernel written in Bass

```python
import numpy as np
import jax
import jax.numpy as jnp

def _softmax(x, axis=-1):
    return jax.nn.softmax(x, axis=axis)

def _gelu(x):
    return jax.nn.gelu(x, approximate=True)

def _silu(x):
    return jax.nn.silu(x)

def _sigmoid(x):
    return jax.nn.sigmoid(x)

def _layernorm(x, axis=-1, eps=1e-05):
    m = jnp.mean(x, axis=axis, keepdims=True)
    v = jnp.var(x, axis=axis, keepdims=True)
    return (x - m) / jnp.sqrt(v + eps)

def _scatter_add(tgt, idx, src, axis=0):
    return tgt.at[idx].add(src)

def _segment_sum(src, seg, n):
    return jax.ops.segment_sum(src, seg, n)
kernel_name = 'mk_decoder_postln_d4_seqx_r8_01f4f5'

def setup_inputs(seed: int=0):
    np.random.seed(seed)
    _w = jnp.asarray

    def _rec_inputs():
        import jax
        import jax.numpy as jnp
        _rk = jax.random.key(seed)
        x = 7.22e-05 + 1 * jax.random.normal(jax.random.fold_in(_rk, 1), (16, 128, 128), jnp.float32)
        _lenS = 128 - jax.random.randint(jax.random.fold_in(_rk, 7), (16,), 0, max(1, 128 // 4) + 1, jnp.int32)
        _lenS2 = 128 - jax.random.randint(jax.random.fold_in(_rk, 8), (16,), 0, max(1, 128 // 4) + 1, jnp.int32)
        _ctx_1024P = jax.random.normal(jax.random.fold_in(_rk, 11), (16, 16, 128), jnp.float32)
        _ctx_1024c = jax.random.dirichlet(jax.random.fold_in(_rk, 511), 0.3 * jnp.ones((16,), jnp.float32), (16, 128))
        _ctx_1024t = jnp.einsum('bsk,bkd->bsd', _ctx_1024c, _ctx_1024P)
        _ctx_1024t = _ctx_1024t * jax.lax.rsqrt(jnp.mean(jnp.square(_ctx_1024t)) + 1e-12) * 0.953939
        ctx_1024 = 4.13588e-05 + 0.999923 * (_ctx_1024t + 0.3 * jax.random.normal(jax.random.fold_in(_rk, 611), (16, 128, 128), jnp.float32))
        _validS = jnp.arange(128)[None, :] < _lenS[:, None]
        _validS2 = jnp.arange(128)[None, :] < _lenS2[:, None]
        _causal = jnp.tril(jnp.ones((128, 128), dtype=bool))
        mask_BxS2_bk1 = jnp.broadcast_to(_validS2[:, :], (16, 128))
        mask_BxS2_bk0 = jnp.logical_not(jnp.broadcast_to(_validS2[:, :], (16, 128)))
        return (x, ctx_1024, mask_BxS2_bk1, mask_BxS2_bk0)
    x, ctx_1024, mask_BxS2_bk1, mask_BxS2_bk0 = _rec_inputs()

    def _L0_attn_setup():
        import jax, jax.numpy as jnp
        import numpy as np
        import math
        NUM_HEADS = 8
        EMB = 128
        HEAD_DIM = 128
        B, T = (1, 512)

        def sinusoidal_pe(T, d, dtype=jnp.float32):
            pos = jnp.arange(T, dtype=dtype)[:, None]
            inv_freq = jnp.exp(-math.log(10000.0) * jnp.arange(0, d, 2, dtype=dtype) / d)
            ang = pos * inv_freq[None, :]
            pe = jnp.zeros((T, d), dtype=dtype)
            pe = pe.at[:, 0::2].set(jnp.sin(ang))
            pe = pe.at[:, 1::2].set(jnp.cos(ang))
            return pe
        key = jax.random.key(seed)
        ks = jax.random.split(key, 6)
        s = lambda fan_in: 1.0 / math.sqrt(fan_in)
        x = jax.random.normal(ks[0], (B, T, EMB), dtype=jnp.float32)
        Wq = jax.random.normal(ks[1], (EMB, NUM_HEADS * HEAD_DIM), dtype=jnp.float32) * s(EMB)
        bq = jax.random.normal(ks[2], (NUM_HEADS * HEAD_DIM,), dtype=jnp.float32) * s(EMB)
        Wkv = jax.random.normal(ks[3], (EMB, 2 * HEAD_DIM), dtype=jnp.float32) * s(EMB)
        bkv = jax.random.normal(ks[4], (2 * HEAD_DIM,), dtype=jnp.float32) * s(EMB)
        Wo = jax.random.normal(ks[5], (NUM_HEADS * HEAD_DIM, EMB), dtype=jnp.float32) * s(NUM_HEADS * HEAD_DIM)
        return {'x': x, 'Wq': Wq, 'bq': bq, 'Wkv': Wkv, 'bkv': bkv, 'Wo': Wo}
    _L0_attn_all = _L0_attn_setup()
    _L0_attn_in = {k: v for k, v in _L0_attn_all.items() if k in ('Wq', 'bq', 'Wkv', 'bkv', 'Wo')}
    del _L0_attn_all

    def _L0_xattn_setup():
        import jax, jax.numpy as jnp
        import numpy as np
        D_MODEL = 128
        NUM_HEAD = 16
        HEAD_DIM = D_MODEL // NUM_HEAD
        B, S = (4, 256)
        key = jax.random.key(seed)
        ks = jax.random.split(key, 8)
        sc = 0.02
        return {'q_in': jax.random.normal(ks[0], (B, S, D_MODEL), jnp.float32), 'k_in': jax.random.normal(ks[1], (B, S, D_MODEL), jnp.float32), 'v_in': jax.random.normal(ks[2], (B, S, D_MODEL), jnp.float32), 'Wq': jax.random.normal(ks[3], (D_MODEL, D_MODEL), jnp.float32) * sc, 'bq': jnp.zeros((D_MODEL,), jnp.float32), 'Wk': jax.random.normal(ks[4], (D_MODEL, D_MODEL), jnp.float32) * sc, 'bk': jnp.zeros((D_MODEL,), jnp.float32), 'Wv': jax.random.normal(ks[5], (D_MODEL, D_MODEL), jnp.float32) * sc, 'bv': jnp.zeros((D_MODEL,), jnp.float32), 'Wo': jax.random.normal(ks[6], (D_MODEL, D_MODEL), jnp.float32) * sc, 'bo': jnp.zeros((D_MODEL,), jnp.float32)}
    _L0_xattn_all = _L0_xattn_setup()
    _L0_xattn_in = {k: v for k, v in _L0_xattn_all.items() if k in ('Wq', 'bq', 'Wk', 'bk', 'Wv', 'bv', 'Wo', 'bo')}
    del _L0_xattn_all

    def _L0_ffn_setup():
        import jax, jax.numpy as jnp
        import numpy as np
        D_MODEL, D_FF, N_EXPERTS, TOP_K = (128, 256, 8, 2)
        B, S = (2, 256)
        key = jax.random.key(seed)
        ks = jax.random.split(key, 6)
        sd = 1.0 / np.sqrt(D_MODEL)
        sf = 1.0 / np.sqrt(D_FF)
        return {'x': jax.random.normal(ks[0], (B, S, D_MODEL), jnp.float32), 'router_w': jax.random.normal(ks[1], (N_EXPERTS, D_MODEL), jnp.float32) * sd, 'gate_w': jax.random.normal(ks[2], (N_EXPERTS, D_MODEL, D_FF), jnp.float32) * sd, 'gate_b': jnp.zeros((N_EXPERTS, D_FF), jnp.float32), 'up_w': jax.random.normal(ks[3], (N_EXPERTS, D_MODEL, D_FF), jnp.float32) * sd, 'up_b': jnp.zeros((N_EXPERTS, D_FF), jnp.float32), 'down_w': jax.random.normal(ks[4], (N_EXPERTS, D_FF, D_MODEL), jnp.float32) * sf, 'down_b': jnp.zeros((N_EXPERTS, D_MODEL), jnp.float32)}
    _L0_ffn_all = _L0_ffn_setup()
    _L0_ffn_in = {k: v for k, v in _L0_ffn_all.items() if k in ('router_w', 'gate_w', 'gate_b', 'up_w', 'up_b', 'down_w', 'down_b')}
    del _L0_ffn_all

    def _L1_attn_setup():
        import jax, jax.numpy as jnp
        import numpy as np
        NUM_HEADS = 16
        WINDOW = 64

        def _rel_pos_bias(rel_bias, window):
            coords = jnp.arange(window)
            rel = coords[:, None] - coords[None, :] + (window - 1)
            bias = rel_bias[rel]
            return jnp.transpose(bias, (2, 0, 1))
        key = jax.random.key(seed)
        ks = jax.random.split(key, 5)
        B, S, D = (8, 512, 128)
        x = jax.random.normal(ks[0], (B, S, D), dtype=jnp.float32)
        qkv_w = jax.random.normal(ks[1], (D, 3 * D), dtype=jnp.float32) * (1.0 / np.sqrt(D))
        qkv_b = jnp.zeros((3 * D,), dtype=jnp.float32)
        proj_w = jax.random.normal(ks[2], (D, D), dtype=jnp.float32) * (1.0 / np.sqrt(D))
        proj_b = jnp.zeros((D,), dtype=jnp.float32)
        rel_bias = jax.random.normal(ks[3], (2 * WINDOW - 1, NUM_HEADS), dtype=jnp.float32) * 0.02
        return {'x': x, 'qkv_w': qkv_w, 'qkv_b': qkv_b, 'proj_w': proj_w, 'proj_b': proj_b, 'rel_bias': rel_bias}
    _L1_attn_all = _L1_attn_setup()
    _L1_attn_in = {k: v for k, v in _L1_attn_all.items() if k in ('qkv_w', 'qkv_b', 'proj_w', 'proj_b', 'rel_bias')}
    del _L1_attn_all

    def _L1_xattn_setup():
        import jax, jax.numpy as jnp
        import numpy as np
        D_MODEL = 128
        NUM_HEADS = 16
        HEAD_DIM = D_MODEL // NUM_HEADS
        key = jax.random.key(seed)
        ks = jax.random.split(key, 10)
        B, SQ, SK = (2, 256, 256)
        scale = 1.0 / np.sqrt(D_MODEL)
        inp = {'x1': jax.random.normal(ks[0], (B, SQ, D_MODEL), jnp.float32), 'x2': jax.random.normal(ks[1], (B, SK, D_MODEL), jnp.float32), 'Wq': jax.random.normal(ks[2], (D_MODEL, D_MODEL), jnp.float32) * scale, 'bq': jnp.zeros((D_MODEL,), jnp.float32), 'Wk': jax.random.normal(ks[3], (D_MODEL, D_MODEL), jnp.float32) * scale, 'bk': jnp.zeros((D_MODEL,), jnp.float32), 'Wv': jax.random.normal(ks[4], (D_MODEL, D_MODEL), jnp.float32) * scale, 'bv': jnp.zeros((D_MODEL,), jnp.float32), 'Wo': jax.random.normal(ks[5], (D_MODEL, D_MODEL), jnp.float32) * scale, 'bo': jnp.zeros((D_MODEL,), jnp.float32)}
        return inp
    _L1_xattn_all = _L1_xattn_setup()
    _L1_xattn_in = {k: v for k, v in _L1_xattn_all.items() if k in ('Wq', 'bq', 'Wk', 'bk', 'Wv', 'bv', 'Wo', 'bo')}
    del _L1_xattn_all

    def _L1_ffn_setup():
        import jax, jax.numpy as jnp
        import numpy as np
        B, S, D = (4, 256, 128)
        O = 128
        E = 8
        K = 2
        key = jax.random.key(seed)
        k1, k2, k3, k4, k5 = jax.random.split(key, 5)
        scale = 1.0 / np.sqrt(D)
        x = jax.random.normal(k1, (B, S, D), dtype=jnp.float32)
        We = jax.random.uniform(k2, (E, D, O), dtype=jnp.float32, minval=-scale, maxval=scale)
        be = jax.random.uniform(k3, (E, O), dtype=jnp.float32, minval=-scale, maxval=scale)
        Wg = jax.random.uniform(k4, (D, E), dtype=jnp.float32, minval=-scale, maxval=scale)
        bg = jax.random.uniform(k5, (E,), dtype=jnp.float32, minval=-scale, maxval=scale)
        return {'x': x, 'We': We, 'be': be, 'Wg': Wg, 'bg': bg}
    _L1_ffn_all = _L1_ffn_setup()
    _L1_ffn_in = {k: v for k, v in _L1_ffn_all.items() if k in ('We', 'be', 'Wg', 'bg')}
    del _L1_ffn_all

    def _L2_attn_setup():
        import jax, jax.numpy as jnp
        import numpy as np
        NUM_HEADS = 16
        D_MODEL = 128
        D_K = D_MODEL // NUM_HEADS
        MAX_SEQ_LEN = 512
        ROPE_BASE = 10000.0
        BATCH = 2
        SEQ_LEN = 256

        def _rope_tables(seq_len, d_k, base=ROPE_BASE):
            theta = 1.0 / base ** (jnp.arange(0, d_k, 2, dtype=jnp.float32) / d_k)
            m = jnp.arange(seq_len, dtype=jnp.float32)
            m_theta = jnp.outer(m, theta)
            ang = jnp.concatenate([m_theta, m_theta], axis=-1)
            return (jnp.cos(ang), jnp.sin(ang))

        def _apply_rope(x, cos, sin):
            d2 = x.shape[-1] // 2
            x1, x2 = (x[..., :d2], x[..., d2:])
            x_flip = jnp.concatenate([-x2, x1], axis=-1)
            return x * cos + x_flip * sin
        key = jax.random.key(seed)
        kx, kq, kk, kv, ko = jax.random.split(key, 5)
        s = 1.0 / np.sqrt(D_MODEL)
        x = jax.random.normal(kx, (BATCH, SEQ_LEN, D_MODEL), dtype=jnp.float32)
        W_Q = jax.random.uniform(kq, (D_MODEL, D_MODEL), jnp.float32, -s, s)
        W_K = jax.random.uniform(kk, (D_MODEL, D_MODEL), jnp.float32, -s, s)
        W_V = jax.random.uniform(kv, (D_MODEL, D_MODEL), jnp.float32, -s, s)
        W_O = jax.random.uniform(ko, (D_MODEL, D_MODEL), jnp.float32, -s, s)
        return {'x': x, 'W_Q': W_Q, 'W_K': W_K, 'W_V': W_V, 'W_O': W_O}
    _L2_attn_all = _L2_attn_setup()
    _L2_attn_in = {k: v for k, v in _L2_attn_all.items() if k in ('W_Q', 'W_K', 'W_V', 'W_O')}
    del _L2_attn_all

    def _L2_xattn_setup():
        import jax, jax.numpy as jnp
        import numpy as np
        B, N, M = (4, 128, 512)
        DQ, DC = (128, 128)
        H, DH = (16, 64)
        INNER = H * DH
        SCALE = DH ** (-0.5)
        key = jax.random.key(seed)
        ks = jax.random.split(key, 6)
        x = jax.random.normal(ks[0], (B, N, DQ), dtype=jnp.float32)
        context = jax.random.normal(ks[1], (B, M, DC), dtype=jnp.float32)
        mask = jax.random.bernoulli(ks[2], 0.9, (B, M))
        Wq = jax.random.normal(ks[3], (DQ, INNER), dtype=jnp.float32) / np.sqrt(DQ)
        Wkv = jax.random.normal(ks[4], (DC, 2 * INNER), dtype=jnp.float32) / np.sqrt(DC)
        Wo = jax.random.normal(ks[5], (INNER, DQ), dtype=jnp.float32) / np.sqrt(INNER)
        bo = jnp.zeros((DQ,), dtype=jnp.float32)
        return {'x': x, 'context': context, 'mask': mask, 'Wq': Wq, 'Wkv': Wkv, 'Wo': Wo, 'bo': bo}
    _L2_xattn_all = _L2_xattn_setup()
    _L2_xattn_in = {k: v for k, v in _L2_xattn_all.items() if k in ('Wq', 'Wkv', 'Wo', 'bo')}
    del _L2_xattn_all

    def _L2_ffn_setup():
        import jax, jax.numpy as jnp
        import numpy as np
        BLOCK = 32
        W_BITS = 4
        ACT_BITS = 16

        def act_qdq(x):
            qmax = 2.0 ** (ACT_BITS - 1) - 1.0
            scale = jnp.maximum(jnp.max(jnp.abs(x)) / qmax, 1e-12)
            return jnp.clip(jnp.round(x / scale), -qmax - 1.0, qmax) * scale

        def fixed_qdq_u16(x):
            scale = 1.0 / 65536.0
            return jnp.clip(jnp.round(x / scale), 0.0, 65535.0) * scale

        def lpbq_dequant(w):
            O, I = w.shape
            qmax = 2.0 ** (W_BITS - 1) - 1.0
            wb = w.reshape(O, I // BLOCK, BLOCK)
            s = jnp.maximum(jnp.max(jnp.abs(wb), axis=-1, keepdims=True) / qmax, 1e-12)
            wq = jnp.clip(jnp.round(wb / s), -qmax - 1.0, qmax) * s
            return wq.reshape(O, I)
        key = jax.random.key(seed)
        k1, k2, k3, k4 = jax.random.split(key, 4)
        B, S, H, I = (2, 512, 128, 384)
        x = jax.random.normal(k1, (B, S, H), jnp.float32)
        w_gate = jax.random.normal(k2, (I, H), jnp.float32) * 0.02
        w_up = jax.random.normal(k3, (I, H), jnp.float32) * 0.02
        w_down = jax.random.normal(k4, (H, I), jnp.float32) * 0.02
        return {'x': x, 'w_gate': w_gate, 'w_up': w_up, 'w_down': w_down}
    _L2_ffn_all = _L2_ffn_setup()
    _L2_ffn_in = {k: v for k, v in _L2_ffn_all.items() if k in ('w_gate', 'w_up', 'w_down')}
    del _L2_ffn_all

    def _L3_attn_setup():
        import jax, jax.numpy as jnp
        import numpy as np
        D_MODEL = 128
        NUM_HEADS = 16
        HEAD_DIM = D_MODEL // NUM_HEADS
        THETA = 10000.0
        B, S = (2, 256)

        def _apply_rope(t, cos, sin):
            te = t[..., 0::2]
            to = t[..., 1::2]
            re = te * cos - to * sin
            ro = te * sin + to * cos
            out = jnp.stack([re, ro], axis=-1)
            return out.reshape(t.shape)
        key = jax.random.key(seed)
        kx, kq, kk, kv, ko = jax.random.split(key, 5)
        std = 2.0 / (2 * D_MODEL) ** 0.5

        def w(k):
            return jnp.clip(std * jax.random.normal(k, (D_MODEL, D_MODEL), jnp.float32), -3.0 * std, 3.0 * std)
        return {'x': jax.random.normal(kx, (B, S, D_MODEL), jnp.float32), 'Wq': w(kq), 'Wk': w(kk), 'Wv': w(kv), 'Wo': w(ko)}
    _L3_attn_all = _L3_attn_setup()
    _L3_attn_in = {k: v for k, v in _L3_attn_all.items() if k in ('Wq', 'Wk', 'Wv', 'Wo')}
    del _L3_attn_all

    def _L3_xattn_setup():
        import jax, jax.numpy as jnp
        import numpy as np
        EPS = 1e-05

        def layer_norm(x, g, b):
            mu = jnp.mean(x, axis=-1, keepdims=True)
            var = jnp.mean((x - mu) ** 2, axis=-1, keepdims=True)
            return (x - mu) * jax.lax.rsqrt(var + EPS) * g + b
        key = jax.random.key(seed)
        ks = jax.random.split(key, 8)
        b, n, l, D = (8, 512, 64, 128)
        heads, dim_head = (16, 64)
        inner = heads * dim_head
        x = jax.random.normal(ks[0], (b, n, D), dtype=jnp.float32)
        latents = jax.random.normal(ks[1], (b, l, D), dtype=jnp.float32)
        mask = jax.random.randint(ks[2], (b, n), 0, 2) > 0
        Wq = jax.random.normal(ks[3], (D, inner), dtype=jnp.float32) * D ** (-0.5)
        Wkv = jax.random.normal(ks[4], (D, 2 * inner), dtype=jnp.float32) * D ** (-0.5)
        Wout = jax.random.normal(ks[5], (inner, D), dtype=jnp.float32) * inner ** (-0.5)
        g1 = jnp.ones((D,), jnp.float32)
        b1 = jnp.zeros((D,), jnp.float32)
        g2 = jnp.ones((D,), jnp.float32)
        b2 = jnp.zeros((D,), jnp.float32)
        return {'x': x, 'latents': latents, 'mask': mask, 'g1': g1, 'b1': b1, 'g2': g2, 'b2': b2, 'Wq': Wq, 'Wkv': Wkv, 'Wout': Wout}
    _L3_xattn_all = _L3_xattn_setup()
    _L3_xattn_in = {k: v for k, v in _L3_xattn_all.items() if k in ('g1', 'b1', 'g2', 'b2', 'Wq', 'Wkv', 'Wout')}
    del _L3_xattn_all

    def _L3_ffn_setup():
        import jax, jax.numpy as jnp
        import numpy as np
        B, S, H, F, G = (8, 256, 128, 512, 128)
        EPS = 1e-05

        def _dequant(q, scales, g):
            K, N = q.shape
            w = (q.astype(jnp.float32) - 128.0).reshape(K // g, g, N) * scales[:, None, :]
            return w.reshape(K, N)
        key = jax.random.key(seed)
        ks = jax.random.split(key, 8)
        x = jax.random.normal(ks[0], (B, S, H), dtype=jnp.float32)
        ln_gamma = jnp.ones((H,), jnp.float32)
        ln_beta = jnp.zeros((H,), jnp.float32)
        fc1_q = jax.random.randint(ks[1], (H, F), 0, 32, dtype=jnp.int32)
        fc2_q = jax.random.randint(ks[2], (F, H), 0, 32, dtype=jnp.int32)
        fc1_scales = jax.random.uniform(ks[3], (H // G, F), jnp.float32) * 0.02 + 0.001
        fc2_scales = jax.random.uniform(ks[4], (F // G, H), jnp.float32) * 0.02 + 0.001
        fc1_bias = jax.random.normal(ks[5], (F,), jnp.float32) * 0.02
        fc2_bias = jax.random.normal(ks[6], (H,), jnp.float32) * 0.02
        return {'x': x, 'ln_gamma': ln_gamma, 'ln_beta': ln_beta, 'fc1_q': fc1_q, 'fc1_scales': fc1_scales, 'fc1_bias': fc1_bias, 'fc2_q': fc2_q, 'fc2_scales': fc2_scales, 'fc2_bias': fc2_bias}
    _L3_ffn_all = _L3_ffn_setup()
    _L3_ffn_in = {k: v for k, v in _L3_ffn_all.items() if k in ('ln_gamma', 'ln_beta', 'fc1_q', 'fc1_scales', 'fc1_bias', 'fc2_q', 'fc2_scales', 'fc2_bias')}
    del _L3_ffn_all
    return {'x': x, 'ctx_1024': ctx_1024, 'mask_BxS2_bk1': mask_BxS2_bk1, 'mask_BxS2_bk0': mask_BxS2_bk0, 'L0_attn_Wq': _L0_attn_in['Wq'], 'L0_attn_bq': _L0_attn_in['bq'], 'L0_attn_Wkv': _L0_attn_in['Wkv'], 'L0_attn_bkv': _L0_attn_in['bkv'], 'L0_attn_Wo': _L0_attn_in['Wo'], 'L0_xattn_Wq': _L0_xattn_in['Wq'], 'L0_xattn_bq': _L0_xattn_in['bq'], 'L0_xattn_Wk': _L0_xattn_in['Wk'], 'L0_xattn_bk': _L0_xattn_in['bk'], 'L0_xattn_Wv': _L0_xattn_in['Wv'], 'L0_xattn_bv': _L0_xattn_in['bv'], 'L0_xattn_Wo': _L0_xattn_in['Wo'], 'L0_xattn_bo': _L0_xattn_in['bo'], 'L0_ffn_router_w': _L0_ffn_in['router_w'], 'L0_ffn_gate_w': _L0_ffn_in['gate_w'], 'L0_ffn_gate_b': _L0_ffn_in['gate_b'], 'L0_ffn_up_w': _L0_ffn_in['up_w'], 'L0_ffn_up_b': _L0_ffn_in['up_b'], 'L0_ffn_down_w': _L0_ffn_in['down_w'], 'L0_ffn_down_b': _L0_ffn_in['down_b'], 'L1_attn_qkv_w': _L1_attn_in['qkv_w'], 'L1_attn_qkv_b': _L1_attn_in['qkv_b'], 'L1_attn_proj_w': _L1_attn_in['proj_w'], 'L1_attn_proj_b': _L1_attn_in['proj_b'], 'L1_attn_rel_bias': _L1_attn_in['rel_bias'], 'L1_xattn_Wq': _L1_xattn_in['Wq'], 'L1_xattn_bq': _L1_xattn_in['bq'], 'L1_xattn_Wk': _L1_xattn_in['Wk'], 'L1_xattn_bk': _L1_xattn_in['bk'], 'L1_xattn_Wv': _L1_xattn_in['Wv'], 'L1_xattn_bv': _L1_xattn_in['bv'], 'L1_xattn_Wo': _L1_xattn_in['Wo'], 'L1_xattn_bo': _L1_xattn_in['bo'], 'L1_ffn_We': _L1_ffn_in['We'], 'L1_ffn_be': _L1_ffn_in['be'], 'L1_ffn_Wg': _L1_ffn_in['Wg'], 'L1_ffn_bg': _L1_ffn_in['bg'], 'L2_attn_W_Q': _L2_attn_in['W_Q'], 'L2_attn_W_K': _L2_attn_in['W_K'], 'L2_attn_W_V': _L2_attn_in['W_V'], 'L2_attn_W_O': _L2_attn_in['W_O'], 'L2_xattn_Wq': _L2_xattn_in['Wq'], 'L2_xattn_Wkv': _L2_xattn_in['Wkv'], 'L2_xattn_Wo': _L2_xattn_in['Wo'], 'L2_xattn_bo': _L2_xattn_in['bo'], 'L2_ffn_w_gate': _L2_ffn_in['w_gate'], 'L2_ffn_w_up': _L2_ffn_in['w_up'], 'L2_ffn_w_down': _L2_ffn_in['w_down'], 'L3_attn_Wq': _L3_attn_in['Wq'], 'L3_attn_Wk': _L3_attn_in['Wk'], 'L3_attn_Wv': _L3_attn_in['Wv'], 'L3_attn_Wo': _L3_attn_in['Wo'], 'L3_xattn_g1': _L3_xattn_in['g1'], 'L3_xattn_b1': _L3_xattn_in['b1'], 'L3_xattn_g2': _L3_xattn_in['g2'], 'L3_xattn_b2': _L3_xattn_in['b2'], 'L3_xattn_Wq': _L3_xattn_in['Wq'], 'L3_xattn_Wkv': _L3_xattn_in['Wkv'], 'L3_xattn_Wout': _L3_xattn_in['Wout'], 'L3_ffn_ln_gamma': _L3_ffn_in['ln_gamma'], 'L3_ffn_ln_beta': _L3_ffn_in['ln_beta'], 'L3_ffn_fc1_q': _L3_ffn_in['fc1_q'], 'L3_ffn_fc1_scales': _L3_ffn_in['fc1_scales'], 'L3_ffn_fc1_bias': _L3_ffn_in['fc1_bias'], 'L3_ffn_fc2_q': _L3_ffn_in['fc2_q'], 'L3_ffn_fc2_scales': _L3_ffn_in['fc2_scales'], 'L3_ffn_fc2_bias': _L3_ffn_in['fc2_bias']}

def reference(x, ctx_1024, mask_BxS2_bk1, mask_BxS2_bk0, L0_attn_Wq, L0_attn_bq, L0_attn_Wkv, L0_attn_bkv, L0_attn_Wo, L0_xattn_Wq, L0_xattn_bq, L0_xattn_Wk, L0_xattn_bk, L0_xattn_Wv, L0_xattn_bv, L0_xattn_Wo, L0_xattn_bo, L0_ffn_router_w, L0_ffn_gate_w, L0_ffn_gate_b, L0_ffn_up_w, L0_ffn_up_b, L0_ffn_down_w, L0_ffn_down_b, L1_attn_qkv_w, L1_attn_qkv_b, L1_attn_proj_w, L1_attn_proj_b, L1_attn_rel_bias, L1_xattn_Wq, L1_xattn_bq, L1_xattn_Wk, L1_xattn_bk, L1_xattn_Wv, L1_xattn_bv, L1_xattn_Wo, L1_xattn_bo, L1_ffn_We, L1_ffn_be, L1_ffn_Wg, L1_ffn_bg, L2_attn_W_Q, L2_attn_W_K, L2_attn_W_V, L2_attn_W_O, L2_xattn_Wq, L2_xattn_Wkv, L2_xattn_Wo, L2_xattn_bo, L2_ffn_w_gate, L2_ffn_w_up, L2_ffn_w_down, L3_attn_Wq, L3_attn_Wk, L3_attn_Wv, L3_attn_Wo, L3_xattn_g1, L3_xattn_b1, L3_xattn_g2, L3_xattn_b2, L3_xattn_Wq, L3_xattn_Wkv, L3_xattn_Wout, L3_ffn_ln_gamma, L3_ffn_ln_beta, L3_ffn_fc1_q, L3_ffn_fc1_scales, L3_ffn_fc1_bias, L3_ffn_fc2_q, L3_ffn_fc2_scales, L3_ffn_fc2_bias):
    import jax
    import jax.numpy as jnp

    def _L0_attn_ref(x, Wq, bq, Wkv, bkv, Wo):
        import jax, jax.numpy as jnp
        import numpy as np
        import math
        NUM_HEADS = 8
        EMB = 128
        HEAD_DIM = 128
        B, T = (1, 512)

        def sinusoidal_pe(T, d, dtype=jnp.float32):
            pos = jnp.arange(T, dtype=dtype)[:, None]
            inv_freq = jnp.exp(-math.log(10000.0) * jnp.arange(0, d, 2, dtype=dtype) / d)
            ang = pos * inv_freq[None, :]
            pe = jnp.zeros((T, d), dtype=dtype)
            pe = pe.at[:, 0::2].set(jnp.sin(ang))
            pe = pe.at[:, 1::2].set(jnp.cos(ang))
            return pe
        Bsz, Tlen, E = x.shape
        q = (x @ Wq + bq).reshape(Bsz, Tlen, NUM_HEADS, HEAD_DIM)
        kv = x @ Wkv + bkv
        k, v = (kv[..., :HEAD_DIM], kv[..., HEAD_DIM:])
        q = jnp.transpose(q, (0, 2, 1, 3))
        pe = sinusoidal_pe(Tlen, HEAD_DIM, x.dtype)
        q = q + pe[None, None, :, :]
        k = k + pe[None, :, :]
        scale = 1.0 / math.sqrt(HEAD_DIM)
        scores = jnp.einsum('bhqd,bkd->bhqk', q, k) * scale
        causal = jnp.tril(jnp.ones((Tlen, Tlen), dtype=bool))
        scores = jnp.where(causal[None, None, :, :], scores, jnp.finfo(scores.dtype).min)
        probs = jax.nn.softmax(scores, axis=-1)
        attn = jnp.einsum('bhqk,bkd->bhqd', probs, v)
        out = jnp.transpose(attn, (0, 2, 1, 3)).reshape(Bsz, Tlen, NUM_HEADS * HEAD_DIM)
        return out @ Wo

    def _L0_xattn_ref(q_in, k_in, v_in, Wq, bq, Wk, bk, Wv, bv, Wo, bo):
        import jax, jax.numpy as jnp
        import numpy as np
        D_MODEL = 128
        NUM_HEAD = 16
        HEAD_DIM = D_MODEL // NUM_HEAD
        B, S = (4, 256)
        b, sq, _ = q_in.shape
        sk = k_in.shape[1]
        Q = q_in @ Wq + bq
        K = k_in @ Wk + bk
        V = v_in @ Wv + bv
        Q = Q.reshape(b, sq, NUM_HEAD, HEAD_DIM).transpose(0, 2, 1, 3)
        K = K.reshape(b, sk, NUM_HEAD, HEAD_DIM).transpose(0, 2, 1, 3)
        V = V.reshape(b, sk, NUM_HEAD, HEAD_DIM).transpose(0, 2, 1, 3)
        scale = 1.0 / jnp.sqrt(jnp.float32(HEAD_DIM))
        scores = jnp.einsum('bhqd,bhkd->bhqk', Q, K) * scale
        causal = jnp.arange(sk)[None, :] <= jnp.arange(sq)[:, None]
        scores = jnp.where(causal[None, None], scores, -jnp.inf)
        attn = jax.nn.softmax(scores, axis=-1)
        out = jnp.einsum('bhqk,bhkd->bhqd', attn, V)
        out = out.transpose(0, 2, 1, 3).reshape(b, sq, D_MODEL)
        return out @ Wo + bo

    def _L0_ffn_ref(x, router_w, gate_w, gate_b, up_w, up_b, down_w, down_b):
        import jax, jax.numpy as jnp
        import numpy as np
        D_MODEL, D_FF, N_EXPERTS, TOP_K = (128, 256, 8, 2)
        B, S = (2, 256)
        b, s, d = x.shape
        xf = x.reshape(b * s, d)
        n = xf.shape[0]
        router_logits = xf @ router_w.T
        probs = jax.nn.softmax(router_logits, axis=-1)
        topv, topi = jax.lax.top_k(probs, TOP_K)
        mask = jnp.zeros_like(probs).at[jnp.arange(n)[:, None], topi].set(1.0)
        probs = probs * mask
        probs = probs / (probs.sum(axis=-1, keepdims=True) + 1e-09)
        g = jnp.einsum('nd,edf->nef', xf, gate_w) + gate_b
        u = jnp.einsum('nd,edf->nef', xf, up_w) + up_b
        h = jax.nn.silu(g) * u
        expert_out = jnp.einsum('nef,efd->ned', h, down_w) + down_b
        y = jnp.einsum('ne,ned->nd', probs, expert_out)
        return y.reshape(b, s, d)

    def _L1_attn_ref(x, qkv_w, qkv_b, proj_w, proj_b, rel_bias):
        import jax, jax.numpy as jnp
        import numpy as np
        NUM_HEADS = 16
        WINDOW = 64

        def _rel_pos_bias(rel_bias, window):
            coords = jnp.arange(window)
            rel = coords[:, None] - coords[None, :] + (window - 1)
            bias = rel_bias[rel]
            return jnp.transpose(bias, (2, 0, 1))
        B, S, D = x.shape
        H, W = (NUM_HEADS, WINDOW)
        hd = D // H
        nW = S // W
        scale = 1.0 / np.sqrt(hd)
        xw = x.reshape(B, nW, W, D)
        qkv = xw @ qkv_w + qkv_b
        qkv = qkv.reshape(B, nW, W, 3, H, hd)
        q, k, v = (qkv[..., 0, :, :], qkv[..., 1, :, :], qkv[..., 2, :, :])
        attn = jnp.einsum('bnqhd,bnkhd->bnhqk', q, k) * scale
        attn = attn + _rel_pos_bias(rel_bias, W)[None, None]
        attn = jax.nn.softmax(attn, axis=-1)
        out = jnp.einsum('bnhqk,bnkhd->bnqhd', attn, v)
        out = out.reshape(B, S, D)
        return out @ proj_w + proj_b

    def _L1_xattn_ref(x1, x2, Wq, bq, Wk, bk, Wv, bv, Wo, bo):
        import jax, jax.numpy as jnp
        import numpy as np
        D_MODEL = 128
        NUM_HEADS = 16
        HEAD_DIM = D_MODEL // NUM_HEADS
        B, SQ, _ = x1.shape
        SK = x2.shape[1]

        def split_heads(t, S):
            return t.reshape(B, S, NUM_HEADS, HEAD_DIM).transpose(0, 2, 1, 3)
        Q = split_heads(x1 @ Wq + bq, SQ)
        K = split_heads(x2 @ Wk + bk, SK)
        V = split_heads(x2 @ Wv + bv, SK)
        scores = jnp.einsum('bhqd,bhkd->bhqk', Q, K) / jnp.sqrt(jnp.asarray(HEAD_DIM, Q.dtype))
        attn = jax.nn.softmax(scores, axis=-1)
        ctx = jnp.einsum('bhqk,bhkd->bhqd', attn, V)
        ctx = ctx.transpose(0, 2, 1, 3).reshape(B, SQ, D_MODEL)
        return ctx @ Wo + bo

    def _L1_ffn_ref(x, We, be, Wg, bg):
        import jax, jax.numpy as jnp
        import numpy as np
        B, S, D = (4, 256, 128)
        O = 128
        E = 8
        K = 2
        b, s, d = x.shape
        x_flat = x.reshape(-1, d)
        gates = jax.nn.softmax(x_flat @ Wg + bg, axis=-1)
        topk_gates, topk_idx = jax.lax.top_k(gates, K)
        topk_gates = topk_gates / jnp.sum(topk_gates, axis=1, keepdims=True)
        expert_out = jnp.einsum('nd,edo->neo', x_flat, We) + be
        selected = jnp.take_along_axis(expert_out, topk_idx[:, :, None], axis=1)
        out = jnp.sum(selected * topk_gates[:, :, None], axis=1)
        return out.reshape(b, s, -1)

    def _L2_attn_ref(x, W_Q, W_K, W_V, W_O):
        import jax, jax.numpy as jnp
        import numpy as np
        NUM_HEADS = 16
        D_MODEL = 128
        D_K = D_MODEL // NUM_HEADS
        MAX_SEQ_LEN = 512
        ROPE_BASE = 10000.0
        BATCH = 2
        SEQ_LEN = 256

        def _rope_tables(seq_len, d_k, base=ROPE_BASE):
            theta = 1.0 / base ** (jnp.arange(0, d_k, 2, dtype=jnp.float32) / d_k)
            m = jnp.arange(seq_len, dtype=jnp.float32)
            m_theta = jnp.outer(m, theta)
            ang = jnp.concatenate([m_theta, m_theta], axis=-1)
            return (jnp.cos(ang), jnp.sin(ang))

        def _apply_rope(x, cos, sin):
            d2 = x.shape[-1] // 2
            x1, x2 = (x[..., :d2], x[..., d2:])
            x_flip = jnp.concatenate([-x2, x1], axis=-1)
            return x * cos + x_flip * sin
        B, S, _ = x.shape

        def proj(W):
            y = jnp.einsum('bsd,ed->bse', x, W)
            return y.reshape(B, S, NUM_HEADS, D_K).transpose(0, 2, 1, 3)
        Q, K, V = (proj(W_Q), proj(W_K), proj(W_V))
        cos, sin = _rope_tables(S, D_K)
        Q = _apply_rope(Q, cos, sin)
        K = _apply_rope(K, cos, sin)
        scores = jnp.einsum('bhsd,bhtd->bhst', Q, K) / jnp.sqrt(jnp.float32(D_K))
        causal = jnp.tril(jnp.ones((S, S), dtype=bool))
        scores = jnp.where(causal[None, None], scores, -jnp.inf)
        attn = jax.nn.softmax(scores, axis=-1)
        out = jnp.einsum('bhst,bhtd->bhsd', attn, V)
        out = out.transpose(0, 2, 1, 3).reshape(B, S, D_MODEL)
        return jnp.einsum('bsd,ed->bse', out, W_O)

    def _L2_xattn_ref(x, context, mask, Wq, Wkv, Wo, bo):
        import jax, jax.numpy as jnp
        import numpy as np
        B, N, M = (4, 128, 512)
        DQ, DC = (128, 128)
        H, DH = (16, 64)
        INNER = H * DH
        SCALE = DH ** (-0.5)
        q = x @ Wq
        kv = context @ Wkv
        k, v = jnp.split(kv, 2, axis=-1)

        def heads(t):
            b, s, _ = t.shape
            return t.reshape(b, s, H, DH).transpose(0, 2, 1, 3)
        q, k, v = (heads(q), heads(k), heads(v))
        sim = jnp.einsum('bhid,bhjd->bhij', q, k) * SCALE
        max_neg = -jnp.finfo(sim.dtype).max
        sim = jnp.where(mask[:, None, None, :], sim, max_neg)
        sim = jnp.clip(sim, -5.0, 5.0)
        attn = jax.nn.softmax(sim, axis=-1)
        out = jnp.einsum('bhij,bhjd->bhid', attn, v)
        out = out.transpose(0, 2, 1, 3).reshape(x.shape[0], x.shape[1], INNER)
        return out @ Wo + bo

    def _L2_ffn_ref(x, w_gate, w_up, w_down):
        import jax, jax.numpy as jnp
        import numpy as np
        BLOCK = 32
        W_BITS = 4
        ACT_BITS = 16

        def act_qdq(x):
            qmax = 2.0 ** (ACT_BITS - 1) - 1.0
            scale = jnp.maximum(jnp.max(jnp.abs(x)) / qmax, 1e-12)
            return jnp.clip(jnp.round(x / scale), -qmax - 1.0, qmax) * scale

        def fixed_qdq_u16(x):
            scale = 1.0 / 65536.0
            return jnp.clip(jnp.round(x / scale), 0.0, 65535.0) * scale

        def lpbq_dequant(w):
            O, I = w.shape
            qmax = 2.0 ** (W_BITS - 1) - 1.0
            wb = w.reshape(O, I // BLOCK, BLOCK)
            s = jnp.maximum(jnp.max(jnp.abs(wb), axis=-1, keepdims=True) / qmax, 1e-12)
            wq = jnp.clip(jnp.round(wb / s), -qmax - 1.0, qmax) * s
            return wq.reshape(O, I)
        x = act_qdq(x)
        up = act_qdq(x @ lpbq_dequant(w_up).T)
        gate = act_qdq(x @ lpbq_dequant(w_gate).T)
        sig = fixed_qdq_u16(jax.nn.sigmoid(gate))
        gate = act_qdq(gate * sig)
        o = act_qdq(gate * up)
        return o @ lpbq_dequant(w_down).T

    def _L3_attn_ref(x, Wq, Wk, Wv, Wo):
        import jax, jax.numpy as jnp
        import numpy as np
        D_MODEL = 128
        NUM_HEADS = 16
        HEAD_DIM = D_MODEL // NUM_HEADS
        THETA = 10000.0
        B, S = (2, 256)

        def _apply_rope(t, cos, sin):
            te = t[..., 0::2]
            to = t[..., 1::2]
            re = te * cos - to * sin
            ro = te * sin + to * cos
            out = jnp.stack([re, ro], axis=-1)
            return out.reshape(t.shape)
        Bv, Sv, _ = x.shape

        def proj(W):
            return jnp.einsum('bsd,ed->bse', x, W).reshape(Bv, Sv, NUM_HEADS, HEAD_DIM).transpose(0, 2, 1, 3)
        q, k, v = (proj(Wq), proj(Wk), proj(Wv))
        pos = jnp.arange(Sv, dtype=jnp.float32)
        inv_freq = THETA ** (-jnp.arange(0, HEAD_DIM, 2, dtype=jnp.float32) / HEAD_DIM)
        ang = pos[:, None] * inv_freq[None, :]
        cos, sin = (jnp.cos(ang), jnp.sin(ang))
        q = _apply_rope(q, cos, sin)
        k = _apply_rope(k, cos, sin)
        scale = 1.0 / jnp.sqrt(jnp.float32(HEAD_DIM))
        scores = jnp.einsum('bhqd,bhkd->bhqk', q.astype(jnp.float32), k.astype(jnp.float32)) * scale
        causal = jnp.tril(jnp.ones((Sv, Sv), dtype=bool))
        scores = jnp.where(causal[None, None], scores, -jnp.inf)
        attn = jax.nn.softmax(scores, axis=-1)
        out = jnp.einsum('bhqk,bhkd->bhqd', attn, v.astype(jnp.float32))
        out = out.transpose(0, 2, 1, 3).reshape(Bv, Sv, D_MODEL)
        return jnp.einsum('bsd,ed->bse', out, Wo)

    def _L3_xattn_ref(x, latents, mask, g1, b1, g2, b2, Wq, Wkv, Wout):
        import jax, jax.numpy as jnp
        import numpy as np
        EPS = 1e-05

        def layer_norm(x, g, b):
            mu = jnp.mean(x, axis=-1, keepdims=True)
            var = jnp.mean((x - mu) ** 2, axis=-1, keepdims=True)
            return (x - mu) * jax.lax.rsqrt(var + EPS) * g + b
        heads, dim_head = (16, 64)
        b, n, D = x.shape
        l = latents.shape[1]
        xn = layer_norm(x, g1, b1)
        ln_lat = layer_norm(latents, g2, b2)
        q = ln_lat @ Wq
        kv = jnp.concatenate([xn, ln_lat], axis=1) @ Wkv
        k, v = jnp.split(kv, 2, axis=-1)

        def to_heads(t):
            return t.reshape(t.shape[0], t.shape[1], heads, dim_head).transpose(0, 2, 1, 3)
        q, k, v = (to_heads(q), to_heads(k), to_heads(v))
        scale = 1.0 / np.sqrt(np.sqrt(dim_head)).astype(np.float32)
        weight = jnp.einsum('bhld,bhnd->bhln', q * scale, k * scale)
        full_mask = jnp.concatenate([mask, jnp.ones((b, l), dtype=bool)], axis=1)
        neg = -jnp.finfo(weight.dtype).max
        weight = jnp.where(full_mask[:, None, None, :], weight, neg)
        weight = jax.nn.softmax(weight.astype(jnp.float32), axis=-1).astype(q.dtype)
        out = jnp.einsum('bhln,bhnd->bhld', weight, v)
        out = out.transpose(0, 2, 1, 3).reshape(b, l, heads * dim_head)
        return out @ Wout

    def _L3_ffn_ref(x, ln_gamma, ln_beta, fc1_q, fc1_scales, fc1_bias, fc2_q, fc2_scales, fc2_bias):
        import jax, jax.numpy as jnp
        import numpy as np
        B, S, H, F, G = (8, 256, 128, 512, 128)
        EPS = 1e-05

        def _dequant(q, scales, g):
            K, N = q.shape
            w = (q.astype(jnp.float32) - 128.0).reshape(K // g, g, N) * scales[:, None, :]
            return w.reshape(K, N)
        residual = x
        mu = jnp.mean(x, axis=-1, keepdims=True)
        var = jnp.mean(jnp.square(x - mu), axis=-1, keepdims=True)
        h = (x - mu) * jax.lax.rsqrt(var + EPS) * ln_gamma + ln_beta
        hf = h.reshape(-1, H)
        w1 = _dequant(fc1_q, fc1_scales, G)
        y = hf @ w1 + fc1_bias
        y = jax.nn.silu(y)
        w2 = _dequant(fc2_q, fc2_scales, G)
        z = y @ w2 + fc2_bias
        return residual + 0.5 * z.reshape(residual.shape)
    x = _layernorm(x + _L0_attn_ref(x, L0_attn_Wq, L0_attn_bq, L0_attn_Wkv, L0_attn_bkv, L0_attn_Wo), axis=-1)
    x = _layernorm(x + _L0_xattn_ref(x, ctx_1024, ctx_1024, L0_xattn_Wq, L0_xattn_bq, L0_xattn_Wk, L0_xattn_bk, L0_xattn_Wv, L0_xattn_bv, L0_xattn_Wo, L0_xattn_bo), axis=-1)
    x = _layernorm(x + _L0_ffn_ref(x, L0_ffn_router_w, L0_ffn_gate_w, L0_ffn_gate_b, L0_ffn_up_w, L0_ffn_up_b, L0_ffn_down_w, L0_ffn_down_b), axis=-1)
    x = _layernorm(x + _L1_attn_ref(x, L1_attn_qkv_w, L1_attn_qkv_b, L1_attn_proj_w, L1_attn_proj_b, L1_attn_rel_bias), axis=-1)
    x = _layernorm(x + _L1_xattn_ref(x, ctx_1024, L1_xattn_Wq, L1_xattn_bq, L1_xattn_Wk, L1_xattn_bk, L1_xattn_Wv, L1_xattn_bv, L1_xattn_Wo, L1_xattn_bo), axis=-1)
    x = _layernorm(x + _L1_ffn_ref(x, L1_ffn_We, L1_ffn_be, L1_ffn_Wg, L1_ffn_bg), axis=-1)
    x = _layernorm(x + _L2_attn_ref(x, L2_attn_W_Q, L2_attn_W_K, L2_attn_W_V, L2_attn_W_O), axis=-1)
    x = _layernorm(x + _L2_xattn_ref(x, ctx_1024, mask_BxS2_bk1, L2_xattn_Wq, L2_xattn_Wkv, L2_xattn_Wo, L2_xattn_bo), axis=-1)
    x = _layernorm(x + _L2_ffn_ref(x, L2_ffn_w_gate, L2_ffn_w_up, L2_ffn_w_down), axis=-1)
    x = _layernorm(x + _L3_attn_ref(x, L3_attn_Wq, L3_attn_Wk, L3_attn_Wv, L3_attn_Wo), axis=-1)
    x = _layernorm(x + _L3_xattn_ref(ctx_1024, x, mask_BxS2_bk0, L3_xattn_g1, L3_xattn_b1, L3_xattn_g2, L3_xattn_b2, L3_xattn_Wq, L3_xattn_Wkv, L3_xattn_Wout), axis=-1)
    x = _layernorm(x + _L3_ffn_ref(x, L3_ffn_ln_gamma, L3_ffn_ln_beta, L3_ffn_fc1_q, L3_ffn_fc1_scales, L3_ffn_fc1_bias, L3_ffn_fc2_q, L3_ffn_fc2_scales, L3_ffn_fc2_bias), axis=-1)
    return x

_drawn_inputs = setup_inputs


def setup_inputs(seed=0):
    import zlib

    import numpy as np

    out = dict(_drawn_inputs(seed))
    spreads = {'L0_xattn_bq': (0.0, 2.0),
     'L0_xattn_bk': (0.0, 2.0),
     'L0_xattn_bv': (0.0, 0.1),
     'L0_xattn_bo': (0.0, 0.1),
     'L0_ffn_gate_b': (0.0, 0.1),
     'L0_ffn_up_b': (0.0, 0.1),
     'L0_ffn_down_b': (0.0, 0.1),
     'L1_attn_qkv_b': (0.0, 0.1),
     'L1_attn_proj_b': (0.0, 0.1),
     'L1_xattn_bq': (0.0, 0.1),
     'L1_xattn_bk': (0.0, 2.0),
     'L1_xattn_bv': (0.0, 0.1),
     'L1_xattn_bo': (0.0, 0.1),
     'L2_xattn_bo': (0.0, 0.1),
     'L3_xattn_g1': (1.0, 0.2),
     'L3_xattn_b1': (0.0, 0.1),
     'L3_xattn_g2': (1.0, 0.2),
     'L3_xattn_b2': (0.0, 0.1),
     'L3_ffn_ln_gamma': (1.0, 0.2),
     'L3_ffn_ln_beta': (0.0, 0.1)}
    factors = {'L3_ffn_fc1_bias': 8.0, 'L3_ffn_fc2_bias': 45.85, 'L0_xattn_Wq': 4.734}
    for name, (base, spread) in spreads.items():
        noise = np.random.default_rng([zlib.crc32(name.encode()), seed]).standard_normal(out[name].shape)
        drawn = base * np.exp(spread * noise) if base else spread * noise
        out[name] = jnp.asarray(drawn.astype(out[name].dtype))
    for name, factor in factors.items():
        out[name] = (out[name] * factor).astype(out[name].dtype)
    return out
```

```python
from contextlib import ExitStack

import numpy as np

import concourse.bass as bass
from concourse import mybir

F32 = mybir.dt.float32
BF16 = mybir.dt.bfloat16
I32 = mybir.dt.int32
U8 = mybir.dt.uint8
ALU = mybir.AluOpType
ACT = mybir.ActivationFunctionType
AX = mybir.AxisListType

B, S, D = 16, 128, 128
G = 4
NIT = B // G
P = 128
EPS = 1e-5
NEG = -1e30
MAGIC = 1.5 * 2.0 ** 23
NE = 8
WINDOW = 64

EARLY = {
    "mqa": [("q0", 3, "dve"), ("q1", 3, "dve"), ("kv", 3, "dve")],
    "h8": [("qk", 3, "act"), ("v", 3, "dve")],
    "h8r": [("qk", 3, "dve"), ("v", 3, "dve")],
    "moe": [("router", 3, "dve")],
    "lin": [("router", 3, "dve")],
    "h64c": [("q0", 5, "act"), ("q1", 5, "act"), ("k0", 4, "dve"), ("k1", 4, "dve"), ("v0", 3, "act"), ("v1", 3, "dve")],
    "h64m": [("q0", 7, "act"), ("q1", 7, "act"), ("k0", 6, "dve"), ("k1", 6, "dve"), ("k2", 5, "dve"), ("k3", 5, "dve"),
             ("v0", 4, "act"), ("v1", 4, "dve"), ("v2", 3, "act"), ("v3", 3, "dve")],
    "ffn": [],
}
UNITS = {"mqa": 2, "h8": 4, "h8r": 4, "moe": 8, "lin": 2, "h64c": 4, "h64m": 8, "ffn": 2}
SOFTMAX = ("mqa", "h8", "h8r", "h64m", "h64c")
STAGES = {
    "scores": tuple(UNITS),
    "negmax": ("mqa", "h8", "h8r", "h64m"),
    "clip": ("h64c",),
    "exp": SOFTMAX,
    "norm": SOFTMAX,
    "silu": ("moe", "ffn"),
    "gate": ("moe",),
    "second": SOFTMAX + ("moe", "ffn"),
    "pt_act": ("h64m",),
    "pt_dve": ("mqa", "h8", "h8r", "h64c"),
    "acc": ("moe", "lin", "ffn"),
    "values": SOFTMAX,
}


class Layer:
    def __init__(self, name, kind, mask=None, ctx=False, bias=False, out_bias=False):
        self.name, self.kind, self.mask, self.ctx, self.bias, self.out_bias = name, kind, mask, ctx, bias, out_bias


LOOP_A = [
    Layer("L0_attn", "mqa", mask="causal"),
    Layer("L0_xattn", "h8", mask="causal", ctx=True, bias=True, out_bias=True),
    Layer("L0_ffn", "moe"),
    Layer("L1_attn", "h8", mask="relpos", bias=True, out_bias=True),
    Layer("L1_xattn", "h8", ctx=True, bias=True, out_bias=True),
    Layer("L1_ffn", "lin"),
    Layer("L2_attn", "h8r", mask="causal"),
    Layer("L2_xattn", "h64c", ctx=True, out_bias=True),
]
LOOP_C = [
    Layer("L3_attn", "h8r", mask="causal"),
    Layer("L3_xattn", "h64m", mask="keys"),
    Layer("L3_ffn", "ffn"),
]


class Plan:

    def __init__(self, layers):
        self.layers = layers
        self.steps = [(L, b) for L in range(len(layers)) for b in range(G)]
        self.units, self.first, self.last = [], [], []
        for s, (L, b) in enumerate(self.steps):
            self.first.append(len(self.units))
            self.units += [(s, i) for i in range(UNITS[layers[L].kind])]
            self.last.append(len(self.units) - 1)
        self.n = len(self.units)
        self.early, self.after = {}, {}
        for s in range(len(self.steps)):
            for name, ahead, eng in EARLY[self.kind(s)]:
                self.early.setdefault(max(self.first[s] - ahead, -3), []).append((s, name, eng))
            for part in range(3):
                self.after.setdefault(self.last[s] + 2 + part, []).append((part, s))
        self.uses = []
        for n in self.slots():
            self.uses += self.early.get(n, [])
            for part, s in self.after.get(n, []):
                if part == 0 and self.kind(s) in SOFTMAX:
                    self.uses.append((s, "y", "dve"))
                if part == self.turn_part(s):
                    self.uses.append((s, "xT", "act"))
        self.at = {(s, name): u for u, (s, name, _) in enumerate(self.uses)}

    def slots(self):
        return range(-3, self.n + 5)

    def layer(self, s):
        return self.layers[self.steps[s][0]]

    def kind(self, s):
        return self.layer(s).kind

    def next_kind(self, s):
        L = self.steps[s][0] + 1
        return self.layers[L].kind if L < len(self.layers) else None

    def affine_next(self, s):
        return self.next_kind(s) in ("h64m", "ffn")

    def turn_part(self, s):
        return None if self.next_kind(s) is None else 2 if self.affine_next(s) else 1

    def unit(self, n):
        s, i = self.units[n]
        return s, i, self.kind(s), self.steps[s][1]

    def count(self, stage, n):
        return sum(self.kind(s) in STAGES[stage] for s, _ in self.units[:n + 1])

    def used_by(self, eng, u):
        return sum(e == eng for _, _, e in self.uses[:u + 1])


def heads_view(ap, n):
    return ap.rearrange("p (n k) -> p n k", n=n)


def over(ap, n):
    return ap.unsqueeze(1).to_broadcast([ap.shape[0], n, ap.shape[1]])


def along(ap, n):
    return ap.unsqueeze(2).to_broadcast([ap.shape[0], ap.shape[1], n])


def quantised_ffn(nc, sb, sem, scope, w, w_in, dram, cols, state, state_t, ident, neg_half, banks, q_in, fc1_q, fc2_q):
    NT, FC = B * S, 3
    QMAX = 32767.0
    wq = sb("wq", [P, 9, D], scope=scope)
    wr = sb("wr", [P, 9, D], scope=scope)
    wt = sb("wt", [P, 9, D], scope=scope)
    bmax = sb("bmax", [P, 36], scope=scope)
    bscale = sb("bscale", [P, 36], scope=scope)
    binv = sb("binv", [P, 36], scope=scope)
    xq = sb("xq", [P, B, D], scope=scope)
    xqt = sb("xqt", [P, NT], scope=scope)
    hid = sb("hid", [P, 2 * FC, NT], scope=scope)
    sig = sb("sig", [P, FC, NT], scope=scope)
    cmax = sb("cmax", [P, 5, 12], scope=scope)
    pmax = sb("pmax", [P, 5], scope=scope)
    gmax = sb("gmax", [P, 5], scope=scope)
    scl = sb("scl", [P, 5], scope=scope)
    inv = sb("inv", [P, 5], scope=scope)
    R = sb("b_r", [P, B, D], scope=scope)
    st6 = sb("b_st6", [P, B, 6], scope=scope)
    mv = sb("b_mv", [P, B, 2], scope=scope)
    ve = sb("b_ve", [P, B], scope=scope)
    rstd = sb("b_rstd", [P, B], scope=scope)
    X_, GATE, UP, GATED, PROD = range(5)

    chain_dve, wq_ready, max_part, max_all, scale_ready, xq_ready = (sem("b_" + n) for n in ("chain", "wq_ready", "max_part", "max_all", "scale_ready", "xq_ready"))
    bank_full, bank_taken, down_taken, gate_ready, sig_ready, up_ready, up_chain, prod_ready, var_ready, rstd_ready, x_ready, neg_ready = (
        sem("b_" + n) for n in ("bank_full", "bank_taken", "down_taken", "gate_ready", "sig_ready", "up_ready", "up_chain", "prod_ready", "var_ready",
                                "rstd_ready", "x_ready", "neg_ready"))
    N_W, N_X, N_H = 3, 4, 24

    with nc.Block() as block:
        @block.sync
        def _(sp):
            sp.dma_start(wq[:, :, :].rearrange("p c d -> p (c d)"), dram["L2_ffn"]).then_inc(w_in["L2_ffn"], 16)
            for layer in LOOP_C:
                sp.dma_start(w[layer.name][:, :], dram[layer.name]).then_inc(w_in[layer.name], 16)
            sp.dma_start(fc1_q[:, :], dram["fc1_q"]).then_inc(q_in, 16)
            sp.dma_start(fc2_q[:, :], dram["fc2_q"]).then_inc(q_in, 16)

        @block.vector
        def _(dve):
            done = [0]

            def link(op):
                done[0] += 1
                op.then_inc(chain_dve, 1)
                dve.wait_ge(chain_dve, done[0])

            def scale(k):
                dve.wait_ge(max_all, k + 1)
                link(dve.tensor_scalar(scl[:, k:k + 1], gmax[:, k:k + 1], 1.0 / QMAX, 1e-12, ALU.mult, ALU.max))
                op = dve.reciprocal(inv[:, k:k + 1], scl[:, k:k + 1])
                op.then_inc(scale_ready, 1)
                dve.wait_ge(scale_ready, k + 1)

            def quantise(to, of, k):
                link(dve.tensor_scalar(to, of, inv[:, k:k + 1], MAGIC, ALU.mult, ALU.add))
                return dve.tensor_scalar(to, to, -MAGIC, scl[:, k:k + 1], ALU.add, ALU.mult)

            def absmax(to, of):
                return dve.tensor_reduce(to, of, axis=AX.X, op=ALU.max, apply_absolute_value=True)

            absmax(pmax[:, X_:X_ + 1], state[:, :, :].rearrange("p b d -> p (b d)")).then_inc(max_part, 1)
            dve.wait_ge(w_in["L2_ffn"], 16)
            blocks = wq[:, :, :].rearrange("p c (n k) -> p (c n) k", k=32)
            rounded = wr[:, :, :].rearrange("p c (n k) -> p (c n) k", k=32)
            link(absmax(bmax[:, :], blocks))
            link(dve.tensor_scalar(bscale[:, :], bmax[:, :], 1.0 / 7.0, 1e-12, ALU.mult, ALU.max))
            link(dve.reciprocal(binv[:, :], bscale[:, :]))
            link(dve.tensor_tensor(rounded, blocks, along(binv[:, :], 32), ALU.mult))
            link(dve.tensor_scalar(rounded, rounded, MAGIC, -MAGIC, ALU.add, ALU.add))
            dve.tensor_tensor(rounded, rounded, along(bscale[:, :], 32), ALU.mult).then_inc(wq_ready, 1)
            scale(X_)
            quantise(xq[:, :, :], state[:, :, :], X_).then_inc(xq_ready, 1)
            for k in range(N_H):
                dve.wait_ge(bank_taken, N_W + N_X + k + 1)
                op = absmax(cmax[:, GATE + k // 12, k % 12:k % 12 + 1], hid[:, k // 4, (k % 4) * 512:(k % 4 + 1) * 512])
                if k % 12 == 11:
                    link(op)
                    g = GATE + k // 12
                    absmax(pmax[:, g:g + 1], cmax[:, g, :]).then_inc(max_part, 1)
            scale(GATE)
            for c in range(FC):
                quantise(hid[:, c, :], hid[:, c, :], GATE).then_inc(gate_ready, 1)
            scale(UP)
            for c in range(FC):
                dve.wait_ge(sig_ready, c + 1)
                link(dve.tensor_scalar(sig[:, c, :], sig[:, c, :], 65536.0, MAGIC, ALU.mult, ALU.add))
                link(dve.tensor_scalar(sig[:, c, :], sig[:, c, :], -MAGIC, 65535.0, ALU.add, ALU.min))
                link(dve.scalar_tensor_tensor(hid[:, c, :], sig[:, c, :], 1.0 / 65536.0, hid[:, c, :], ALU.mult, ALU.mult))
                op = absmax(cmax[:, GATED, c:c + 1], hid[:, c, :])
            link(op)
            absmax(pmax[:, GATED:GATED + 1], cmax[:, GATED, 0:FC]).then_inc(max_part, 1)
            scale(GATED)
            for c in range(FC):
                link(quantise(hid[:, c, :], hid[:, c, :], GATED))
                dve.wait_ge(up_ready, c + 1)
                link(dve.tensor_tensor(hid[:, c, :], hid[:, c, :], hid[:, FC + c, :], ALU.mult))
                op = absmax(cmax[:, PROD, c:c + 1], hid[:, c, :])
            link(op)
            absmax(pmax[:, PROD:PROD + 1], cmax[:, PROD, 0:FC]).then_inc(max_part, 1)
            scale(PROD)
            for c in range(FC):
                quantise(hid[:, c, :], hid[:, c, :], PROD).then_inc(prod_ready, 1)
            for g in range(4):
                u = N_W + N_X + N_H + g
                dve.wait_ge(bank_full, u + 1)
                sl = slice(4 * g, 4 * g + 4)
                dve.tensor_tensor(R[:, sl, :], heads_view(banks[u % 8][:, :], 4), state[:, sl, :], ALU.add).then_inc(down_taken, 1)
                dve.wait_ge(down_taken, g + 1)
                for b in range(4 * g, 4 * g + 4):
                    op = dve.bn_stats(st6[:, b, :], R[:, b, :])
                link(op)
                for b in range(4 * g, 4 * g + 4):
                    op = dve.bn_aggr(mv[:, b, :], st6[:, b, :])
                link(op)
                dve.tensor_scalar(ve[:, sl], mv[:, sl, 1], EPS, None, ALU.add).then_inc(var_ready, 1)
            for g in range(4):
                dve.wait_ge(rstd_ready, g + 1)
                for b in range(4 * g, 4 * g + 4):
                    op = dve.tensor_scalar(state[:, b, :], R[:, b, :], mv[:, b, 0:1], rstd[:, b:b + 1], ALU.subtract, ALU.mult)
                op.then_inc(x_ready, 1)

        @block.gpsimd
        def _(pool):
            for k in range(3):
                pool.wait_ge(max_part, k + 1)
                pool.partition_all_reduce(gmax[:, k:k + 1], pmax[:, k:k + 1], P, bass.bass_isa.ReduceOp.max).then_inc(max_all, 1)
            pool.wait_ge(scale_ready, UP + 1)
            for c in range(FC):
                up = hid[:, FC + c, :]
                pool.tensor_scalar(up, up, inv[:, UP:UP + 1], MAGIC, ALU.mult, ALU.add).then_inc(up_chain, 1)
                pool.wait_ge(up_chain, c + 1)
                pool.tensor_scalar(up, up, -MAGIC, scl[:, UP:UP + 1], ALU.add, ALU.mult).then_inc(up_ready, 1)
            for k in range(3, 5):
                pool.wait_ge(max_part, k + 1)
                pool.partition_all_reduce(gmax[:, k:k + 1], pmax[:, k:k + 1], P, bass.bass_isa.ReduceOp.max).then_inc(max_all, 1)
            for g in range(4):
                pool.wait_ge(var_ready, g + 1)
                pool.tensor_tensor(rstd[:, 4 * g:4 * g + 4], ve[:, 4 * g:4 * g + 4], neg_half[:, :], ALU.pow).then_inc(rstd_ready, 1)

        @block.tensor
        def _(pe):
            pe.wait_ge(wq_ready, 1)
            for u in range(N_W):
                for j in range(3):
                    mm = pe.transpose(banks[u][:, j * P:(j + 1) * P], wr[:, 3 * u + j, :], ident)
                mm.then_inc(bank_full, 1)
            pe.wait_ge(xq_ready, 1)
            for t in range(N_X):
                for j in range(4):
                    mm = pe.transpose(banks[N_W + t][:, j * P:(j + 1) * P], xq[:, 4 * t + j, :], ident)
                mm.then_inc(bank_full, 1)
            pe.wait_ge(bank_taken, N_W + N_X)
            for k in range(N_H):
                u = N_W + N_X + k
                if u >= N_W + N_X + 1:
                    pe.wait_ge(bank_taken, max(u - 7, N_W + N_X))
                pe.matmul(banks[u % 8][:, :], wt[:, k // 4, :], xqt[:, (k % 4) * 512:(k % 4 + 1) * 512], start=True, stop=True).then_inc(bank_full, 1)
            pe.wait_ge(prod_ready, FC)
            pe.wait_ge(bank_taken, N_W + N_X + N_H)
            for g in range(4):
                u = N_W + N_X + N_H + g
                for j in range(4):
                    t = 4 * g + j
                    for c in range(FC):
                        mm = pe.matmul(banks[u % 8][:, j * D:(j + 1) * D], hid[:, c, t * S:(t + 1) * S], wt[:, 6 + c, :], start=c == 0, stop=c == FC - 1)
                mm.then_inc(bank_full, 1)
            for g in range(4):
                u = N_W + N_X + N_H + 4 + g
                pe.wait_ge(x_ready, g + 1)
                for j in range(4):
                    mm = pe.transpose(banks[u % 8][:, j * S:(j + 1) * S], state[:, 4 * g + j, :], ident)
                mm.then_inc(bank_full, 1)

        @block.scalar
        def _(act):
            for u in range(N_W):
                act.wait_ge(bank_full, u + 1)
                act.activation(wt[:, 3 * u:3 * u + 3, :], heads_view(banks[u][:, 0:3 * P], 3), ACT.Copy).then_inc(bank_taken, 1)
            for t in range(N_X):
                act.wait_ge(bank_full, N_W + t + 1)
                act.activation(xqt[:, t * 512:(t + 1) * 512], banks[N_W + t][:, :], ACT.Copy).then_inc(bank_taken, 1)
            for k in range(N_H):
                u = N_W + N_X + k
                act.wait_ge(bank_full, u + 1)
                act.activation(hid[:, k // 4, (k % 4) * 512:(k % 4 + 1) * 512], banks[u % 8][:, :], ACT.Copy).then_inc(bank_taken, 1)
            for c in range(FC):
                act.wait_ge(gate_ready, c + 1)
                act.activation(sig[:, c, :], hid[:, c, :], ACT.Sigmoid).then_inc(sig_ready, 1)
            for g in range(4):
                u = N_W + N_X + N_H + 4 + g
                act.wait_ge(bank_full, u + 1)
                act.activation(state_t[:, 4 * g:4 * g + 4, :], heads_view(banks[u % 8][:, :], 4), ACT.Copy).then_inc(bank_taken, 1)


def decoder_kernel(nc, dram, out, cols):
    ctx = ExitStack()
    with ctx:
        def sb(name, shape, dt=F32, scope=ctx):
            return scope.enter_context(nc.sbuf_tensor(name, shape, dt))

        def sem(name):
            return ctx.enter_context(nc.semaphore(name))

        def part(tensor, pack, name):
            a, n = cols[pack][name]
            return tensor[:, a:a + n]

        w_in = {k: sem(f"w_in_{k}") for k in cols}
        body_names = ["x_in", "xt_in", "ctx_in", "mask_in", "x_out",
                      "proj_ready",
                      "proj_by_act", "proj_by_dve",
                      "masked",
                      "rope_ready",
                      "scores_ready", "negmax_ready", "clip_done", "exp_done", "rsum_ready", "norm_done",
                      "second_ready", "pt_act", "pt_dve", "values_ready", "out_taken",
                      "silu_done", "gate_done", "acc_done", "acc_start",
                      "resid_ready",
                      "logits_ready", "route_exp", "route_ready",
                      "var_ready", "rstd_ready", "x_ready", "stat2_ready", "rstd2_ready", "norm2_ready",
                      "chain_dve", "chain_pool", "keymask_ready",
                      "ctx_stats", "ctx_rstd", "ctx_norm", "state_in_dve", "state_in_act"]
        sems = {n: sem("body_" + n) for n in body_names}
        nums = sorted(x.num for x in sems.values())
        assert nums == list(range(nums[0], nums[-1] + 1))
        body_range = range(nums[0], nums[-1] + 1)

        score_bank = [ctx.enter_context(nc.psum_tensor(f"score_bank{i}", [P, 512], F32)) for i in range(3)]
        second_bank = [ctx.enter_context(nc.psum_tensor(f"second_bank{i}", [P, 512], F32)) for i in range(2)]
        value_bank = ctx.enter_context(nc.psum_tensor("value_bank", [P, 512], F32))
        proj_bank = [ctx.enter_context(nc.psum_tensor(f"proj_bank{i}", [P, 512], F32)) for i in range(2)]

        const = sb("const", [P, sum(n for _, n in cols["const"].values())])
        ident = part(const, "const", "ident")
        head_scale = part(const, "const", "group")
        head_pick = part(const, "const", "pick")
        value_pick = part(const, "const", "vpick").rearrange("p (j d) -> p j d", j=4)
        lower = part(const, "const", "lower").rearrange("p (i j) -> p i j", i=NE)
        ident_b = sb("ident_b", [P, P], BF16)
        causal_b = sb("causal_b", [P, 4, P], BF16)
        neg_half = sb("neg_half", [P, G])
        state = sb("state", [P, B, D])

        def run_loop(tag, plan, w, scope, last_loop, state_t=None):
            X = sb(tag + "x", [P, G, D], scope=scope)
            XT = sb(tag + "xt", [P, G, S], scope=scope)
            XR = sb(tag + "xr", [P, G, D], scope=scope)
            R = sb(tag + "r", [P, G, D], scope=scope)
            st6 = sb(tag + "st6", [P, G, 6], scope=scope)
            mv = sb(tag + "mv", [P, G, 2], scope=scope)
            ve = sb(tag + "ve", [P, G], scope=scope)
            rstd = sb(tag + "rstd", [P, G], scope=scope)
            Pb = sb(tag + "probs", [P, 3, 512], scope=scope)
            PT = sb(tag + "probs_t", [P, 2, 512], scope=scope)
            negmax = sb(tag + "negmax", [P, 4, 4], scope=scope)
            rsum = sb(tag + "rsum", [P, 4, 4], scope=scope)
            rinv = sb(tag + "rinv", [P, 4, 4], scope=scope)
            OT = sb(tag + "ot", [P, 2, 8, S], scope=scope)
            QK = sb(tag + "qk", [P, 2, 2, S], scope=scope)
            RT2 = sb(tag + "rt", [P, 2, 2, S], scope=scope)
            Qg = sb(tag + "qg", [P, 2, 4, S], scope=scope)
            Km = sb(tag + "km", [P, 2, 4, S], scope=scope)
            Vm = sb(tag + "vm", [P, 2, 4, D], scope=scope)
            Qz = sb(tag + "qz", [P, 2, 8, 2, S], scope=scope)
            nkeys = 2 * S if last_loop else S
            K64 = sb(tag + "k64", [P, 2, 8, nkeys], scope=scope)
            V64 = sb(tag + "v64", [P, 2, nkeys // S, 1024], scope=scope)
            H = sb(tag + "h", [P, 3, 2, S], scope=scope)
            HS = sb(tag + "hs", [P, 3, 2, S], scope=scope)
            if last_loop:
                KV = sb(tag + "kv", [P, G, 2, S], scope=scope)
                CX = sb(tag + "cx", [P, G, D], scope=scope)
                LH = sb(tag + "lh", [P, G, D], scope=scope)
                st6b = sb(tag + "st6b", [P, G, 6], scope=scope)
                mv2 = sb(tag + "mv2", [P, G, 2], scope=scope)
                ve2 = sb(tag + "ve2", [P, G], scope=scope)
                rstd2 = sb(tag + "rstd2", [P, G], scope=scope)
                mask_u8 = sb(tag + "mask_u8", [P, G, S], U8, scope=scope)
                key_mask = sb(tag + "key_mask", [P, G, 2, 2, S], BF16, scope=scope)
            else:
                CT = sb(tag + "ct", [P, G, S], scope=scope)
                Q8 = sb(tag + "q8", [P, 3, 8, S], scope=scope)
                K8 = sb(tag + "k8", [P, 3, S], scope=scope)
                V8 = sb(tag + "v8", [P, 3, D], scope=scope)
                mask_u8 = sb(tag + "mask_u8", [P, G, S], U8, scope=scope)
                clip_hi = sb(tag + "clip_hi", [P, G, S], scope=scope)
                lg = sb(tag + "lg", [P, G, NE], scope=scope)
                lmax = sb(tag + "lmax", [P, G], scope=scope)
                lexp = sb(tag + "lexp", [P, G, NE], scope=scope)
                lsum = sb(tag + "lsum", [P, G], scope=scope)
                linv = sb(tag + "linv", [P, G], scope=scope)
                beat = sb(tag + "beat", [P, G, NE, NE], scope=scope)
                tie = sb(tag + "tie", [P, G, NE, NE], scope=scope)
                rank = sb(tag + "rank", [P, G, NE], scope=scope)
                pick = sb(tag + "pick", [P, G, NE], scope=scope)
                wsum = sb(tag + "wsum", [P, G], scope=scope)
                winv = sb(tag + "winv", [P, G], scope=scope)
                gatew = sb(tag + "gatew", [P, G, NE], scope=scope)
                eb = sb(tag + "eb", [P, NE, D], scope=scope)
            with nc.Block() as block:
                @block.gpsimd
                def _(pool):
                    pool.memset(Qz[0:64, :, :, 1, :], 0.0)
                    pool.memset(Qz[64:128, :, :, 0, :], 0.0)
            iters = nc.Fori(0, NIT)
            it = iters.__enter__()

            names = [plan.layers[L].name for L, _ in plan.steps]

            def used(eng, s, name):
                u = plan.at[s, name]
                reader = plan.uses[u][2]
                return sems["proj_by_" + reader], plan.used_by(reader, u)

            def after_reader(eng, s, name):
                eng.wait_ge(*used(eng, s, name))

            def state_t_ready(eng, s):
                if s < G:
                    if last_loop:
                        eng.wait_ge(sems["state_in_act"], 1)
                    else:
                        eng.wait_ge(sems["xt_in"], 16)
                else:
                    after_reader(eng, s - G, "xT")

            def state_ready(eng, s):
                if s < G:
                    if last_loop:
                        eng.wait_ge(sems["state_in_dve"], 1)
                    else:
                        eng.wait_ge(sems["x_in"], 16)
                else:
                    eng.wait_ge(sems["x_ready"], s - G + 1)

            def weights(eng, s):
                eng.wait_ge(w_in[names[s]], 16)

            def W(s, name):
                return part(w[names[s]], names[s], name)

            def out_before(n):
                k = 1 if last_loop else 0
                for m in range(min(n, plan.n)):
                    s, i, kind, _ = plan.unit(m)
                    k += kind in ("mqa", "h64c", "h64m") or (kind in ("h8", "h8r") and i == 3)
                return k

            def values_before(n):
                return plan.count("values", n) + (1 if last_loop else 0)

            with nc.Block() as block:
                @block.sync
                def _(sp):
                    if last_loop:
                        sp.dma_start(CX[:, :, :].rearrange("p a n -> p (a n)"), dram["ctx"][bass.ds(it, 1)].rearrange("a p n -> p (a n)")).then_inc(sems["ctx_in"], 16)
                        sp.dma_start(mask_u8[:, :, :].rearrange("p a n -> p (a n)"), dram["mask_bk0"][bass.ds(it, 1)].rearrange("a n -> (a n)").partition_broadcast(P)).then_inc(sems["mask_in"], 16)
                        for b in range(G):
                            sp.wait_ge(sems["x_ready"], (len(plan.layers) - 1) * G + b + 1)
                            sp.dma_start(out[bass.ds(it * G + b, 1)].rearrange("a p d -> p (a d)"), X[:, b, :]).then_inc(sems["x_out"], 16)
                        sp.wait_ge(sems["x_out"], 16 * G)
                    else:
                        sp.dma_start(XT[:, :, :].rearrange("p a n -> p (a n)"), dram["xT"][bass.ds(it, 1)].rearrange("a p n -> p (a n)")).then_inc(sems["xt_in"], 16)
                        sp.dma_start(X[:, :, :].rearrange("p a n -> p (a n)"), dram["x"][bass.ds(it, 1)].rearrange("a p n -> p (a n)")).then_inc(sems["x_in"], 16)
                        sp.dma_start(CT[:, :, :].rearrange("p a n -> p (a n)"), dram["ctxT"][bass.ds(it, 1)].rearrange("a p n -> p (a n)")).then_inc(sems["ctx_in"], 16)
                        sp.dma_start(mask_u8[:, :, :].rearrange("p a n -> p (a n)"), dram["mask_bk1"][bass.ds(it, 1)].rearrange("a n -> (a n)").partition_broadcast(P)).then_inc(sems["mask_in"], 16)

                @block.tensor
                def _(pe):
                    def open_use(s, name):
                        u = plan.at[s, name]
                        if u >= 2:
                            after_reader(pe, *plan.uses[u - 2][:2])
                        return proj_bank[u % 2]

                    def project(s, name):
                        kind, b = plan.kind(s), plan.steps[s][1]
                        bank = open_use(s, name)
                        if b == 0:
                            weights(pe, s)
                        if kind != "h64m" or name[0] == "q":
                            state_t_ready(pe, s)
                        kv = XT
                        if plan.layer(s).ctx and name != "q0" and name != "q1":
                            pe.wait_ge(sems["ctx_in"], 16)
                            kv = CT
                        xt = XT[:, b, :]
                        if kind == "mqa" and name != "kv":
                            for j in range(4):
                                h = 4 * int(name[1]) + j
                                mm = pe.matmul(bank[:, j * S:(j + 1) * S], W(s, "Wq")[:, h * P:(h + 1) * P], xt, start=True, stop=True)
                        elif kind == "mqa":
                            pe.matmul(bank[:, 0:S], W(s, "Wkv")[:, 0:P], xt, start=True, stop=True)
                            mm = pe.matmul(bank[:, S:2 * S], xt, W(s, "Wkv")[:, P:2 * P], start=True, stop=True)
                        elif name == "qk":
                            pe.matmul(bank[:, 0:S], W(s, "Wq"), xt, start=True, stop=True)
                            mm = pe.matmul(bank[:, S:2 * S], W(s, "Wk"), kv[:, b, :], start=True, stop=True)
                            if kind == "h8r":
                                pe.matmul(bank[:, 2 * S:3 * S], W(s, "Wq_turned"), xt, start=True, stop=True)
                                mm = pe.matmul(bank[:, 3 * S:4 * S], W(s, "Wk_turned"), xt, start=True, stop=True)
                        elif name == "v":
                            mm = pe.matmul(bank[:, 0:D], kv[:, b, :], W(s, "Wv"), start=True, stop=True)
                        elif name == "router":
                            mm = pe.matmul(bank[:, 0:64], xt, W(s, "Wr"), start=True, stop=True)
                        elif kind == "h64c":
                            half = int(name[1])
                            for j in range(4):
                                c = 4 * half + j
                                to = bank[:, j * S:(j + 1) * S]
                                if name[0] == "q":
                                    mm = pe.matmul(to, W(s, "Wq")[:, c * P:(c + 1) * P], xt, start=True, stop=True)
                                if name[0] == "k":
                                    mm = pe.matmul(to, W(s, "Wk")[:, c * P:(c + 1) * P], CT[:, b, :], start=True, stop=True)
                            if name[0] == "v":
                                mm = pe.matmul(bank[:, :], CT[:, b, :], W(s, "Wv")[:, half * 512:(half + 1) * 512], start=True, stop=True)
                        else:
                            after_reader(pe, s - G, "xT")
                            i = int(name[1])
                            if name[0] == "q":
                                for j in range(4):
                                    c = 4 * i + j
                                    mm = pe.matmul(bank[:, j * S:(j + 1) * S], W(s, "Wq")[:, c * P:(c + 1) * P], KV[:, b, 1, :], start=True, stop=True)
                            elif name[0] == "k":
                                for j in range(2):
                                    c = 2 * i + j
                                    mm = pe.matmul(bank[:, j * 256:(j + 1) * 256], W(s, "Wk")[:, c * P:(c + 1) * P],
                                                   KV[:, b, :, :].rearrange("p a k -> p (a k)"), start=True, stop=True)
                            else:
                                mm = pe.matmul(bank[:, :], KV[:, b, i // 2, :], W(s, "Wv")[:, (i % 2) * 512:(i % 2 + 1) * 512], start=True, stop=True)
                        mm.then_inc(sems["proj_ready"], 1)

                    def scores(n):
                        s, i, kind, b = plan.unit(n)
                        bank = score_bank[n % 3]
                        if n >= 3:
                            k3 = plan.unit(n - 3)[2]
                            done = {"moe": ("gate_done", "gate"), "lin": ("acc_done", "acc"), "ffn": ("silu_done", "silu"),
                                    "h64c": ("clip_done", "clip")}.get(k3, ("exp_done", "exp"))
                            pe.wait_ge(sems[done[0]], plan.count(done[1], n - 3))
                        if i == 0:
                            for name, _, _ in EARLY[kind]:
                                after_reader(pe, s, name)
                            if kind in ("h8", "h8r"):
                                pe.wait_ge(sems["masked"], 2 * (1 + sum(plan.kind(t) in ("h8", "h8r") for t in range(s))))
                            if kind == "h64m" and b == 0:
                                pe.wait_ge(sems["keymask_ready"], 1)
                            if kind == "ffn":
                                if b == 0:
                                    weights(pe, s)
                                state_t_ready(pe, s)
                        mask = plan.layer(s).mask
                        if mask == "causal":
                            pe.matmul(bank[:, :], ident_b[:, :], causal_b[:, :, :].rearrange("p a k -> p (a k)"), start=True, stop=False)
                        elif mask == "keys":
                            pe.matmul(bank[:, :], ident_b[:, :], key_mask[:, b, :, :, :].rearrange("p a c k -> p (a c k)"), start=True, stop=False)
                        elif mask == "relpos":
                            pe.matmul(bank[:, :], ident, W(s, "relpos")[:, i * 512:(i + 1) * 512], start=True, stop=False)
                        if kind == "mqa":
                            for j in range(4):
                                mm = pe.matmul(bank[:, j * S:(j + 1) * S], Q8[:, s % 3, 4 * i + j, :], K8[:, s % 3, :], start=False, stop=j == 3)
                        elif kind in ("h8", "h8r"):
                            mm = pe.matmul(bank[:, :], Qg[:, s % 2, i, :], Km[:, s % 2, :, :].rearrange("p j k -> p (j k)"), start=mask is None, stop=True)
                        elif kind == "h64c":
                            for j in range(4):
                                mm = pe.matmul(bank[:, j * S:(j + 1) * S], Qz[:, s % 2, 2 * i + j // 2, j % 2, :], K64[:, s % 2, 2 * i + j // 2, :], start=True, stop=True)
                        elif kind == "h64m":
                            for j in range(2):
                                mm = pe.matmul(bank[:, j * 256:(j + 1) * 256], Qz[:, s % 2, i, j, :], K64[:, s % 2, i, :], start=False, stop=j == 1)
                        elif kind == "moe":
                            for j in range(4):
                                c = (2 * i + j % 2) * P
                                mm = pe.matmul(bank[:, j * S:(j + 1) * S], W(s, "gate_w" if j < 2 else "up_w")[:, c:c + P], XT[:, b, :], start=True, stop=True)
                        elif kind == "lin":
                            mm = pe.matmul(bank[:, :], XT[:, b, :], W(s, "We")[:, i * 512:(i + 1) * 512], start=True, stop=True)
                        elif kind == "ffn":
                            for j in range(2):
                                c = (2 * i + j) * P
                                mm = pe.matmul(bank[:, j * S:(j + 1) * S], fc1[:, c:c + P], XT[:, b, :], start=True, stop=True)
                        mm.then_inc(sems["scores_ready"], 1)

                    def second(n):
                        s, i, kind, b = plan.unit(n)
                        if kind not in STAGES["second"]:
                            return
                        m = plan.count("second", n) - 1
                        bank = second_bank[m % 2]
                        if m >= 2:
                            before = [k for k in range(n) if plan.unit(k)[2] in STAGES["second"]][-2]
                            kb = plan.unit(before)[2]
                            stage = "acc" if kb in ("moe", "ffn") else "pt_act" if kb in STAGES["pt_act"] else "pt_dve"
                            pe.wait_ge(sems["acc_done" if stage == "acc" else stage], plan.count(stage, before))
                        if kind in SOFTMAX:
                            pe.wait_ge(sems["norm_done"], plan.count("norm", n))
                            for j in range(4):
                                mm = pe.transpose(bank[:, j * S:(j + 1) * S], Pb[:, n % 3, j * S:(j + 1) * S], ident)
                        elif kind == "moe":
                            pe.wait_ge(sems["gate_done"], plan.count("gate", n))
                            for j in range(2):
                                c = (2 * i + j) * D
                                mm = pe.matmul(bank[:, 0:D], H[:, n % 3, j, :], W(s, "down_w")[:, c:c + D], start=j == 0, stop=j == 1)
                        else:
                            pe.wait_ge(sems["silu_done"], plan.count("silu", n))
                            for j in range(2):
                                mm = pe.matmul(bank[:, 0:D], H[:, n % 3, j, :], fc2[:, 2 * i + j, :], start=j == 0, stop=j == 1)
                        mm.then_inc(sems["second_ready"], 1)

                    def values(n):
                        s, i, kind, b = plan.unit(n)
                        if kind not in SOFTMAX:
                            return
                        stage = "pt_act" if kind in STAGES["pt_act"] else "pt_dve"
                        pe.wait_ge(sems[stage], plan.count(stage, n))
                        outs = out_before(n)
                        if outs:
                            pe.wait_ge(sems["out_taken"], outs)
                        pt = PT[:, n % 2, :]
                        if kind == "mqa":
                            mm = pe.matmul(value_bank[:, :], V8[:, s % 3, :], pt, start=True, stop=True)
                        elif kind in ("h8", "h8r"):
                            for j in range(4):
                                mm = pe.matmul(value_bank[32 * i:32 * i + 32, 0:S], Vm[:, s % 2, j, 32 * i:32 * i + 32], pt[:, j * S:(j + 1) * S], start=j == 0, stop=j == 3)
                        elif kind == "h64c":
                            for j in range(4):
                                h = 4 * i + j
                                mm = pe.matmul(value_bank[64 * (j % 2):64 * (j % 2) + 64, (j // 2) * S:(j // 2 + 1) * S],
                                               V64[:, s % 2, 0, h * 64:(h + 1) * 64], pt[:, j * S:(j + 1) * S], start=True, stop=True)
                        else:
                            for c in range(2):
                                for j in range(2):
                                    h = 2 * i + j
                                    mm = pe.matmul(value_bank[64 * j:64 * j + 64, 0:S], V64[:, s % 2, c, h * 64:(h + 1) * 64],
                                                   pt[:, (2 * j + c) * S:(2 * j + c + 1) * S], start=c == 0, stop=c == 1)
                        mm.then_inc(sems["values_ready"], 1)

                    def output(s):
                        bank = open_use(s, "y")
                        pe.wait_ge(sems["out_taken"], out_before(plan.last[s] + 1))
                        chunks = 1 if plan.kind(s) in ("h8", "h8r") else 8
                        for c in range(chunks):
                            mm = pe.matmul(bank[:, 0:D], OT[:, s % 2, c, :], W(s, "Wo")[:, c * D:(c + 1) * D], start=c == 0, stop=c == chunks - 1)
                        mm.then_inc(sems["proj_ready"], 1)

                    def turn(s):
                        b = plan.steps[s][1]
                        bank = open_use(s, "xT")
                        if plan.affine_next(s):
                            pe.wait_ge(sems["norm2_ready"], 1 + sum(plan.affine_next(t) for t in range(s)))
                            mm = pe.transpose(bank[:, 0:S], LH[:, b, :], ident)
                        else:
                            pe.wait_ge(sems["x_ready"], s + 1)
                            mm = pe.transpose(bank[:, 0:S], X[:, b, :], ident)
                        mm.then_inc(sems["proj_ready"], 1)

                    if last_loop:
                        pe.wait_ge(sems["ctx_norm"], 1)
                        for b in range(G):
                            mm = pe.transpose(value_bank[:, b * S:(b + 1) * S], CX[:, b, :], ident)
                        mm.then_inc(sems["values_ready"], 1)
                    for n in plan.slots():
                        for s, name, _ in plan.early.get(n, []):
                            project(s, name)
                        if 0 <= n + 2 < plan.n:
                            scores(n + 2)
                        if 0 <= n < plan.n:
                            second(n)
                        if 0 <= n - 1 < plan.n:
                            values(n - 1)
                        for p, s in plan.after.get(n, []):
                            if p == 0 and plan.kind(s) in SOFTMAX:
                                output(s)
                            if p == plan.turn_part(s):
                                turn(s)

                @block.scalar
                def _(act):
                    def take(s, name):
                        kind, b = plan.kind(s), plan.steps[s][1]
                        u = plan.at[s, name]
                        bank = proj_bank[u % 2]
                        act.wait_ge(sems["proj_ready"], u + 1)
                        if name == "qk":
                            if b == 0:
                                weights(act, s)
                            act.activation(QK[:, s % 2, 0, :], bank[:, 0:S], ACT.Identity, bias=W(s, "bq"))
                            op = act.activation(QK[:, s % 2, 1, :], bank[:, S:2 * S], ACT.Identity, bias=W(s, "bk"))
                        elif name[0] == "q":
                            half = int(name[1])
                            for j in range(2):
                                op = act.activation(Qz[64 * j:64 * j + 64, s % 2, 4 * half:4 * half + 4, j, :],
                                                    heads_view(bank[64 * j:64 * j + 64, :], 4), ACT.Copy, scale=0.125)
                        elif name[0] == "v":
                            i = int(name[1])
                            op = act.activation(V64[:, s % 2, i // 2, (i % 2) * 512:(i % 2 + 1) * 512], bank[:, :], ACT.Copy)
                        else:
                            to = plan.next_kind(s)
                            if to == "h64m":
                                if b == 0:
                                    act.wait_ge(w_in["L3_xattn"], 16)
                                g, e = (part(w["L3_xattn"], "L3_xattn", k) for k in ("g2", "b2"))
                                op = act.activation(KV[:, b, 1, :], bank[:, 0:S], ACT.Identity, scale=g, bias=e)
                            elif to == "ffn":
                                if b == 0:
                                    act.wait_ge(w_in["L3_ffn"], 16)
                                g, e = (part(w["L3_ffn"], "L3_ffn", k) for k in ("gamma", "beta"))
                                op = act.activation(XT[:, b, :], bank[:, 0:S], ACT.Identity, scale=g, bias=e)
                            else:
                                op = act.activation(XT[:, b, :], bank[:, 0:S], ACT.Copy)
                        op.then_inc(sems["proj_by_act"], 1)

                    def front(n):
                        s, i, kind, b = plan.unit(n)
                        if kind in SOFTMAX:
                            heads, width = (2, 256) if kind == "h64m" else (4, S)
                            if kind == "h64c":
                                act.wait_ge(sems["clip_done"], plan.count("clip", n))
                            else:
                                act.wait_ge(sems["negmax_ready"], plan.count("negmax", n))
                            for j in range(heads):
                                p = Pb[:, n % 3, j * width:(j + 1) * width]
                                if kind == "h64c":
                                    op = act.activation(p, p, ACT.Exp, accum_out=rsum[:, n % 4, j:j + 1])
                                else:
                                    op = act.activation(p, score_bank[n % 3][:, j * width:(j + 1) * width], ACT.Exp,
                                                        bias=negmax[:, n % 4, j:j + 1], accum_out=rsum[:, n % 4, j:j + 1])
                            op.then_inc(sems["exp_done"], 1)
                        elif kind == "moe":
                            if i == 0 and b == 0:
                                weights(act, s)
                            act.wait_ge(sems["scores_ready"], n + 1)
                            for j in range(2):
                                op = act.activation(HS[:, n % 3, j, :], score_bank[n % 3][:, j * S:(j + 1) * S], ACT.Silu,
                                                    bias=W(s, "gate_b")[:, 2 * i + j:2 * i + j + 1])
                            op.then_inc(sems["silu_done"], 1)
                        elif kind == "ffn":
                            act.wait_ge(sems["scores_ready"], n + 1)
                            for j in range(2):
                                op = act.activation(H[:, n % 3, j, :], score_bank[n % 3][:, j * S:(j + 1) * S], ACT.Silu,
                                                    bias=W(s, "fc1_b")[:, 2 * i + j:2 * i + j + 1])
                            op.then_inc(sems["silu_done"], 1)

                    def turned(n):
                        kind = plan.unit(n)[2]
                        if kind in STAGES["pt_act"]:
                            act.wait_ge(sems["second_ready"], plan.count("second", n))
                            m = plan.count("second", n) - 1
                            act.activation(PT[:, n % 2, :], second_bank[m % 2][:, :], ACT.Copy).then_inc(sems["pt_act"], 1)

                    def outs(n):
                        s, i, kind, b = plan.unit(n)
                        if kind in ("h8", "h8r") and i < 3 or kind not in SOFTMAX:
                            return
                        act.wait_ge(sems["values_ready"], values_before(n))
                        if kind == "mqa":
                            if i == 0 and b == 0:
                                weights(act, s)
                            op = act.activation(OT[:, s % 2, 4 * i:4 * i + 4, :], heads_view(value_bank[:, :], 4), ACT.Identity, bias=W(s, "bkv")[:, 1:2])
                        elif kind == "h8" and plan.layer(s).bias:
                            op = act.activation(OT[:, s % 2, 0, :], value_bank[:, 0:S], ACT.Identity, bias=W(s, "bv"))
                        elif kind == "h8r":
                            op = act.activation(OT[:, s % 2, 0, :], value_bank[:, 0:S], ACT.Copy)
                        elif kind == "h64c":
                            op = act.activation(OT[:, s % 2, 2 * i:2 * i + 2, :], heads_view(value_bank[:, 0:2 * S], 2), ACT.Copy)
                        else:
                            op = act.activation(OT[:, s % 2, i, :], value_bank[:, 0:S], ACT.Copy)
                        op.then_inc(sems["out_taken"], 1)

                    def route(s):
                        b = plan.steps[s][1]
                        k = 1 + sum(plan.kind(t) in ("moe", "lin") for t in range(s))
                        act.wait_ge(sems["logits_ready"], k)
                        act.activation(lexp[:, b, :], lg[:, b, :], ACT.Exp, bias=lmax[:, b:b + 1], accum_out=lsum[:, b:b + 1]).then_inc(sems["route_exp"], 1)

                    if last_loop:
                        act.activation(XT[:, :, :], state_t[:, bass.ds(it * G, G), :], ACT.Copy).then_inc(sems["state_in_act"], 1)
                        act.wait_ge(sems["values_ready"], 1)
                        act.wait_ge(w_in["L3_xattn"], 16)
                        act.activation(KV[:, :, 0, :], heads_view(value_bank[:, :], G), ACT.Identity,
                                       scale=part(w["L3_xattn"], "L3_xattn", "g1"), bias=part(w["L3_xattn"], "L3_xattn", "b1")).then_inc(sems["out_taken"], 1)
                    for n in plan.slots():
                        for s, name, eng in plan.early.get(n, []):
                            if eng == "act":
                                take(s, name)
                            if name == "router":
                                route(s)
                        if 0 <= n + 2 < plan.n:
                            front(n + 2)
                        if 0 <= n < plan.n:
                            turned(n)
                        if 0 <= n - 1 < plan.n:
                            outs(n - 1)
                        for p, s in plan.after.get(n, []):
                            if p == plan.turn_part(s):
                                take(s, "xT")

                @block.vector
                def _(dve):
                    chain = [0]

                    def link(op):
                        chain[0] += 1
                        op.then_inc(sems["chain_dve"], 1)
                        dve.wait_ge(sems["chain_dve"], chain[0])

                    def take(s, name):
                        kind, b = plan.kind(s), plan.steps[s][1]
                        u = plan.at[s, name]
                        bank = proj_bank[u % 2]
                        dve.wait_ge(sems["proj_ready"], u + 1)
                        if kind == "mqa" and name != "kv":
                            half = int(name[1])
                            op = dve.tensor_tensor(Q8[:, s % 3, 4 * half:4 * half + 4, :], heads_view(bank[:, :], 4), qpe[:, 4 * half:4 * half + 4, :], ALU.add)
                        elif kind == "mqa":
                            dve.scalar_tensor_tensor(K8[:, s % 3, :], bank[:, 0:S], D ** -0.5, kpe[:, :], ALU.mult, ALU.add)
                            op = dve.tensor_copy(V8[:, s % 3, :], bank[:, S:2 * S])
                        elif name == "qk":
                            if b == 0:
                                weights(dve, s)
                            dve.tensor_tensor(QK[:, s % 2, :, :], heads_view(bank[:, 0:2 * S], 2), over(W(s, "cos"), 2), ALU.mult)
                            op = dve.tensor_tensor(RT2[:, s % 2, :, :], heads_view(bank[:, 2 * S:4 * S], 2), over(W(s, "sin"), 2), ALU.mult)
                        elif name == "v":
                            op = dve.tensor_tensor(Vm[:, s % 2, :, :], over(bank[:, 0:D], 4), value_pick, ALU.mult)
                        elif name == "router":
                            if b == 0:
                                weights(dve, s)
                            if kind == "lin":
                                op = dve.tensor_tensor(lg[:, b, :], bank[:, 0:NE], W(s, "bg"), ALU.add)
                            else:
                                op = dve.tensor_copy(lg[:, b, :], bank[:, 0:NE])
                        elif name[0] == "k":
                            i = int(name[1])
                            n = 4 if kind == "h64c" else 2
                            op = dve.tensor_copy(K64[:, s % 2, n * i:n * i + n, :], heads_view(bank[:, :], n))
                        elif name[0] == "v":
                            i = int(name[1])
                            op = dve.tensor_copy(V64[:, s % 2, i // 2, (i % 2) * 512:(i % 2 + 1) * 512], bank[:, :])
                        op.then_inc(sems["proj_by_dve"], 1)
                        if name == "qk":
                            after_reader(dve, s, name)
                            dve.tensor_tensor(QK[:, s % 2, :, :], QK[:, s % 2, :, :], RT2[:, s % 2, :, :], ALU.add).then_inc(sems["rope_ready"], 1)
                        if name == "router":
                            after_reader(dve, s, name)
                            dve.tensor_reduce(lmax[:, b:b + 1], lg[:, b, :], axis=AX.X, op=ALU.max, negate=True).then_inc(sems["logits_ready"], 1)
                            choose(s)

                    def choose(s):
                        b, kind = plan.steps[s][1], plan.kind(s)
                        k = 1 + sum(plan.kind(t) in ("moe", "lin") for t in range(s))
                        mine, other = along(lg[:, b, :], NE), over(lg[:, b, :], NE)
                        dve.tensor_tensor(beat[:, b, :, :], other, mine, ALU.is_gt)
                        link(dve.tensor_tensor(tie[:, b, :, :], other, mine, ALU.is_equal))
                        link(dve.tensor_tensor(tie[:, b, :, :], tie[:, b, :, :], lower, ALU.mult))
                        link(dve.tensor_tensor(beat[:, b, :, :], beat[:, b, :, :], tie[:, b, :, :], ALU.add))
                        link(dve.tensor_reduce(rank[:, b, :], beat[:, b, :, :], axis=AX.X, op=ALU.add))
                        link(dve.tensor_scalar(pick[:, b, :], rank[:, b, :], 2.0, None, ALU.is_lt))
                        dve.wait_ge(sems["route_exp"], k)
                        link(dve.reciprocal(linv[:, b:b + 1], lsum[:, b:b + 1]))
                        link(dve.scalar_tensor_tensor(pick[:, b, :], lexp[:, b, :], linv[:, b:b + 1], pick[:, b, :], ALU.mult, ALU.mult))
                        link(dve.tensor_reduce(wsum[:, b:b + 1], pick[:, b, :], axis=AX.X, op=ALU.add))
                        if kind == "moe":
                            link(dve.tensor_scalar(wsum[:, b:b + 1], wsum[:, b:b + 1], 1e-9, None, ALU.add))
                        link(dve.reciprocal(winv[:, b:b + 1], wsum[:, b:b + 1]))
                        dve.tensor_scalar(gatew[:, b, :], pick[:, b, :], winv[:, b:b + 1], None, ALU.mult).then_inc(sems["route_ready"], 1)

                    def front(n):
                        s, i, kind, b = plan.unit(n)
                        bank = score_bank[n % 3]
                        if kind in STAGES["negmax"]:
                            heads = 2 if kind == "h64m" else 4
                            dve.wait_ge(sems["scores_ready"], n + 1)
                            dve.tensor_reduce(negmax[:, n % 4, 0:heads], heads_view(bank[:, :], heads), axis=AX.X, op=ALU.max, negate=True).then_inc(sems["negmax_ready"], 1)
                        elif kind == "h64c":
                            if i == 0 and b == 0:
                                dve.wait_ge(sems["keymask_ready"], 1)
                            dve.wait_ge(sems["scores_ready"], n + 1)
                            dve.scalar_tensor_tensor(heads_view(Pb[:, n % 3, :], 4), heads_view(bank[:, :], 4), -5.0, over(clip_hi[:, b, :], 4),
                                                     ALU.max, ALU.min).then_inc(sems["clip_done"], 1)
                        elif kind == "moe":
                            dve.wait_ge(sems["silu_done"], plan.count("silu", n))
                            for j in range(2):
                                op = dve.scalar_tensor_tensor(H[:, n % 3, j, :], bank[:, (2 + j) * S:(3 + j) * S], W(s, "up_b")[:, 2 * i + j:2 * i + j + 1],
                                                              HS[:, n % 3, j, :], ALU.add, ALU.mult)
                            op.then_inc(sems["gate_done"], 1)

                    def inverse(n):
                        s, i, kind, b = plan.unit(n)
                        if kind in SOFTMAX:
                            heads = 2 if kind == "h64m" else 4
                            dve.wait_ge(sems["exp_done"], plan.count("exp", n))
                            dve.reciprocal(rinv[:, n % 4, 0:heads], rsum[:, n % 4, 0:heads]).then_inc(sems["rsum_ready"], 1)

                    def back(n):
                        s, i, kind, b = plan.unit(n)
                        if kind in STAGES["pt_dve"]:
                            m = plan.count("second", n) - 1
                            dve.wait_ge(sems["second_ready"], m + 1)
                            dve.tensor_copy(PT[:, n % 2, :], second_bank[m % 2][:, :]).then_inc(sems["pt_dve"], 1)
                        elif kind in STAGES["acc"]:
                            k = plan.count("acc", n)
                            if i == 0:
                                dve.wait_ge(sems["acc_start"], 1 + sum(plan.kind(t) in STAGES["acc"] for t in range(s)))
                            else:
                                dve.wait_ge(sems["acc_done"], k - 1)
                            if kind == "lin":
                                dve.wait_ge(sems["scores_ready"], n + 1)
                                for j in range(4):
                                    e = 4 * i + j
                                    op = dve.scalar_tensor_tensor(R[:, b, :], score_bank[n % 3][:, j * D:(j + 1) * D], gatew[:, b, e:e + 1], R[:, b, :], ALU.mult, ALU.add)
                                    if j < 3:
                                        link(op)
                            else:
                                m = plan.count("second", n) - 1
                                dve.wait_ge(sems["second_ready"], m + 1)
                                by = gatew[:, b, i:i + 1] if kind == "moe" else 0.5
                                op = dve.scalar_tensor_tensor(R[:, b, :], second_bank[m % 2][:, 0:D], by, R[:, b, :], ALU.mult, ALU.add)
                            op.then_inc(sems["acc_done"], 1)

                    def add_and_stats(s):
                        b, kind = plan.steps[s][1], plan.kind(s)
                        if kind in SOFTMAX:
                            u = plan.at[s, "y"]
                            if plan.layer(s).out_bias:
                                dve.wait_ge(sems["resid_ready"], 1 + sum(plan.layer(t).out_bias for t in range(s)))
                            else:
                                state_ready(dve, s)
                            dve.wait_ge(sems["proj_ready"], u + 1)
                            dve.tensor_tensor(R[:, b, :], proj_bank[u % 2][:, 0:D], (XR if plan.layer(s).out_bias else X)[:, b, :], ALU.add).then_inc(sems["proj_by_dve"], 1)
                            after_reader(dve, s, "y")
                        else:
                            dve.wait_ge(sems["acc_done"], plan.count("acc", plan.last[s]))
                        link(dve.bn_stats(st6[:, b, :], R[:, b, :]))
                        link(dve.bn_aggr(mv[:, b, :], st6[:, b, :]))
                        dve.tensor_scalar(ve[:, b:b + 1], mv[:, b, 1:2], EPS, None, ALU.add).then_inc(sems["var_ready"], 1)

                    def normalise(s):
                        b = plan.steps[s][1]
                        dve.wait_ge(sems["rstd_ready"], s + 1)
                        to = X[:, b, :]
                        if plan.next_kind(s) is None and not last_loop:
                            to = state[:, bass.ds(it * G + b, 1), :].rearrange("p a d -> p (a d)")
                        dve.tensor_scalar(to, R[:, b, :], mv[:, b, 0:1], rstd[:, b:b + 1], ALU.subtract, ALU.mult).then_inc(sems["x_ready"], 1)
                        if plan.affine_next(s):
                            dve.wait_ge(sems["x_ready"], s + 1)
                            link(dve.bn_stats(st6b[:, b, :], X[:, b, :]))
                            link(dve.bn_aggr(mv2[:, b, :], st6b[:, b, :]))
                            dve.tensor_scalar(ve2[:, b:b + 1], mv2[:, b, 1:2], EPS, None, ALU.add).then_inc(sems["stat2_ready"], 1)

                    def normalise_again(s):
                        b = plan.steps[s][1]
                        dve.wait_ge(sems["rstd2_ready"], 1 + sum(plan.affine_next(t) for t in range(s)))
                        dve.tensor_scalar(LH[:, b, :], X[:, b, :], mv2[:, b, 0:1], rstd2[:, b:b + 1], ALU.subtract, ALU.mult).then_inc(sems["norm2_ready"], 1)

                    if last_loop:
                        dve.tensor_copy(X[:, :, :], state[:, bass.ds(it * G, G), :]).then_inc(sems["state_in_dve"], 1)
                        dve.wait_ge(sems["ctx_in"], 16)
                        for b in range(G):
                            op = dve.bn_stats(st6b[:, b, :], CX[:, b, :])
                        link(op)
                        for b in range(G):
                            op = dve.bn_aggr(mv2[:, b, :], st6b[:, b, :])
                        link(op)
                        dve.tensor_scalar(ve2[:, :], mv2[:, :, 1], EPS, None, ALU.add).then_inc(sems["ctx_stats"], 1)
                        dve.wait_ge(sems["mask_in"], 16)
                        for j in range(2):
                            dve.tensor_scalar(key_mask[:, :, j, 0, :], mask_u8[:, :, :], -NEG, NEG, ALU.mult, ALU.add)
                            op = dve.memset(key_mask[:, :, j, 1, :], 0.0)
                        op.then_inc(sems["keymask_ready"], 1)
                        dve.wait_ge(sems["ctx_rstd"], 1)
                        for b in range(G):
                            op = dve.tensor_scalar(CX[:, b, :], CX[:, b, :], mv2[:, b, 0:1], rstd2[:, b:b + 1], ALU.subtract, ALU.mult)
                        op.then_inc(sems["ctx_norm"], 1)
                    else:
                        dve.wait_ge(sems["mask_in"], 16)
                        dve.tensor_scalar(clip_hi[:, :, :], mask_u8[:, :, :], 10.0, -5.0, ALU.mult, ALU.add).then_inc(sems["keymask_ready"], 1)
                    for n in plan.slots():
                        for s, name, eng in plan.early.get(n, []):
                            if eng == "dve":
                                take(s, name)
                        if 0 <= n + 2 < plan.n:
                            front(n + 2)
                        if 0 <= n + 1 < plan.n:
                            inverse(n + 1)
                        if 0 <= n < plan.n:
                            back(n)
                        for p, s in plan.after.get(n, []):
                            if p == 0:
                                add_and_stats(s)
                            if p == 1:
                                normalise(s)
                            if p == 2 and plan.affine_next(s):
                                normalise_again(s)

                @block.gpsimd
                def _(pool):
                    chain = [0]

                    def link(op):
                        chain[0] += 1
                        op.then_inc(sems["chain_pool"], 1)
                        pool.wait_ge(sems["chain_pool"], chain[0])

                    def spread(s):
                        if plan.kind(s) == "h8r":
                            pool.wait_ge(sems["rope_ready"], 1 + sum(plan.kind(t) == "h8r" for t in range(s)))
                        else:
                            after_reader(pool, s, "qk")
                        pool.tensor_tensor(Qg[:, s % 2, :, :], over(QK[:, s % 2, 0, :], 4), along(head_scale, S), ALU.mult).then_inc(sems["masked"], 1)
                        pool.tensor_tensor(Km[:, s % 2, :, :], over(QK[:, s % 2, 1, :], 4), along(head_pick, S), ALU.mult).then_inc(sems["masked"], 1)

                    def residual(s):
                        b = plan.steps[s][1]
                        if b == 0:
                            weights(pool, s)
                        state_ready(pool, s)
                        pool.tensor_tensor(XR[:, b, :], X[:, b, :], W(s, "bo"), ALU.add).then_inc(sems["resid_ready"], 1)

                    def start_sum(s):
                        b, kind = plan.steps[s][1], plan.kind(s)
                        if b == 0:
                            weights(pool, s)
                        state_ready(pool, s)
                        if kind == "ffn":
                            link(pool.tensor_tensor(R[:, b, :], X[:, b, :], half_b2[:, :], ALU.add))
                            pool.tensor_tensor(R[:, b, :], R[:, b, :], X[:, b, :], ALU.add).then_inc(sems["acc_start"], 1)
                            return
                        pool.wait_ge(sems["route_ready"], 1 + sum(plan.kind(t) in ("moe", "lin") for t in range(s)))
                        sums = sum(plan.kind(t) in STAGES["acc"] for t in range(s))
                        if sums:
                            pool.wait_ge(sems["acc_start"], sums)
                        link(pool.tensor_tensor(eb[:, :, :], heads_view(W(s, "be"), NE), along(gatew[:, b, :], D), ALU.mult))
                        link(pool.tensor_tensor(eb[:, 0:4, :], eb[:, 0:4, :], eb[:, 4:8, :], ALU.add))
                        link(pool.tensor_tensor(eb[:, 0:2, :], eb[:, 0:2, :], eb[:, 2:4, :], ALU.add))
                        link(pool.tensor_tensor(eb[:, 0, :], eb[:, 0, :], eb[:, 1, :], ALU.add))
                        pool.tensor_tensor(R[:, b, :], X[:, b, :], eb[:, 0, :], ALU.add).then_inc(sems["acc_start"], 1)

                    def probabilities(n):
                        s, i, kind, b = plan.unit(n)
                        if kind in SOFTMAX:
                            heads = 2 if kind == "h64m" else 4
                            pool.wait_ge(sems["rsum_ready"], plan.count("norm", n))
                            p = heads_view(Pb[:, n % 3, :], heads)
                            pool.tensor_tensor(p, p, along(rinv[:, n % 4, 0:heads], 512 // heads), ALU.mult).then_inc(sems["norm_done"], 1)

                    if last_loop:
                        pool.wait_ge(sems["ctx_stats"], 1)
                        pool.tensor_tensor(rstd2[:, :], ve2[:, :], neg_half[:, :], ALU.pow).then_inc(sems["ctx_rstd"], 1)
                    for n in plan.slots():
                        for s, name, eng in plan.early.get(n, []):
                            if name == "qk":
                                spread(s)
                            if name == "router":
                                start_sum(s)
                        for s in range(len(plan.steps)):
                            if plan.first[s] - 2 == n:
                                if plan.layer(s).out_bias:
                                    residual(s)
                                if plan.kind(s) == "ffn":
                                    start_sum(s)
                        if 0 <= n + 1 < plan.n:
                            probabilities(n + 1)
                        for p, s in plan.after.get(n, []):
                            b = plan.steps[s][1]
                            if p == 0:
                                pool.wait_ge(sems["var_ready"], s + 1)
                                pool.tensor_tensor(rstd[:, b:b + 1], ve[:, b:b + 1], neg_half[:, 0:1], ALU.pow).then_inc(sems["rstd_ready"], 1)
                            if p == 1 and plan.affine_next(s):
                                pool.wait_ge(sems["stat2_ready"], 1 + sum(plan.affine_next(t) for t in range(s)))
                                pool.tensor_tensor(rstd2[:, b:b + 1], ve2[:, b:b + 1], neg_half[:, 0:1], ALU.pow).then_inc(sems["rstd2_ready"], 1)

            nc.all_engine_barrier(sems_to_clear=body_range)
            iters.__exit__(None, None, None)

        a_names = ["const"] + [layer.name for layer in LOOP_A]
        with ExitStack() as scope:
            w = {}
            for layer in LOOP_A:
                w[layer.name] = sb("w_" + layer.name, [P, sum(n for _, n in cols[layer.name].values())], scope=scope)
            qpe = sb("qpe", [P, 8, S], scope=scope)
            kpe = sb("kpe", [P, S], scope=scope)
            with nc.Block() as block:
                @block.sync
                def _(sp):
                    sp.dma_start(const[:, :], dram["const"]).then_inc(w_in["const"], 16)
                    for layer in LOOP_A:
                        sp.dma_start(w[layer.name][:, :], dram[layer.name]).then_inc(w_in[layer.name], 16)

                @block.vector
                def _(dve):
                    dve.wait_ge(w_in["const"], 16)
                    dve.tensor_copy(ident_b[:, :], ident)
                    dve.tensor_copy(causal_b[:, :, :], over(part(const, "const", "causal"), 4))

                @block.gpsimd
                def _(pool):
                    pool.memset(neg_half[:, :], -0.5)
                    pool.wait_ge(w_in["const"], 16)
                    pool.wait_ge(w_in["L0_attn"], 16)
                    pe_t = part(const, "const", "pe")
                    pool.tensor_tensor(qpe[:, :, :], over(pe_t, 8), along(part(w["L0_attn"], "L0_attn", "bq"), S), ALU.add)
                    pool.tensor_scalar(kpe[:, :], pe_t, part(w["L0_attn"], "L0_attn", "bkv")[:, 0:1], D ** -0.5, ALU.add, ALU.mult)
            run_loop("a_", Plan(LOOP_A), w, scope, False)

        with ExitStack() as scope:
            w = {}
            for layer in LOOP_C:
                w[layer.name] = sb("w_" + layer.name, [P, sum(n for _, n in cols[layer.name].values())], scope=scope)
            q_in = sem("q_in")
            fc1_q = sb("fc1_q", [P, 512], I32, scope=scope)
            fc2_q = sb("fc2_q", [P, 512], I32, scope=scope)
            fc1 = sb("fc1", [P, 512], scope=scope)
            fc2 = sb("fc2", [P, 4, D], scope=scope)
            half_b2 = sb("half_b2", [P, D], scope=scope)
            state_t = sb("state_t", [P, B, S], scope=scope)
            with ExitStack() as own:
                quantised_ffn(nc, sb, sem, own, w, w_in, dram, cols, state, state_t, ident, neg_half,
                              score_bank + second_bank + [value_bank] + proj_bank, q_in, fc1_q, fc2_q)
            with nc.Block() as block:
                @block.vector
                def _(dve):
                    dve.wait_ge(w_in["L3_ffn"], 16)
                    dve.wait_ge(q_in, 32)
                    ffn = w["L3_ffn"]
                    dve.scalar_tensor_tensor(fc1[:, :], fc1_q[:, :], -128.0, part(ffn, "L3_ffn", "fc1_s"), ALU.add, ALU.mult)
                    dve.scalar_tensor_tensor(fc2[:, :, :].rearrange("p c d -> p (c d)"), fc2_q[:, :], -128.0, part(ffn, "L3_ffn", "fc2_s"), ALU.add, ALU.mult)
                    dve.tensor_scalar(half_b2[:, :], part(ffn, "L3_ffn", "fc2_b"), 0.5, None, ALU.mult)
            run_loop("c_", Plan(LOOP_C), w, scope, True, state_t)


def rope_tables():
    f = np.float32
    pos = np.arange(S, dtype=f)
    freq2 = (f(1.0) / f(10000.0) ** (np.arange(0, 8, 2, dtype=f) / f(8))).astype(f)
    freq3 = (f(10000.0) ** (-np.arange(0, 8, 2, dtype=f) / f(8))).astype(f)
    a2 = (freq2[np.arange(8) % 4][:, None] * pos[None, :]).astype(f)
    a3 = (freq3[np.arange(8) // 2][:, None] * pos[None, :]).astype(f)
    sign2 = np.where(np.arange(8) < 4, -1, 1).astype(f)[:, None]
    sign3 = np.where(np.arange(8) % 2 == 0, -1, 1).astype(f)[:, None]
    rows = lambda a: np.tile(a.astype(f), (16, 1))
    return rows(np.cos(a2)), rows(np.sin(a2) * sign2), rows(np.cos(a3)), rows(np.sin(a3) * sign3)


def constants():
    f = np.float32
    p = np.arange(P)
    group = np.where(p[:, None] // 32 == np.arange(4)[None, :], f(1.0 / np.sqrt(f(8.0))), 0).astype(f)
    pick = (p[:, None] % 32 // 8 == np.arange(4)[None, :]).astype(f)
    vpick = np.broadcast_to(pick.T.reshape(1, 4 * P), (P, 4 * P))
    lower = np.broadcast_to(np.tril(np.ones((NE, NE), f), -1).reshape(1, NE * NE), (P, NE * NE))
    causal = np.where(np.tril(np.ones((S, S), bool)), 0, NEG).astype(f)
    pos = np.arange(S, dtype=f)[:, None]
    ang = pos * np.exp(f(-np.log(10000.0)) * np.arange(0, D, 2, dtype=f) / f(D))[None, :]
    pe = np.zeros((S, D), f)
    pe[:, 0::2], pe[:, 1::2] = np.sin(ang), np.cos(ang)
    return [("ident", np.eye(P, dtype=f)), ("group", group), ("pick", pick), ("vpick", vpick), ("lower", lower), ("causal", causal), ("pe", pe.T)]


def laid_out(i):
    def column(v):
        return v.reshape(-1, P).T

    def row(v):
        return np.broadcast_to(v.reshape(1, -1), (P, v.size))

    def chunks(m):
        return m.reshape(-1, P, m.shape[1]).transpose(1, 0, 2).reshape(P, -1)

    def padded(m, n):
        return np.concatenate([m, np.zeros((P, n - m.shape[1]), m.dtype)], axis=1)

    cos2, sin2, cos3, sin3 = rope_tables()
    d = np.arange(P)
    turn2, turn3 = d // 8 * 8 + (d % 8 + 4) % 8, d ^ 1
    rel = np.arange(WINDOW)[:, None] - np.arange(WINDOW)[None, :] + WINDOW - 1
    relpos = np.full((S, 16, S), NEG, np.float32)
    for k in range(0, S, WINDOW):
        relpos[k:k + WINDOW, :, k:k + WINDOW] = i["L1_attn_rel_bias"][rel].transpose(0, 2, 1)
    packs = {"const": constants()}
    packs["L0_attn"] = [("Wq", i["L0_attn_Wq"]), ("Wkv", i["L0_attn_Wkv"]), ("Wo", chunks(i["L0_attn_Wo"])),
                        ("bq", column(i["L0_attn_bq"])), ("bkv", column(i["L0_attn_bkv"]))]
    for n in ("L0_xattn", "L1_xattn"):
        packs[n] = [(k, i[f"{n}_{k}"]) for k in ("Wq", "Wk", "Wv", "Wo")] + [(k, column(i[f"{n}_{k}"])) for k in ("bq", "bk", "bv")] + [("bo", row(i[f"{n}_bo"]))]
    packs["L0_ffn"] = [("Wr", padded(i["L0_ffn_router_w"].T, 64)),
                       ("gate_w", i["L0_ffn_gate_w"].transpose(1, 0, 2).reshape(P, -1)), ("up_w", i["L0_ffn_up_w"].transpose(1, 0, 2).reshape(P, -1)),
                       ("down_w", chunks(i["L0_ffn_down_w"].reshape(-1, D))),
                       ("gate_b", column(i["L0_ffn_gate_b"].reshape(-1))), ("up_b", column(i["L0_ffn_up_b"].reshape(-1))), ("be", row(i["L0_ffn_down_b"]))]
    qkv, qkv_b = i["L1_attn_qkv_w"], i["L1_attn_qkv_b"]
    packs["L1_attn"] = [("Wq", qkv[:, 0:D]), ("Wk", qkv[:, D:2 * D]), ("Wv", qkv[:, 2 * D:]), ("Wo", i["L1_attn_proj_w"]),
                        ("bq", column(qkv_b[0:D])), ("bk", column(qkv_b[D:2 * D])), ("bv", column(qkv_b[2 * D:])), ("bo", row(i["L1_attn_proj_b"])),
                        ("relpos", relpos.reshape(P, -1))]
    packs["L1_ffn"] = [("Wr", padded(i["L1_ffn_Wg"], 64)), ("We", i["L1_ffn_We"].transpose(1, 0, 2).reshape(P, -1)), ("be", row(i["L1_ffn_be"])), ("bg", row(i["L1_ffn_bg"]))]
    for n, turned, q, c, s in (("L2_attn", turn2, "W_", cos2, sin2), ("L3_attn", turn3, "W", cos3, sin3)):
        wq, wk, wv, wo = (i[f"{n}_{q}{k}"].T for k in (("Q", "K", "V", "O") if q == "W_" else ("q", "k", "v", "o")))
        packs[n] = [("Wq", wq), ("Wk", wk), ("Wv", wv), ("Wo", wo), ("Wq_turned", wq[:, turned]), ("Wk_turned", wk[:, turned]), ("cos", c), ("sin", s)]
    packs["L2_xattn"] = [("Wq", i["L2_xattn_Wq"]), ("Wk", i["L2_xattn_Wkv"][:, :1024]), ("Wv", i["L2_xattn_Wkv"][:, 1024:]), ("Wo", chunks(i["L2_xattn_Wo"])),
                         ("bo", row(i["L2_xattn_bo"]))]
    packs["L2_ffn"] = [("gate", chunks(i["L2_ffn_w_gate"])), ("up", chunks(i["L2_ffn_w_up"])), ("down", i["L2_ffn_w_down"])]
    packs["L3_xattn"] = [("Wq", i["L3_xattn_Wq"]), ("Wk", i["L3_xattn_Wkv"][:, :1024]), ("Wv", i["L3_xattn_Wkv"][:, 1024:]), ("Wo", chunks(i["L3_xattn_Wout"]))] + [
        (k, column(i[f"L3_xattn_{k}"])) for k in ("g1", "b1", "g2", "b2")]
    packs["L3_ffn"] = [("gamma", column(i["L3_ffn_ln_gamma"])), ("beta", column(i["L3_ffn_ln_beta"])), ("fc1_s", row(i["L3_ffn_fc1_scales"])),
                       ("fc1_b", column(i["L3_ffn_fc1_bias"])), ("fc2_s", row(i["L3_ffn_fc2_scales"])), ("fc2_b", row(i["L3_ffn_fc2_bias"]))]
    return packs


def kernel(**inputs):
    import concourse.bacc as bacc
    from concourse.bass_utils import run_bass_kernel_spmd

    i = {k: np.asarray(v) for k, v in inputs.items()}
    packs = laid_out(i)
    arrays, cols = {}, {}
    for name, parts in packs.items():
        cols[name], at = {}, 0
        for k, a in parts:
            cols[name][k] = (at, a.shape[1])
            at += a.shape[1]
        arrays[name] = np.ascontiguousarray(np.concatenate([a for _, a in parts], axis=1))
    tokens = lambda a: np.ascontiguousarray(a.reshape(NIT, G, S, D).transpose(0, 2, 1, 3).reshape(NIT, P, G * D))
    widths = lambda a: np.ascontiguousarray(a.reshape(NIT, G, S, D).transpose(0, 3, 1, 2).reshape(NIT, P, G * S))
    arrays["x"], arrays["xT"] = tokens(i["x"]), widths(i["x"])
    arrays["ctx"], arrays["ctxT"] = tokens(i["ctx_1024"]), widths(i["ctx_1024"])
    for k in ("bk0", "bk1"):
        arrays["mask_" + k] = np.ascontiguousarray(i["mask_BxS2_" + k]).reshape(NIT, G * S)
    arrays["fc1_q"] = np.ascontiguousarray(i["L3_ffn_fc1_q"])
    arrays["fc2_q"] = np.ascontiguousarray(i["L3_ffn_fc2_q"].reshape(4, P, D).transpose(1, 0, 2).reshape(P, 4 * D))

    nc = bacc.Bacc("TRN2", target_bir_lowering=False, num_devices=1)
    dram, feed = {}, {}
    for name, a in arrays.items():
        dram[name] = nc.dram_tensor("in_" + name, a.shape, mybir.dt.from_np(a.dtype), kind="ExternalInput").ap()
        feed["in_" + name] = a
    out = nc.dram_tensor("out", (B, S, D), F32, kind="ExternalOutput").ap()
    decoder_kernel(nc, dram, out, cols)
    r = run_bass_kernel_spmd(nc, [feed], core_ids=[0])
    return r.results[0]["out"]
```

```python
from contextlib import ExitStack

import numpy as np

import concourse.bass as bass
from concourse import mybir

F32 = mybir.dt.float32
BF16 = mybir.dt.bfloat16
I32 = mybir.dt.int32
U8 = mybir.dt.uint8
ALU = mybir.AluOpType
ACT = mybir.ActivationFunctionType
AX = mybir.AxisListType

B, S, D = 16, 128, 128
G = 4
NIT = B // G
P = 128
EPS = 1e-5
NEG = -1e30
MAGIC = 1.5 * 2.0 ** 23
NE = 8
N_PROJ = 3
WINDOW = 64

EARLY = {
    "mqa": [("q0", 4, "dve"), ("q1", 4, "dve"), ("kv", 4, "dve")],
    "h8": [("qk", 6, "act"), ("v", 4, "dve")],
    "h8r": [("qk", 6, "dve"), ("v", 4, "dve")],
    "moe": [("router", 24, "dve"), ("gateT", 22, "act"), ("biases", 21, "dve")],
    "lin": [("router", 24, "dve"), ("gateT", 22, "act"), ("biases", 21, "dve")],
    "h64c": [("q0", 6, "act"), ("q1", 6, "act"), ("k0", 5, "dve"), ("k1", 5, "dve"), ("v0", 4, "act"), ("v1", 4, "dve")],
    "h64m": [("c", 9, "act"), ("q0", 8, "act"), ("q1", 8, "act"), ("k0", 7, "dve"), ("k1", 7, "dve"), ("k2", 6, "dve"), ("k3", 6, "dve"),
             ("v0", 5, "act"), ("v1", 5, "dve"), ("v2", 4, "act"), ("v3", 4, "dve")],
    "ffn": [],
}
UNITS = {"mqa": 2, "h8": 4, "h8r": 4, "moe": 8, "lin": 2, "h64c": 4, "h64m": 8, "ffn": 2}
SOFTMAX = ("mqa", "h8", "h8r", "h64m", "h64c")
STAGES = {
    "scores": tuple(UNITS),
    "negmax": ("mqa", "h8", "h8r", "h64m"),
    "clip": ("h64c",),
    "exp": SOFTMAX,
    "norm": SOFTMAX,
    "silu": ("moe", "ffn"),
    "gate": ("moe",),
    "second": SOFTMAX + ("moe", "ffn"),
    "pt_act": ("h64m",),
    "pt_dve": ("mqa", "h8", "h8r", "h64c"),
    "acc": ("moe", "lin", "ffn"),
    "values": SOFTMAX,
}


class Layer:
    def __init__(self, name, kind, mask=None, ctx=False, bias=False, out_bias=False):
        self.name, self.kind, self.mask, self.ctx, self.bias, self.out_bias = name, kind, mask, ctx, bias, out_bias


LOOP_A = [
    Layer("L0_attn", "mqa", mask="causal"),
    Layer("L0_xattn", "h8", mask="causal", ctx=True, bias=True, out_bias=True),
    Layer("L0_ffn", "moe"),
    Layer("L1_attn", "h8", mask="relpos", bias=True, out_bias=True),
    Layer("L1_xattn", "h8", ctx=True, bias=True, out_bias=True),
    Layer("L1_ffn", "lin"),
    Layer("L2_attn", "h8r", mask="causal"),
    Layer("L2_xattn", "h64c", ctx=True, out_bias=True),
]
LOOP_C = [
    Layer("L3_attn", "h8r", mask="causal"),
    Layer("L3_xattn", "h64m", mask="keys"),
    Layer("L3_ffn", "ffn"),
]


class Plan:

    def __init__(self, layers):
        self.layers = layers
        self.steps = [(L, b) for L in range(len(layers)) for b in range(G)]
        self.units, self.first, self.last = [], [], []
        for s, (L, b) in enumerate(self.steps):
            self.first.append(len(self.units))
            self.units += [(s, i) for i in range(UNITS[layers[L].kind])]
            self.last.append(len(self.units) - 1)
        self.n = len(self.units)
        self.early, self.after = {}, {}
        for s in range(len(self.steps)):
            for name, ahead, eng in EARLY[self.kind(s)]:
                made = self.last[s - G] + dict(self.rest(s - G))["turn"] // 2 if s >= G else -6
                if self.kind(s) in ("moe", "lin"):
                    made += EARLY[self.kind(s)][0][1] - ahead
                self.early.setdefault(max(self.first[s] - ahead, made), []).append((s, name, eng))
            for what, half in self.rest(s):
                self.after.setdefault(2 * self.last[s] + half, []).append((what, s))
        self.uses = []
        for n in self.slots():
            for half in (0, 1):
                for what, s in self.after.get(2 * n + half, []):
                    if what == "output" and self.kind(s) in SOFTMAX:
                        self.uses.append((s, "y", "dve"))
                    if what == "turn":
                        self.uses.append((s, "xT", "act"))
            self.uses += self.early.get(n, [])
        self.at = {(s, name): u for u, (s, name, _) in enumerate(self.uses)}

    def rest(self, s):
        return 3 if self.kind(s) in SOFTMAX and not self.tight(s) else 2

    def tight(self, s):
        return self.kind(s) in ("mqa", "lin") or self.next_kind(s) in ("lin", "ffn")

    def slots(self):
        return range(-4, self.n + 7)

    def layer(self, s):
        return self.layers[self.steps[s][0]]

    def kind(self, s):
        return self.layer(s).kind

    def next_kind(self, s):
        L = self.steps[s][0] + 1
        return self.layers[L].kind if L < len(self.layers) else None

    def affine_next(self, s):
        return self.next_kind(s) in ("h64m", "ffn")

    def rest(self, s):
        tight = self.kind(s) in ("mqa", "lin") or self.next_kind(s) in ("lin", "ffn")
        if tight or self.kind(s) not in SOFTMAX:
            parts = [("output", 4), ("normalise", 6)]
        else:
            parts = [("output", 7), ("normalise", 9)]
        at = parts[-1][1]
        if self.affine_next(s):
            at += 2
            parts.append(("normalise_again", at))
        if self.next_kind(s):
            parts.append(("turn", at if tight else at + 2))
        return parts

    def slots(self):
        return range(-6, self.n + 7)

    def unit(self, n):
        s, i = self.units[n]
        return s, i, self.kind(s), self.steps[s][1]

    def count(self, stage, n):
        return sum(self.kind(s) in STAGES[stage] for s, _ in self.units[:n + 1])

    def used_by(self, eng, u):
        return sum(e == eng for _, _, e in self.uses[:u + 1])


def heads_view(ap, n):
    return ap.rearrange("p (n k) -> p n k", n=n)


def over(ap, n):
    return ap.unsqueeze(1).to_broadcast([ap.shape[0], n, ap.shape[1]])


def along(ap, n):
    return ap.unsqueeze(2).to_broadcast([ap.shape[0], ap.shape[1], n])


def quantised_ffn(nc, sb, sem, scope, w, w_in, dram, cols, state, state_t, ident, neg_half, banks, q_in, fc1_q, fc2_q):
    NT, FC = B * S, 3
    QMAX = 32767.0
    wq = sb("wq", [P, 9, D], scope=scope)
    wr = sb("wr", [P, 9, D], scope=scope)
    wt = sb("wt", [P, 9, D], scope=scope)
    bmax = sb("bmax", [P, 36], scope=scope)
    bscale = sb("bscale", [P, 36], scope=scope)
    binv = sb("binv", [P, 36], scope=scope)
    xq = sb("xq", [P, B, D], scope=scope)
    xqt = sb("xqt", [P, NT], scope=scope)
    hid = sb("hid", [P, 2 * FC, NT], scope=scope)
    sig = sb("sig", [P, FC, NT], scope=scope)
    cmax = sb("cmax", [P, 5, 12], scope=scope)
    pmax = sb("pmax", [P, 5], scope=scope)
    gmax = sb("gmax", [P, 5], scope=scope)
    scl = sb("scl", [P, 5], scope=scope)
    inv = sb("inv", [P, 5], scope=scope)
    R = sb("b_r", [P, B, D], scope=scope)
    st6 = sb("b_st6", [P, B, 6], scope=scope)
    mv = sb("b_mv", [P, B, 2], scope=scope)
    ve = sb("b_ve", [P, B], scope=scope)
    rstd = sb("b_rstd", [P, B], scope=scope)
    X_, GATE, UP, GATED, PROD = range(5)

    chain_dve, wq_ready, max_part, max_all, scale_ready, xq_ready = (sem("b_" + n) for n in ("chain", "wq_ready", "max_part", "max_all", "scale_ready", "xq_ready"))
    bank_full, bank_taken, down_taken, gate_ready, sig_ready, up_ready, up_chain, prod_ready, var_ready, rstd_ready, x_ready, neg_ready = (
        sem("b_" + n) for n in ("bank_full", "bank_taken", "down_taken", "gate_ready", "sig_ready", "up_ready", "up_chain", "prod_ready", "var_ready",
                                "rstd_ready", "x_ready", "neg_ready"))
    N_W, N_X, N_H = 3, 4, 24

    with nc.Block() as block:
        @block.sync
        def _(sp):
            sp.dma_start(wq[:, :, :].rearrange("p c d -> p (c d)"), dram["L2_ffn"]).then_inc(w_in["L2_ffn"], 16)
            for layer in LOOP_C:
                sp.dma_start(w[layer.name][:, :], dram[layer.name]).then_inc(w_in[layer.name], 16)
            sp.dma_start(fc1_q[:, :], dram["fc1_q"]).then_inc(q_in, 16)
            sp.dma_start(fc2_q[:, :], dram["fc2_q"]).then_inc(q_in, 16)

        @block.vector
        def _(dve):
            done = [0]

            def link(op):
                done[0] += 1
                op.then_inc(chain_dve, 1)
                dve.wait_ge(chain_dve, done[0])

            def scale(k):
                dve.wait_ge(max_all, k + 1)
                link(dve.tensor_scalar(scl[:, k:k + 1], gmax[:, k:k + 1], 1.0 / QMAX, 1e-12, ALU.mult, ALU.max))
                op = dve.reciprocal(inv[:, k:k + 1], scl[:, k:k + 1])
                op.then_inc(scale_ready, 1)
                dve.wait_ge(scale_ready, k + 1)

            def quantise(to, of, k):
                link(dve.tensor_scalar(to, of, inv[:, k:k + 1], MAGIC, ALU.mult, ALU.add))
                return dve.tensor_scalar(to, to, -MAGIC, scl[:, k:k + 1], ALU.add, ALU.mult)

            def absmax(to, of):
                return dve.tensor_reduce(to, of, axis=AX.X, op=ALU.max, apply_absolute_value=True)

            absmax(pmax[:, X_:X_ + 1], state[:, :, :].rearrange("p b d -> p (b d)")).then_inc(max_part, 1)
            dve.wait_ge(w_in["L2_ffn"], 16)
            blocks = wq[:, :, :].rearrange("p c (n k) -> p (c n) k", k=32)
            rounded = wr[:, :, :].rearrange("p c (n k) -> p (c n) k", k=32)
            link(absmax(bmax[:, :], blocks))
            link(dve.tensor_scalar(bscale[:, :], bmax[:, :], 1.0 / 7.0, 1e-12, ALU.mult, ALU.max))
            link(dve.reciprocal(binv[:, :], bscale[:, :]))
            link(dve.tensor_tensor(rounded, blocks, along(binv[:, :], 32), ALU.mult))
            link(dve.tensor_scalar(rounded, rounded, MAGIC, -MAGIC, ALU.add, ALU.add))
            dve.tensor_tensor(rounded, rounded, along(bscale[:, :], 32), ALU.mult).then_inc(wq_ready, 1)
            scale(X_)
            quantise(xq[:, :, :], state[:, :, :], X_).then_inc(xq_ready, 1)
            for k in range(N_H):
                dve.wait_ge(bank_taken, N_W + N_X + k + 1)
                op = absmax(cmax[:, GATE + k // 12, k % 12:k % 12 + 1], hid[:, k // 4, (k % 4) * 512:(k % 4 + 1) * 512])
                if k % 12 == 11:
                    link(op)
                    g = GATE + k // 12
                    absmax(pmax[:, g:g + 1], cmax[:, g, :]).then_inc(max_part, 1)
            scale(GATE)
            for c in range(FC):
                quantise(hid[:, c, :], hid[:, c, :], GATE).then_inc(gate_ready, 1)
            scale(UP)
            for c in range(FC):
                dve.wait_ge(sig_ready, c + 1)
                link(dve.tensor_scalar(sig[:, c, :], sig[:, c, :], 65536.0, MAGIC, ALU.mult, ALU.add))
                link(dve.tensor_scalar(sig[:, c, :], sig[:, c, :], -MAGIC, 65535.0, ALU.add, ALU.min))
                link(dve.scalar_tensor_tensor(hid[:, c, :], sig[:, c, :], 1.0 / 65536.0, hid[:, c, :], ALU.mult, ALU.mult))
                op = absmax(cmax[:, GATED, c:c + 1], hid[:, c, :])
            link(op)
            absmax(pmax[:, GATED:GATED + 1], cmax[:, GATED, 0:FC]).then_inc(max_part, 1)
            scale(GATED)
            for c in range(FC):
                link(quantise(hid[:, c, :], hid[:, c, :], GATED))
                dve.wait_ge(up_ready, c + 1)
                link(dve.tensor_tensor(hid[:, c, :], hid[:, c, :], hid[:, FC + c, :], ALU.mult))
                op = absmax(cmax[:, PROD, c:c + 1], hid[:, c, :])
            link(op)
            absmax(pmax[:, PROD:PROD + 1], cmax[:, PROD, 0:FC]).then_inc(max_part, 1)
            scale(PROD)
            for c in range(FC):
                quantise(hid[:, c, :], hid[:, c, :], PROD).then_inc(prod_ready, 1)
            for g in range(4):
                u = N_W + N_X + N_H + g
                dve.wait_ge(bank_full, u + 1)
                sl = slice(4 * g, 4 * g + 4)
                dve.tensor_tensor(R[:, sl, :], heads_view(banks[u % 8][:, :], 4), state[:, sl, :], ALU.add).then_inc(down_taken, 1)
                dve.wait_ge(down_taken, g + 1)
                for b in range(4 * g, 4 * g + 4):
                    op = dve.bn_stats(st6[:, b, :], R[:, b, :])
                link(op)
                for b in range(4 * g, 4 * g + 4):
                    op = dve.bn_aggr(mv[:, b, :], st6[:, b, :])
                link(op)
                dve.tensor_scalar(ve[:, sl], mv[:, sl, 1], EPS, None, ALU.add).then_inc(var_ready, 1)
            for g in range(4):
                dve.wait_ge(rstd_ready, g + 1)
                for b in range(4 * g, 4 * g + 4):
                    op = dve.tensor_scalar(state[:, b, :], R[:, b, :], mv[:, b, 0:1], rstd[:, b:b + 1], ALU.subtract, ALU.mult)
                op.then_inc(x_ready, 1)

        @block.gpsimd
        def _(pool):
            for k in range(3):
                pool.wait_ge(max_part, k + 1)
                pool.partition_all_reduce(gmax[:, k:k + 1], pmax[:, k:k + 1], P, bass.bass_isa.ReduceOp.max).then_inc(max_all, 1)
            pool.wait_ge(scale_ready, UP + 1)
            for c in range(FC):
                up = hid[:, FC + c, :]
                pool.tensor_scalar(up, up, inv[:, UP:UP + 1], MAGIC, ALU.mult, ALU.add).then_inc(up_chain, 1)
                pool.wait_ge(up_chain, c + 1)
                pool.tensor_scalar(up, up, -MAGIC, scl[:, UP:UP + 1], ALU.add, ALU.mult).then_inc(up_ready, 1)
            for k in range(3, 5):
                pool.wait_ge(max_part, k + 1)
                pool.partition_all_reduce(gmax[:, k:k + 1], pmax[:, k:k + 1], P, bass.bass_isa.ReduceOp.max).then_inc(max_all, 1)
            for g in range(4):
                pool.wait_ge(var_ready, g + 1)
                pool.tensor_tensor(rstd[:, 4 * g:4 * g + 4], ve[:, 4 * g:4 * g + 4], neg_half[:, :], ALU.pow).then_inc(rstd_ready, 1)

        @block.tensor
        def _(pe):
            pe.wait_ge(wq_ready, 1)
            for u in range(N_W):
                for j in range(3):
                    mm = pe.transpose(banks[u][:, j * P:(j + 1) * P], wr[:, 3 * u + j, :], ident)
                mm.then_inc(bank_full, 1)
            pe.wait_ge(xq_ready, 1)
            for t in range(N_X):
                for j in range(4):
                    mm = pe.transpose(banks[N_W + t][:, j * P:(j + 1) * P], xq[:, 4 * t + j, :], ident)
                mm.then_inc(bank_full, 1)
            pe.wait_ge(bank_taken, N_W + N_X)
            for k in range(N_H):
                u = N_W + N_X + k
                if u >= N_W + N_X + 1:
                    pe.wait_ge(bank_taken, max(u - 7, N_W + N_X))
                pe.matmul(banks[u % 8][:, :], wt[:, k // 4, :], xqt[:, (k % 4) * 512:(k % 4 + 1) * 512], start=True, stop=True).then_inc(bank_full, 1)
            pe.wait_ge(prod_ready, FC)
            pe.wait_ge(bank_taken, N_W + N_X + N_H)
            for g in range(4):
                u = N_W + N_X + N_H + g
                for j in range(4):
                    t = 4 * g + j
                    for c in range(FC):
                        mm = pe.matmul(banks[u % 8][:, j * D:(j + 1) * D], hid[:, c, t * S:(t + 1) * S], wt[:, 6 + c, :], start=c == 0, stop=c == FC - 1)
                mm.then_inc(bank_full, 1)
            for g in range(4):
                u = N_W + N_X + N_H + 4 + g
                pe.wait_ge(x_ready, g + 1)
                for j in range(4):
                    mm = pe.transpose(banks[u % 8][:, j * S:(j + 1) * S], state[:, 4 * g + j, :], ident)
                mm.then_inc(bank_full, 1)

        @block.scalar
        def _(act):
            for u in range(N_W):
                act.wait_ge(bank_full, u + 1)
                act.activation(wt[:, 3 * u:3 * u + 3, :], heads_view(banks[u][:, 0:3 * P], 3), ACT.Copy).then_inc(bank_taken, 1)
            for t in range(N_X):
                act.wait_ge(bank_full, N_W + t + 1)
                act.activation(xqt[:, t * 512:(t + 1) * 512], banks[N_W + t][:, :], ACT.Copy).then_inc(bank_taken, 1)
            for k in range(N_H):
                u = N_W + N_X + k
                act.wait_ge(bank_full, u + 1)
                act.activation(hid[:, k // 4, (k % 4) * 512:(k % 4 + 1) * 512], banks[u % 8][:, :], ACT.Copy).then_inc(bank_taken, 1)
            for c in range(FC):
                act.wait_ge(gate_ready, c + 1)
                act.activation(sig[:, c, :], hid[:, c, :], ACT.Sigmoid).then_inc(sig_ready, 1)
            for g in range(4):
                u = N_W + N_X + N_H + 4 + g
                act.wait_ge(bank_full, u + 1)
                act.activation(state_t[:, 4 * g:4 * g + 4, :], heads_view(banks[u % 8][:, :], 4), ACT.Copy).then_inc(bank_taken, 1)


def decoder_kernel(nc, dram, out, cols):
    ctx = ExitStack()
    with ctx:
        def sb(name, shape, dt=F32, scope=ctx):
            return scope.enter_context(nc.sbuf_tensor(name, shape, dt))

        def sem(name):
            return ctx.enter_context(nc.semaphore(name))

        def part(tensor, pack, name):
            a, n = cols[pack][name]
            return tensor[:, a:a + n]

        w_in = {k: sem(f"w_in_{k}") for k in cols}
        body_names = ["x_in", "xt_in", "ctx_in", "mask_in", "x_out",
                      "proj_ready",
                      "proj_by_act", "proj_by_dve",
                      "masked",
                      "rope_ready",
                      "scores_ready", "negmax_ready", "clip_done", "exp_done", "rsum_ready", "norm_done",
                      "second_ready", "pt_act", "pt_dve", "values_ready", "out_taken",
                      "silu_done", "gate_done", "acc_done", "acc_start",
                      "resid_ready",
                      "logits_ready", "route_exp", "route_ready",
                      "var_ready", "rstd_ready", "x_ready", "stat2_ready", "rstd2_ready", "norm2_ready",
                      "chain_dve", "chain_pool", "keymask_ready",
                      "ctx_stats", "ctx_rstd", "ctx_norm", "state_in_dve", "state_in_act"]
        sems = {n: sem("body_" + n) for n in body_names}
        nums = sorted(x.num for x in sems.values())
        assert nums == list(range(nums[0], nums[-1] + 1))
        body_range = range(nums[0], nums[-1] + 1)

        score_bank = [ctx.enter_context(nc.psum_tensor(f"score_bank{i}", [P, 512], F32)) for i in range(3)]
        second_bank = ctx.enter_context(nc.psum_tensor("second_bank", [P, 512], F32))
        value_bank = ctx.enter_context(nc.psum_tensor("value_bank", [P, 512], F32))
        proj_bank = [ctx.enter_context(nc.psum_tensor(f"proj_bank{i}", [P, 512], F32)) for i in range(N_PROJ)]

        const = sb("const", [P, sum(n for _, n in cols["const"].values())])
        ident = part(const, "const", "ident")
        head_scale = part(const, "const", "group")
        value_pick = part(const, "const", "vpick").rearrange("p (j d) -> p j d", j=4)
        lower = part(const, "const", "lower").rearrange("p (i j) -> p i j", i=NE)
        ident_b = sb("ident_b", [P, P], BF16)
        causal_b = sb("causal_b", [P, 4, P], BF16)
        neg_half = sb("neg_half", [P, G])
        state = sb("state", [P, B, D])

        def run_loop(tag, plan, w, scope, last_loop, state_t=None):
            X = sb(tag + "x", [P, G, D], scope=scope)
            XT = sb(tag + "xt", [P, G, S], scope=scope)
            XR = sb(tag + "xr", [P, G, D], scope=scope)
            R = sb(tag + "r", [P, G, D], scope=scope)
            st6 = sb(tag + "st6", [P, G, 6], scope=scope)
            mv = sb(tag + "mv", [P, G, 2], scope=scope)
            ve = sb(tag + "ve", [P, G], scope=scope)
            rstd = sb(tag + "rstd", [P, G], scope=scope)
            Pb = sb(tag + "probs", [P, 3, 512], scope=scope)
            PT = sb(tag + "probs_t", [P, 2, 512], scope=scope)
            negmax = sb(tag + "negmax", [P, 4, 4], scope=scope)
            rsum = sb(tag + "rsum", [P, 4, 4], scope=scope)
            rinv = sb(tag + "rinv", [P, 4, 4], scope=scope)
            OT = sb(tag + "ot", [P, 2, 8, S], scope=scope)
            QK = sb(tag + "qk", [P, 2, 2, S], scope=scope)
            RT2 = sb(tag + "rt", [P, 2, 2, S], scope=scope)
            Qg = sb(tag + "qg", [P, 2, 4, S], scope=scope)
            Km = sb(tag + "km", [P, 2, 4, S], scope=scope)
            Vm = sb(tag + "vm", [P, 2, 4, D], scope=scope)
            Qz = sb(tag + "qz", [P, 2, 8, 2, S], scope=scope)
            nkeys = 2 * S if last_loop else S
            K64 = sb(tag + "k64", [P, 2, 8, nkeys], scope=scope)
            V64 = sb(tag + "v64", [P, 2, nkeys // S, 1024], scope=scope)
            H = sb(tag + "h", [P, 3, 2, S], scope=scope)
            HS = sb(tag + "hs", [P, 3, 2, S], scope=scope)
            if last_loop:
                KV = sb(tag + "kv", [P, G, 2, S], scope=scope)
                CX = sb(tag + "cx", [P, G, D], scope=scope)
                LH = sb(tag + "lh", [P, G, D], scope=scope)
                st6b = sb(tag + "st6b", [P, G, 6], scope=scope)
                mv2 = sb(tag + "mv2", [P, G, 2], scope=scope)
                ve2 = sb(tag + "ve2", [P, G], scope=scope)
                rstd2 = sb(tag + "rstd2", [P, G], scope=scope)
                mask_u8 = sb(tag + "mask_u8", [P, G, S], U8, scope=scope)
                key_mask = sb(tag + "key_mask", [P, G, 2, 2, S], BF16, scope=scope)
            else:
                CT = sb(tag + "ct", [P, G, S], scope=scope)
                Q8 = sb(tag + "q8", [P, 3, 8, S], scope=scope)
                K8 = sb(tag + "k8", [P, 3, S], scope=scope)
                V8 = sb(tag + "v8", [P, 3, D], scope=scope)
                mask_u8 = sb(tag + "mask_u8", [P, G, S], U8, scope=scope)
                clip_hi = sb(tag + "clip_hi", [P, G, S], scope=scope)
                lg = sb(tag + "lg", [P, G, NE], scope=scope)
                lmax = sb(tag + "lmax", [P, G], scope=scope)
                lexp = sb(tag + "lexp", [P, G, NE], scope=scope)
                lsum = sb(tag + "lsum", [P, G], scope=scope)
                beat = sb(tag + "beat", [P, G, NE, 2, NE], scope=scope)
                rank = sb(tag + "rank", [P, G, NE], scope=scope)
                pick = sb(tag + "pick", [P, G, NE], scope=scope)
                wsum = sb(tag + "wsum", [P, G], scope=scope)
                winv = sb(tag + "winv", [P, G], scope=scope)
                gatew = sb(tag + "gatew", [P, G, NE], scope=scope)
                gatewT = sb(tag + "gatew_t", [NE, G, S], scope=scope)
            with nc.Block() as block:
                @block.vector
                def _(dve):
                    dve.memset(Km[:, :, :, :], 0.0)

                @block.gpsimd
                def _(pool):
                    pool.memset(Qz[0:64, :, :, 1, :], 0.0)
                    pool.memset(Qz[64:128, :, :, 0, :], 0.0)
            iters = nc.Fori(0, NIT)
            it = iters.__enter__()

            names = [plan.layers[L].name for L, _ in plan.steps]

            def used(eng, s, name):
                u = plan.at[s, name]
                reader = plan.uses[u][2]
                return sems["proj_by_" + reader], plan.used_by(reader, u)

            def after_reader(eng, s, name):
                eng.wait_ge(*used(eng, s, name))

            def state_t_ready(eng, s):
                if s < G:
                    if last_loop:
                        eng.wait_ge(sems["state_in_act"], 1)
                    else:
                        eng.wait_ge(sems["xt_in"], 16)
                else:
                    after_reader(eng, s - G, "xT")

            def state_ready(eng, s):
                if s < G:
                    if last_loop:
                        eng.wait_ge(sems["state_in_dve"], 1)
                    else:
                        eng.wait_ge(sems["x_in"], 16)
                else:
                    eng.wait_ge(sems["x_ready"], s - G + 1)

            def weights(eng, s):
                eng.wait_ge(w_in[names[s]], 16)

            def W(s, name):
                return part(w[names[s]], names[s], name)

            def routed(s):
                return sum(plan.kind(t) in ("moe", "lin") for t in range(s + 1))

            def second_of(n):
                s, i, kind, _ = plan.unit(n)
                return value_bank if kind in ("moe", "ffn") and i % 2 else second_bank

            def out_before(n):
                k = 0
                for m in range(min(n, plan.n)):
                    s, i, kind, _ = plan.unit(m)
                    k += kind in ("mqa", "h64c", "h64m") or (kind in ("h8", "h8r") and i == 3)
                return k

            with nc.Block() as block:
                @block.sync
                def _(sp):
                    if last_loop:
                        sp.dma_start(CX[:, :, :].rearrange("p a n -> p (a n)"), dram["ctx"][bass.ds(it, 1)].rearrange("a p n -> p (a n)")).then_inc(sems["ctx_in"], 16)
                        sp.dma_start(mask_u8[:, :, :].rearrange("p a n -> p (a n)"), dram["mask_bk0"][bass.ds(it, 1)].rearrange("a n -> (a n)").partition_broadcast(P)).then_inc(sems["mask_in"], 16)
                        for b in range(G):
                            sp.wait_ge(sems["x_ready"], (len(plan.layers) - 1) * G + b + 1)
                            sp.dma_start(out[bass.ds(it * G + b, 1)].rearrange("a p d -> p (a d)"), X[:, b, :]).then_inc(sems["x_out"], 16)
                        sp.wait_ge(sems["x_out"], 16 * G)
                    else:
                        sp.dma_start(XT[:, :, :].rearrange("p a n -> p (a n)"), dram["xT"][bass.ds(it, 1)].rearrange("a p n -> p (a n)")).then_inc(sems["xt_in"], 16)
                        sp.dma_start(X[:, :, :].rearrange("p a n -> p (a n)"), dram["x"][bass.ds(it, 1)].rearrange("a p n -> p (a n)")).then_inc(sems["x_in"], 16)
                        sp.dma_start(CT[:, :, :].rearrange("p a n -> p (a n)"), dram["ctxT"][bass.ds(it, 1)].rearrange("a p n -> p (a n)")).then_inc(sems["ctx_in"], 16)
                        sp.dma_start(mask_u8[:, :, :].rearrange("p a n -> p (a n)"), dram["mask_bk1"][bass.ds(it, 1)].rearrange("a n -> (a n)").partition_broadcast(P)).then_inc(sems["mask_in"], 16)

                @block.tensor
                def _(pe):
                    def open_use(s, name):
                        u = plan.at[s, name]
                        if u >= N_PROJ:
                            after_reader(pe, *plan.uses[u - N_PROJ][:2])
                        return proj_bank[u % N_PROJ]

                    def project(s, name):
                        kind, b = plan.kind(s), plan.steps[s][1]
                        bank = open_use(s, name)
                        if b == 0:
                            weights(pe, s)
                        if name not in ("gateT", "biases") and kind != "h64m":
                            state_t_ready(pe, s)
                        kv = XT
                        if plan.layer(s).ctx and name != "q0" and name != "q1":
                            pe.wait_ge(sems["ctx_in"], 16)
                            kv = CT
                        xt = XT[:, b, :]
                        if kind == "mqa" and name != "kv":
                            for j in range(4):
                                h = 4 * int(name[1]) + j
                                mm = pe.matmul(bank[:, j * S:(j + 1) * S], W(s, "Wq")[:, h * P:(h + 1) * P], xt, start=True, stop=True)
                        elif kind == "mqa":
                            pe.matmul(bank[:, 0:S], W(s, "Wkv")[:, 0:P], xt, start=True, stop=True)
                            mm = pe.matmul(bank[:, S:2 * S], xt, W(s, "Wkv")[:, P:2 * P], start=True, stop=True)
                        elif name == "qk":
                            pe.matmul(bank[:, 0:S], W(s, "Wq"), xt, start=True, stop=True)
                            mm = pe.matmul(bank[:, S:2 * S], W(s, "Wk"), kv[:, b, :], start=True, stop=True)
                            if kind == "h8r":
                                pe.matmul(bank[:, 2 * S:3 * S], W(s, "Wq_turned"), xt, start=True, stop=True)
                                mm = pe.matmul(bank[:, 3 * S:4 * S], W(s, "Wk_turned"), xt, start=True, stop=True)
                        elif name == "v":
                            mm = pe.matmul(bank[:, 0:D], kv[:, b, :], W(s, "Wv"), start=True, stop=True)
                        elif name == "router":
                            mm = pe.matmul(bank[:, 0:64], xt, W(s, "Wr"), start=True, stop=True)
                        elif name == "gateT":
                            pe.wait_ge(sems["route_ready"], routed(s))
                            mm = pe.transpose(bank[0:NE, 0:P], gatew[:, b, :], ident)
                        elif name == "biases":
                            after_reader(pe, s, "gateT")
                            mm = pe.matmul(bank[:, 0:D], gatewT[:, b, :], W(s, "be")[0:NE, :], start=True, stop=True)
                        elif kind == "h64c":
                            half = int(name[1])
                            for j in range(4):
                                c = 4 * half + j
                                to = bank[:, j * S:(j + 1) * S]
                                if name[0] == "q":
                                    mm = pe.matmul(to, W(s, "Wq")[:, c * P:(c + 1) * P], xt, start=True, stop=True)
                                if name[0] == "k":
                                    mm = pe.matmul(to, W(s, "Wk")[:, c * P:(c + 1) * P], CT[:, b, :], start=True, stop=True)
                            if name[0] == "v":
                                mm = pe.matmul(bank[:, :], CT[:, b, :], W(s, "Wv")[:, half * 512:(half + 1) * 512], start=True, stop=True)
                        else:
                            if name == "c":
                                pe.wait_ge(sems["ctx_norm"], 1)
                            else:
                                after_reader(pe, s, "c")
                                after_reader(pe, s - G, "xT")
                                i = int(name[1])
                            if name == "c":
                                mm = pe.transpose(bank[:, 0:S], CX[:, b, :], ident)
                            elif name[0] == "q":
                                for j in range(4):
                                    c = 4 * i + j
                                    mm = pe.matmul(bank[:, j * S:(j + 1) * S], W(s, "Wq")[:, c * P:(c + 1) * P], KV[:, b, 1, :], start=True, stop=True)
                            elif name[0] == "k":
                                for j in range(2):
                                    c = 2 * i + j
                                    mm = pe.matmul(bank[:, j * 256:(j + 1) * 256], W(s, "Wk")[:, c * P:(c + 1) * P],
                                                   KV[:, b, :, :].rearrange("p a k -> p (a k)"), start=True, stop=True)
                            else:
                                mm = pe.matmul(bank[:, :], KV[:, b, i // 2, :], W(s, "Wv")[:, (i % 2) * 512:(i % 2 + 1) * 512], start=True, stop=True)
                        mm.then_inc(sems["proj_ready"], 1)

                    def scores(n):
                        s, i, kind, b = plan.unit(n)
                        bank = score_bank[n % 3]
                        if n >= 3:
                            k3 = plan.unit(n - 3)[2]
                            done = {"moe": ("gate_done", "gate"), "lin": ("acc_done", "acc"), "ffn": ("silu_done", "silu"),
                                    "h64c": ("clip_done", "clip")}.get(k3, ("exp_done", "exp"))
                            pe.wait_ge(sems[done[0]], plan.count(done[1], n - 3))
                        if i == 0:
                            if kind in SOFTMAX:
                                for name, _, _ in EARLY[kind]:
                                    if name[0] != "v":
                                        after_reader(pe, s, name)
                            if kind in ("moe", "lin"):
                                if b == 0:
                                    weights(pe, s)
                                state_t_ready(pe, s)
                            if kind in ("h8", "h8r"):
                                pe.wait_ge(sems["masked"], (1 + sum(plan.kind(t) in ("h8", "h8r") for t in range(s))))
                            if kind == "h64m" and b == 0:
                                pe.wait_ge(sems["keymask_ready"], 1)
                            if kind == "ffn":
                                if b == 0:
                                    weights(pe, s)
                                state_t_ready(pe, s)
                        mask = plan.layer(s).mask
                        if mask == "causal":
                            pe.matmul(bank[:, :], ident_b[:, :], causal_b[:, :, :].rearrange("p a k -> p (a k)"), start=True, stop=False)
                        elif mask == "keys":
                            pe.matmul(bank[:, :], ident_b[:, :], key_mask[:, b, :, :, :].rearrange("p a c k -> p (a c k)"), start=True, stop=False)
                        elif mask == "relpos":
                            pe.matmul(bank[:, :], ident, W(s, "relpos")[:, i * 512:(i + 1) * 512], start=True, stop=False)
                        if kind == "mqa":
                            for j in range(4):
                                mm = pe.matmul(bank[:, j * S:(j + 1) * S], Q8[:, s % 3, 4 * i + j, :], K8[:, s % 3, :], start=False, stop=j == 3)
                        elif kind in ("h8", "h8r"):
                            mm = pe.matmul(bank[:, :], Qg[:, s % 2, i, :], Km[:, s % 2, :, :].rearrange("p j k -> p (j k)"), start=mask is None, stop=True)
                        elif kind == "h64c":
                            for j in range(4):
                                mm = pe.matmul(bank[:, j * S:(j + 1) * S], Qz[:, s % 2, 2 * i + j // 2, j % 2, :], K64[:, s % 2, 2 * i + j // 2, :], start=True, stop=True)
                        elif kind == "h64m":
                            for j in range(2):
                                mm = pe.matmul(bank[:, j * 256:(j + 1) * 256], Qz[:, s % 2, i, j, :], K64[:, s % 2, i, :], start=False, stop=j == 1)
                        elif kind == "moe":
                            for j in range(4):
                                c = (2 * i + j % 2) * P
                                mm = pe.matmul(bank[:, j * S:(j + 1) * S], W(s, "gate_w" if j < 2 else "up_w")[:, c:c + P], XT[:, b, :], start=True, stop=True)
                        elif kind == "lin":
                            mm = pe.matmul(bank[:, :], XT[:, b, :], W(s, "We")[:, i * 512:(i + 1) * 512], start=True, stop=True)
                        elif kind == "ffn":
                            for j in range(2):
                                c = (2 * i + j) * P
                                mm = pe.matmul(bank[:, j * S:(j + 1) * S], fc1[:, c:c + P], XT[:, b, :], start=True, stop=True)
                        mm.then_inc(sems["scores_ready"], 1)

                    def second(n):
                        s, i, kind, b = plan.unit(n)
                        if kind not in STAGES["second"]:
                            return
                        bank = second_of(n)
                        before = [k for k in range(n) if plan.unit(k)[2] in STAGES["second"] and second_of(k) is bank]
                        if before:
                            kb = plan.unit(before[-1])[2]
                            stage = "acc" if kb in ("moe", "ffn") else "pt_act" if kb in STAGES["pt_act"] else "pt_dve"
                            pe.wait_ge(sems["acc_done" if stage == "acc" else stage], plan.count(stage, before[-1]))
                        if bank is value_bank and out_before(n):
                            pe.wait_ge(sems["out_taken"], out_before(n))
                        if kind in SOFTMAX:
                            pe.wait_ge(sems["norm_done"], plan.count("norm", n))
                            for j in range(4):
                                mm = pe.transpose(bank[:, j * S:(j + 1) * S], Pb[:, n % 3, j * S:(j + 1) * S], ident)
                        elif kind == "moe":
                            pe.wait_ge(sems["gate_done"], plan.count("gate", n))
                            for j in range(2):
                                c = (2 * i + j) * D
                                mm = pe.matmul(bank[:, 0:D], H[:, n % 3, j, :], W(s, "down_w")[:, c:c + D], start=j == 0, stop=j == 1)
                        else:
                            pe.wait_ge(sems["silu_done"], plan.count("silu", n))
                            for j in range(2):
                                mm = pe.matmul(bank[:, 0:D], H[:, n % 3, j, :], fc2[:, 2 * i + j, :], start=j == 0, stop=j == 1)
                        mm.then_inc(sems["second_ready"], 1)

                    def values(n):
                        s, i, kind, b = plan.unit(n)
                        if kind not in SOFTMAX:
                            return
                        stage = "pt_act" if kind in STAGES["pt_act"] else "pt_dve"
                        if i == 0:
                            for name, _, _ in EARLY[kind]:
                                if name[0] == "v":
                                    after_reader(pe, s, name)
                        pe.wait_ge(sems[stage], plan.count(stage, n))
                        outs = out_before(n)
                        if outs:
                            pe.wait_ge(sems["out_taken"], outs)
                        experts = [k for k in range(n) if second_of(k) is value_bank]
                        if experts:
                            pe.wait_ge(sems["acc_done"], plan.count("acc", experts[-1]))
                        pt = PT[:, n % 2, :]
                        if kind == "mqa":
                            mm = pe.matmul(value_bank[:, :], V8[:, s % 3, :], pt, start=True, stop=True)
                        elif kind in ("h8", "h8r"):
                            for j in range(4):
                                mm = pe.matmul(value_bank[32 * j:32 * j + 32, 0:S], Vm[:, s % 2, i, 32 * j:32 * j + 32], pt[:, j * S:(j + 1) * S], start=i == 0, stop=i == 3)
                        elif kind == "h64c":
                            for j in range(4):
                                h = 4 * i + j
                                mm = pe.matmul(value_bank[64 * (j % 2):64 * (j % 2) + 64, (j // 2) * S:(j // 2 + 1) * S],
                                               V64[:, s % 2, 0, h * 64:(h + 1) * 64], pt[:, j * S:(j + 1) * S], start=True, stop=True)
                        else:
                            for c in range(2):
                                for j in range(2):
                                    h = 2 * i + j
                                    mm = pe.matmul(value_bank[64 * j:64 * j + 64, 0:S], V64[:, s % 2, c, h * 64:(h + 1) * 64],
                                                   pt[:, (2 * j + c) * S:(2 * j + c + 1) * S], start=c == 0, stop=c == 1)
                        mm.then_inc(sems["values_ready"], 1)

                    def output(s):
                        bank = open_use(s, "y")
                        pe.wait_ge(sems["out_taken"], out_before(plan.last[s] + 1))
                        chunks = 1 if plan.kind(s) in ("h8", "h8r") else 8
                        for c in range(chunks):
                            mm = pe.matmul(bank[:, 0:D], OT[:, s % 2, c, :], W(s, "Wo")[:, c * D:(c + 1) * D], start=c == 0, stop=c == chunks - 1)
                        mm.then_inc(sems["proj_ready"], 1)

                    def turn(s):
                        b = plan.steps[s][1]
                        bank = open_use(s, "xT")
                        if plan.affine_next(s):
                            pe.wait_ge(sems["norm2_ready"], 1 + sum(plan.affine_next(t) for t in range(s)))
                            mm = pe.transpose(bank[:, 0:S], LH[:, b, :], ident)
                        else:
                            pe.wait_ge(sems["x_ready"], s + 1)
                            mm = pe.transpose(bank[:, 0:S], X[:, b, :], ident)
                        mm.then_inc(sems["proj_ready"], 1)

                    def after(half):
                        for what, s in plan.after.get(half, []):
                            if what == "output" and plan.kind(s) in SOFTMAX:
                                output(s)
                            if what == "turn":
                                turn(s)

                    for n in plan.slots():
                        after(2 * n)
                        if 0 <= n + 2 < plan.n:
                            scores(n + 2)
                        if 0 <= n < plan.n:
                            second(n)
                        if 0 <= n - 1 < plan.n:
                            values(n - 1)
                        after(2 * n + 1)
                        for s, name, _ in plan.early.get(n, []):
                            project(s, name)

                @block.scalar
                def _(act):
                    def take(s, name):
                        kind, b = plan.kind(s), plan.steps[s][1]
                        u = plan.at[s, name]
                        bank = proj_bank[u % N_PROJ]
                        act.wait_ge(sems["proj_ready"], u + 1)
                        if name == "qk":
                            if b == 0:
                                weights(act, s)
                            act.activation(QK[:, s % 2, 0, :], bank[:, 0:S], ACT.Identity, bias=W(s, "bq"))
                            for j in range(4):
                                rows = slice(32 * j, 32 * j + 32)
                                op = act.activation(Km[rows, s % 2, j, :], bank[rows, S:2 * S], ACT.Identity, bias=W(s, "bk")[rows, :])
                        elif name == "c":
                            if b == 0:
                                act.wait_ge(w_in["L3_xattn"], 16)
                            g, e = (part(w["L3_xattn"], "L3_xattn", k) for k in ("g1", "b1"))
                            op = act.activation(KV[:, b, 0, :], bank[:, 0:S], ACT.Identity, scale=g, bias=e)
                        elif name == "gateT":
                            op = act.activation(gatewT[:, b, :], bank[0:NE, 0:P], ACT.Copy)
                        elif name[0] == "q":
                            half = int(name[1])
                            for j in range(2):
                                op = act.activation(Qz[64 * j:64 * j + 64, s % 2, 4 * half:4 * half + 4, j, :],
                                                    heads_view(bank[64 * j:64 * j + 64, :], 4), ACT.Copy, scale=0.125)
                        elif name[0] == "v":
                            i = int(name[1])
                            op = act.activation(V64[:, s % 2, i // 2, (i % 2) * 512:(i % 2 + 1) * 512], bank[:, :], ACT.Copy)
                        else:
                            to = plan.next_kind(s)
                            if to == "h64m":
                                if b == 0:
                                    act.wait_ge(w_in["L3_xattn"], 16)
                                g, e = (part(w["L3_xattn"], "L3_xattn", k) for k in ("g2", "b2"))
                                op = act.activation(KV[:, b, 1, :], bank[:, 0:S], ACT.Identity, scale=g, bias=e)
                            elif to == "ffn":
                                if b == 0:
                                    act.wait_ge(w_in["L3_ffn"], 16)
                                g, e = (part(w["L3_ffn"], "L3_ffn", k) for k in ("gamma", "beta"))
                                op = act.activation(XT[:, b, :], bank[:, 0:S], ACT.Identity, scale=g, bias=e)
                            else:
                                op = act.activation(XT[:, b, :], bank[:, 0:S], ACT.Copy)
                        op.then_inc(sems["proj_by_act"], 1)

                    def front(n):
                        s, i, kind, b = plan.unit(n)
                        if kind in SOFTMAX:
                            heads, width = (2, 256) if kind == "h64m" else (4, S)
                            if kind == "h64c":
                                act.wait_ge(sems["clip_done"], plan.count("clip", n))
                            else:
                                act.wait_ge(sems["negmax_ready"], plan.count("negmax", n))
                            for j in range(heads):
                                p = Pb[:, n % 3, j * width:(j + 1) * width]
                                if kind == "h64c":
                                    op = act.activation(p, p, ACT.Exp, accum_out=rsum[:, n % 4, j:j + 1])
                                else:
                                    op = act.activation(p, score_bank[n % 3][:, j * width:(j + 1) * width], ACT.Exp,
                                                        bias=negmax[:, n % 4, j:j + 1], accum_out=rsum[:, n % 4, j:j + 1])
                            op.then_inc(sems["exp_done"], 1)
                        elif kind == "moe":
                            if i == 0 and b == 0:
                                weights(act, s)
                            act.wait_ge(sems["scores_ready"], n + 1)
                            for j in range(2):
                                op = act.activation(HS[:, n % 3, j, :], score_bank[n % 3][:, j * S:(j + 1) * S], ACT.Silu,
                                                    bias=W(s, "gate_b")[:, 2 * i + j:2 * i + j + 1])
                            op.then_inc(sems["silu_done"], 1)
                        elif kind == "ffn":
                            act.wait_ge(sems["scores_ready"], n + 1)
                            for j in range(2):
                                op = act.activation(H[:, n % 3, j, :], score_bank[n % 3][:, j * S:(j + 1) * S], ACT.Silu,
                                                    bias=W(s, "fc1_b")[:, 2 * i + j:2 * i + j + 1])
                            op.then_inc(sems["silu_done"], 1)

                    def turned(n):
                        kind = plan.unit(n)[2]
                        if kind in STAGES["pt_act"]:
                            act.wait_ge(sems["second_ready"], plan.count("second", n))
                            m = plan.count("second", n) - 1
                            act.activation(PT[:, n % 2, :], second_of(n)[:, :], ACT.Copy).then_inc(sems["pt_act"], 1)

                    def outs(n):
                        s, i, kind, b = plan.unit(n)
                        if kind in ("h8", "h8r") and i < 3 or kind not in SOFTMAX:
                            return
                        act.wait_ge(sems["values_ready"], plan.count("values", n))
                        if kind == "mqa":
                            if i == 0 and b == 0:
                                weights(act, s)
                            op = act.activation(OT[:, s % 2, 4 * i:4 * i + 4, :], heads_view(value_bank[:, :], 4), ACT.Identity, bias=W(s, "bkv")[:, 1:2])
                        elif kind == "h8" and plan.layer(s).bias:
                            op = act.activation(OT[:, s % 2, 0, :], value_bank[:, 0:S], ACT.Identity, bias=W(s, "bv"))
                        elif kind == "h8r":
                            op = act.activation(OT[:, s % 2, 0, :], value_bank[:, 0:S], ACT.Copy)
                        elif kind == "h64c":
                            op = act.activation(OT[:, s % 2, 2 * i:2 * i + 2, :], heads_view(value_bank[:, 0:2 * S], 2), ACT.Copy)
                        else:
                            op = act.activation(OT[:, s % 2, i, :], value_bank[:, 0:S], ACT.Copy)
                        op.then_inc(sems["out_taken"], 1)

                    def route(s):
                        b = plan.steps[s][1]
                        act.wait_ge(sems["logits_ready"], routed(s))
                        act.activation(lexp[:, b, :], lg[:, b, :], ACT.Exp, bias=lmax[:, b:b + 1], accum_out=lsum[:, b:b + 1]).then_inc(sems["route_exp"], 1)

                    def after(half):
                        for what, s in plan.after.get(half, []):
                            if what == "turn":
                                take(s, "xT")

                    if last_loop:
                        act.activation(XT[:, :, :], state_t[:, bass.ds(it * G, G), :], ACT.Copy).then_inc(sems["state_in_act"], 1)
                    for n in plan.slots():
                        after(2 * n)
                        if 0 <= n + 2 < plan.n:
                            front(n + 2)
                        if 0 <= n < plan.n:
                            turned(n)
                        if 0 <= n - 1 < plan.n:
                            outs(n - 1)
                        after(2 * n + 1)
                        for s, name, eng in plan.early.get(n, []):
                            if eng == "act":
                                take(s, name)
                            if name == "router":
                                route(s)

                @block.vector
                def _(dve):
                    chain = [0]

                    def link(op):
                        chain[0] += 1
                        op.then_inc(sems["chain_dve"], 1)
                        dve.wait_ge(sems["chain_dve"], chain[0])

                    def take(s, name):
                        kind, b = plan.kind(s), plan.steps[s][1]
                        u = plan.at[s, name]
                        bank = proj_bank[u % N_PROJ]
                        dve.wait_ge(sems["proj_ready"], u + 1)
                        if kind == "mqa" and name != "kv":
                            half = int(name[1])
                            op = dve.tensor_tensor(Q8[:, s % 3, 4 * half:4 * half + 4, :], heads_view(bank[:, :], 4), qpe[:, 4 * half:4 * half + 4, :], ALU.add)
                        elif kind == "mqa":
                            dve.scalar_tensor_tensor(K8[:, s % 3, :], bank[:, 0:S], D ** -0.5, kpe[:, :], ALU.mult, ALU.add)
                            op = dve.tensor_copy(V8[:, s % 3, :], bank[:, S:2 * S])
                        elif name == "qk":
                            if b == 0:
                                weights(dve, s)
                            dve.tensor_tensor(QK[:, s % 2, :, :], heads_view(bank[:, 0:2 * S], 2), over(W(s, "cos"), 2), ALU.mult)
                            op = dve.tensor_tensor(RT2[:, s % 2, :, :], heads_view(bank[:, 2 * S:4 * S], 2), over(W(s, "sin"), 2), ALU.mult)
                        elif name == "v":
                            op = dve.tensor_tensor(Vm[:, s % 2, :, :], over(bank[:, 0:D], 4), value_pick, ALU.mult)
                        elif name == "router":
                            if b == 0:
                                weights(dve, s)
                            if kind == "lin":
                                op = dve.tensor_tensor(lg[:, b, :], bank[:, 0:NE], W(s, "bg"), ALU.add)
                            else:
                                op = dve.tensor_copy(lg[:, b, :], bank[:, 0:NE])
                        elif name == "biases":
                            state_ready(dve, s)
                            op = dve.tensor_tensor(R[:, b, :], bank[:, 0:D], X[:, b, :], ALU.add)
                        elif name[0] == "k":
                            i = int(name[1])
                            n = 4 if kind == "h64c" else 2
                            op = dve.tensor_copy(K64[:, s % 2, n * i:n * i + n, :], heads_view(bank[:, :], n))
                        elif name[0] == "v":
                            i = int(name[1])
                            op = dve.tensor_copy(V64[:, s % 2, i // 2, (i % 2) * 512:(i % 2 + 1) * 512], bank[:, :])
                        op.then_inc(sems["proj_by_dve"], 1)
                        if name == "qk":
                            after_reader(dve, s, name)
                            for j in range(4):
                                rows = slice(32 * j, 32 * j + 32)
                                dve.tensor_tensor(Km[rows, s % 2, j, :], QK[rows, s % 2, 1, :], RT2[rows, s % 2, 1, :], ALU.add)
                            dve.tensor_tensor(QK[:, s % 2, 0, :], QK[:, s % 2, 0, :], RT2[:, s % 2, 0, :], ALU.add).then_inc(sems["rope_ready"], 1)
                        if name == "router":
                            after_reader(dve, s, name)
                            dve.tensor_reduce(lmax[:, b:b + 1], lg[:, b, :], axis=AX.X, op=ALU.max, negate=True).then_inc(sems["logits_ready"], 1)
                            rank_experts(s)

                    def rank_experts(s):
                        b = plan.steps[s][1]
                        mine, other = along(lg[:, b, :], NE), over(lg[:, b, :], NE)
                        dve.tensor_tensor(beat[:, b, :, 0, :], other, mine, ALU.is_gt)
                        link(dve.tensor_tensor(beat[:, b, :, 1, :], other, mine, ALU.is_equal))
                        link(dve.tensor_tensor(beat[:, b, :, 1, :], beat[:, b, :, 1, :], lower, ALU.mult))
                        link(dve.tensor_reduce(rank[:, b, :], beat[:, b, :, :, :].rearrange("p i a j -> p i (a j)"), axis=AX.X, op=ALU.add))

                    def choose(s):
                        b, kind = plan.steps[s][1], plan.kind(s)
                        dve.wait_ge(sems["route_exp"], routed(s))
                        link(dve.scalar_tensor_tensor(pick[:, b, :], rank[:, b, :], 2.0, lexp[:, b, :], ALU.is_lt, ALU.mult))
                        link(dve.tensor_reduce(wsum[:, b:b + 1], pick[:, b, :], axis=AX.X, op=ALU.add))
                        if kind == "moe":
                            link(dve.scalar_tensor_tensor(wsum[:, b:b + 1], lsum[:, b:b + 1], 1e-9, wsum[:, b:b + 1], ALU.mult, ALU.add))
                        link(dve.reciprocal(winv[:, b:b + 1], wsum[:, b:b + 1]))
                        dve.tensor_scalar(gatew[:, b, :], pick[:, b, :], winv[:, b:b + 1], None, ALU.mult).then_inc(sems["route_ready"], 1)

                    def front(n):
                        s, i, kind, b = plan.unit(n)
                        bank = score_bank[n % 3]
                        if kind in STAGES["negmax"]:
                            heads = 2 if kind == "h64m" else 4
                            dve.wait_ge(sems["scores_ready"], n + 1)
                            dve.tensor_reduce(negmax[:, n % 4, 0:heads], heads_view(bank[:, :], heads), axis=AX.X, op=ALU.max, negate=True).then_inc(sems["negmax_ready"], 1)
                        elif kind == "h64c":
                            if i == 0 and b == 0:
                                dve.wait_ge(sems["keymask_ready"], 1)
                            dve.wait_ge(sems["scores_ready"], n + 1)
                            dve.scalar_tensor_tensor(heads_view(Pb[:, n % 3, :], 4), heads_view(bank[:, :], 4), -5.0, over(clip_hi[:, b, :], 4),
                                                     ALU.max, ALU.min).then_inc(sems["clip_done"], 1)
                        elif kind == "moe":
                            dve.wait_ge(sems["silu_done"], plan.count("silu", n))
                            for j in range(2):
                                op = dve.scalar_tensor_tensor(H[:, n % 3, j, :], bank[:, (2 + j) * S:(3 + j) * S], W(s, "up_b")[:, 2 * i + j:2 * i + j + 1],
                                                              HS[:, n % 3, j, :], ALU.add, ALU.mult)
                            op.then_inc(sems["gate_done"], 1)

                    def inverse(n):
                        s, i, kind, b = plan.unit(n)
                        if kind in SOFTMAX:
                            heads = 2 if kind == "h64m" else 4
                            dve.wait_ge(sems["exp_done"], plan.count("exp", n))
                            dve.reciprocal(rinv[:, n % 4, 0:heads], rsum[:, n % 4, 0:heads]).then_inc(sems["rsum_ready"], 1)

                    def back(n):
                        s, i, kind, b = plan.unit(n)
                        if kind in STAGES["pt_dve"]:
                            m = plan.count("second", n) - 1
                            dve.wait_ge(sems["second_ready"], m + 1)
                            dve.tensor_copy(PT[:, n % 2, :], second_of(n)[:, :]).then_inc(sems["pt_dve"], 1)
                        elif kind in STAGES["acc"]:
                            k = plan.count("acc", n)
                            if i == 0 and kind == "ffn":
                                dve.wait_ge(sems["acc_start"], 1 + sum(plan.kind(t) == "ffn" for t in range(s)))
                            elif i == 0:
                                after_reader(dve, s, "biases")
                            else:
                                dve.wait_ge(sems["acc_done"], k - 1)
                            if kind == "lin":
                                dve.wait_ge(sems["scores_ready"], n + 1)
                                for j in range(4):
                                    e = 4 * i + j
                                    op = dve.scalar_tensor_tensor(R[:, b, :], score_bank[n % 3][:, j * D:(j + 1) * D], gatew[:, b, e:e + 1], R[:, b, :], ALU.mult, ALU.add)
                                    if j < 3:
                                        link(op)
                            else:
                                m = plan.count("second", n) - 1
                                dve.wait_ge(sems["second_ready"], m + 1)
                                by = gatew[:, b, i:i + 1] if kind == "moe" else 0.5
                                op = dve.scalar_tensor_tensor(R[:, b, :], second_of(n)[:, 0:D], by, R[:, b, :], ALU.mult, ALU.add)
                            op.then_inc(sems["acc_done"], 1)

                    def add_and_stats(s):
                        b, kind = plan.steps[s][1], plan.kind(s)
                        if kind in SOFTMAX:
                            u = plan.at[s, "y"]
                            if plan.layer(s).out_bias:
                                dve.wait_ge(sems["resid_ready"], 1 + sum(plan.layer(t).out_bias for t in range(s)))
                            else:
                                state_ready(dve, s)
                            dve.wait_ge(sems["proj_ready"], u + 1)
                            dve.tensor_tensor(R[:, b, :], proj_bank[u % N_PROJ][:, 0:D], (XR if plan.layer(s).out_bias else X)[:, b, :], ALU.add).then_inc(sems["proj_by_dve"], 1)
                            after_reader(dve, s, "y")
                        else:
                            dve.wait_ge(sems["acc_done"], plan.count("acc", plan.last[s]))
                        link(dve.bn_stats(st6[:, b, :], R[:, b, :]))
                        link(dve.bn_aggr(mv[:, b, :], st6[:, b, :]))
                        dve.tensor_scalar(ve[:, b:b + 1], mv[:, b, 1:2], EPS, None, ALU.add).then_inc(sems["var_ready"], 1)

                    def normalise(s):
                        b = plan.steps[s][1]
                        dve.wait_ge(sems["rstd_ready"], s + 1)
                        to = X[:, b, :]
                        if plan.next_kind(s) is None and not last_loop:
                            to = state[:, bass.ds(it * G + b, 1), :].rearrange("p a d -> p (a d)")
                        dve.tensor_scalar(to, R[:, b, :], mv[:, b, 0:1], rstd[:, b:b + 1], ALU.subtract, ALU.mult).then_inc(sems["x_ready"], 1)
                        if plan.affine_next(s):
                            dve.wait_ge(sems["x_ready"], s + 1)
                            link(dve.bn_stats(st6b[:, b, :], X[:, b, :]))
                            link(dve.bn_aggr(mv2[:, b, :], st6b[:, b, :]))
                            dve.tensor_scalar(ve2[:, b:b + 1], mv2[:, b, 1:2], EPS, None, ALU.add).then_inc(sems["stat2_ready"], 1)

                    def normalise_again(s):
                        b = plan.steps[s][1]
                        dve.wait_ge(sems["rstd2_ready"], 1 + sum(plan.affine_next(t) for t in range(s)))
                        dve.tensor_scalar(LH[:, b, :], X[:, b, :], mv2[:, b, 0:1], rstd2[:, b:b + 1], ALU.subtract, ALU.mult).then_inc(sems["norm2_ready"], 1)

                    def after(half):
                        for what, s in plan.after.get(half, []):
                            if what == "output":
                                add_and_stats(s)
                            if what == "normalise":
                                normalise(s)
                            if what == "normalise_again":
                                normalise_again(s)

                    if last_loop:
                        dve.tensor_copy(X[:, :, :], state[:, bass.ds(it * G, G), :]).then_inc(sems["state_in_dve"], 1)
                        dve.wait_ge(sems["ctx_in"], 16)
                        for b in range(G):
                            op = dve.bn_stats(st6b[:, b, :], CX[:, b, :])
                        link(op)
                        for b in range(G):
                            op = dve.bn_aggr(mv2[:, b, :], st6b[:, b, :])
                        link(op)
                        dve.tensor_scalar(ve2[:, :], mv2[:, :, 1], EPS, None, ALU.add).then_inc(sems["ctx_stats"], 1)
                        dve.wait_ge(sems["mask_in"], 16)
                        for j in range(2):
                            dve.tensor_scalar(key_mask[:, :, j, 0, :], mask_u8[:, :, :], -NEG, NEG, ALU.mult, ALU.add)
                            op = dve.memset(key_mask[:, :, j, 1, :], 0.0)
                        op.then_inc(sems["keymask_ready"], 1)
                        dve.wait_ge(sems["ctx_rstd"], 1)
                        for b in range(G):
                            op = dve.tensor_scalar(CX[:, b, :], CX[:, b, :], mv2[:, b, 0:1], rstd2[:, b:b + 1], ALU.subtract, ALU.mult)
                        op.then_inc(sems["ctx_norm"], 1)
                    else:
                        dve.wait_ge(sems["mask_in"], 16)
                        dve.tensor_scalar(clip_hi[:, :, :], mask_u8[:, :, :], 10.0, -5.0, ALU.mult, ALU.add).then_inc(sems["keymask_ready"], 1)
                    for n in plan.slots():
                        for s, name, _ in plan.early.get(n - 1, []):
                            if name == "router":
                                choose(s)
                        after(2 * n)
                        if 0 <= n + 2 < plan.n:
                            front(n + 2)
                        if 0 <= n + 1 < plan.n:
                            inverse(n + 1)
                        if 0 <= n < plan.n:
                            back(n)
                        after(2 * n + 1)
                        for s, name, eng in plan.early.get(n, []):
                            if eng == "dve":
                                take(s, name)

                @block.gpsimd
                def _(pool):
                    chain = [0]

                    def link(op):
                        chain[0] += 1
                        op.then_inc(sems["chain_pool"], 1)
                        pool.wait_ge(sems["chain_pool"], chain[0])

                    def spread(s):
                        if plan.kind(s) == "h8r":
                            pool.wait_ge(sems["rope_ready"], 1 + sum(plan.kind(t) == "h8r" for t in range(s)))
                        else:
                            after_reader(pool, s, "qk")
                        pool.tensor_tensor(Qg[:, s % 2, :, :], over(QK[:, s % 2, 0, :], 4), along(head_scale, S), ALU.mult).then_inc(sems["masked"], 1)

                    def residual(s):
                        b = plan.steps[s][1]
                        if b == 0:
                            weights(pool, s)
                        state_ready(pool, s)
                        pool.tensor_tensor(XR[:, b, :], X[:, b, :], W(s, "bo"), ALU.add).then_inc(sems["resid_ready"], 1)

                    def start_sum(s):
                        b = plan.steps[s][1]
                        state_ready(pool, s)
                        link(pool.tensor_tensor(R[:, b, :], X[:, b, :], half_b2[:, :], ALU.add))
                        pool.tensor_tensor(R[:, b, :], R[:, b, :], X[:, b, :], ALU.add).then_inc(sems["acc_start"], 1)

                    def probabilities(n):
                        s, i, kind, b = plan.unit(n)
                        if kind in SOFTMAX:
                            heads = 2 if kind == "h64m" else 4
                            pool.wait_ge(sems["rsum_ready"], plan.count("norm", n))
                            p = heads_view(Pb[:, n % 3, :], heads)
                            pool.tensor_tensor(p, p, along(rinv[:, n % 4, 0:heads], 512 // heads), ALU.mult).then_inc(sems["norm_done"], 1)

                    def after(half):
                        for what, s in plan.after.get(half, []):
                            b = plan.steps[s][1]
                            if what == "output":
                                pool.wait_ge(sems["var_ready"], s + 1)
                                pool.tensor_tensor(rstd[:, b:b + 1], ve[:, b:b + 1], neg_half[:, 0:1], ALU.pow).then_inc(sems["rstd_ready"], 1)
                            if what == "normalise" and plan.affine_next(s):
                                pool.wait_ge(sems["stat2_ready"], 1 + sum(plan.affine_next(t) for t in range(s)))
                                pool.tensor_tensor(rstd2[:, b:b + 1], ve2[:, b:b + 1], neg_half[:, 0:1], ALU.pow).then_inc(sems["rstd2_ready"], 1)

                    if last_loop:
                        pool.wait_ge(sems["ctx_stats"], 1)
                        pool.tensor_tensor(rstd2[:, :], ve2[:, :], neg_half[:, :], ALU.pow).then_inc(sems["ctx_rstd"], 1)
                    for n in plan.slots():
                        after(2 * n)
                        for s in range(len(plan.steps)):
                            if plan.first[s] - 2 == n:
                                if plan.layer(s).out_bias:
                                    residual(s)
                                if plan.kind(s) == "ffn":
                                    start_sum(s)
                        if 0 <= n + 1 < plan.n:
                            probabilities(n + 1)
                        after(2 * n + 1)
                        for s, name, _ in plan.early.get(n - 1, []):
                            if name == "qk":
                                spread(s)

            nc.all_engine_barrier(sems_to_clear=body_range)
            iters.__exit__(None, None, None)

        a_names = ["const"] + [layer.name for layer in LOOP_A]
        with ExitStack() as scope:
            w = {}
            for layer in LOOP_A:
                w[layer.name] = sb("w_" + layer.name, [P, sum(n for _, n in cols[layer.name].values())], scope=scope)
            qpe = sb("qpe", [P, 8, S], scope=scope)
            kpe = sb("kpe", [P, S], scope=scope)
            with nc.Block() as block:
                @block.sync
                def _(sp):
                    sp.dma_start(const[:, :], dram["const"]).then_inc(w_in["const"], 16)
                    for layer in LOOP_A:
                        sp.dma_start(w[layer.name][:, :], dram[layer.name]).then_inc(w_in[layer.name], 16)

                @block.vector
                def _(dve):
                    dve.wait_ge(w_in["const"], 16)
                    dve.tensor_copy(ident_b[:, :], ident)
                    dve.tensor_copy(causal_b[:, :, :], over(part(const, "const", "causal"), 4))

                @block.gpsimd
                def _(pool):
                    pool.memset(neg_half[:, :], -0.5)
                    pool.wait_ge(w_in["const"], 16)
                    pool.wait_ge(w_in["L0_attn"], 16)
                    pe_t = part(const, "const", "pe")
                    pool.tensor_tensor(qpe[:, :, :], over(pe_t, 8), along(part(w["L0_attn"], "L0_attn", "bq"), S), ALU.add)
                    pool.tensor_scalar(kpe[:, :], pe_t, part(w["L0_attn"], "L0_attn", "bkv")[:, 0:1], D ** -0.5, ALU.add, ALU.mult)
            run_loop("a_", Plan(LOOP_A), w, scope, False)

        with ExitStack() as scope:
            w = {}
            for layer in LOOP_C:
                w[layer.name] = sb("w_" + layer.name, [P, sum(n for _, n in cols[layer.name].values())], scope=scope)
            q_in = sem("q_in")
            fc1_q = sb("fc1_q", [P, 512], I32, scope=scope)
            fc2_q = sb("fc2_q", [P, 512], I32, scope=scope)
            fc1 = sb("fc1", [P, 512], scope=scope)
            fc2 = sb("fc2", [P, 4, D], scope=scope)
            half_b2 = sb("half_b2", [P, D], scope=scope)
            state_t = sb("state_t", [P, B, S], scope=scope)
            with ExitStack() as own:
                quantised_ffn(nc, sb, sem, own, w, w_in, dram, cols, state, state_t, ident, neg_half,
                              score_bank + [second_bank, value_bank] + proj_bank, q_in, fc1_q, fc2_q)
            with nc.Block() as block:
                @block.vector
                def _(dve):
                    dve.wait_ge(w_in["L3_ffn"], 16)
                    dve.wait_ge(q_in, 32)
                    ffn = w["L3_ffn"]
                    dve.scalar_tensor_tensor(fc1[:, :], fc1_q[:, :], -128.0, part(ffn, "L3_ffn", "fc1_s"), ALU.add, ALU.mult)
                    dve.scalar_tensor_tensor(fc2[:, :, :].rearrange("p c d -> p (c d)"), fc2_q[:, :], -128.0, part(ffn, "L3_ffn", "fc2_s"), ALU.add, ALU.mult)
                    dve.tensor_scalar(half_b2[:, :], part(ffn, "L3_ffn", "fc2_b"), 0.5, None, ALU.mult)
            run_loop("c_", Plan(LOOP_C), w, scope, True, state_t)


def rope_tables():
    f = np.float32
    pos = np.arange(S, dtype=f)
    freq2 = (f(1.0) / f(10000.0) ** (np.arange(0, 8, 2, dtype=f) / f(8))).astype(f)
    freq3 = (f(10000.0) ** (-np.arange(0, 8, 2, dtype=f) / f(8))).astype(f)
    a2 = (freq2[np.arange(8) % 4][:, None] * pos[None, :]).astype(f)
    a3 = (freq3[np.arange(8) // 2][:, None] * pos[None, :]).astype(f)
    sign2 = np.where(np.arange(8) < 4, -1, 1).astype(f)[:, None]
    sign3 = np.where(np.arange(8) % 2 == 0, -1, 1).astype(f)[:, None]
    rows = lambda a: np.tile(a.astype(f), (16, 1))
    return rows(np.cos(a2)), rows(np.sin(a2) * sign2), rows(np.cos(a3)), rows(np.sin(a3) * sign3)


def constants():
    f = np.float32
    p = np.arange(P)
    pick = (p[:, None] % 32 // 8 == np.arange(4)[None, :]).astype(f)
    group = np.where(pick > 0, f(1.0 / np.sqrt(f(8.0))), f(0))
    vpick = np.broadcast_to(pick.T.reshape(1, 4 * P), (P, 4 * P))
    lower = np.broadcast_to(np.tril(np.ones((NE, NE), f), -1).reshape(1, NE * NE), (P, NE * NE))
    causal = np.where(np.tril(np.ones((S, S), bool)), 0, NEG).astype(f)
    pos = np.arange(S, dtype=f)[:, None]
    ang = pos * np.exp(f(-np.log(10000.0)) * np.arange(0, D, 2, dtype=f) / f(D))[None, :]
    pe = np.zeros((S, D), f)
    pe[:, 0::2], pe[:, 1::2] = np.sin(ang), np.cos(ang)
    return [("ident", np.eye(P, dtype=f)), ("group", group), ("vpick", vpick), ("lower", lower), ("causal", causal), ("pe", pe.T)]


def laid_out(i):
    def column(v):
        return v.reshape(-1, P).T

    def row(v):
        return np.broadcast_to(v.reshape(1, -1), (P, v.size))

    def chunks(m):
        return m.reshape(-1, P, m.shape[1]).transpose(1, 0, 2).reshape(P, -1)

    def rows_below(m):
        return np.concatenate([m, np.zeros((P - m.shape[0], m.shape[1]), m.dtype)], axis=0)

    def padded(m, n):
        return np.concatenate([m, np.zeros((P, n - m.shape[1]), m.dtype)], axis=1)

    cos2, sin2, cos3, sin3 = rope_tables()
    d = np.arange(P)
    turn2, turn3 = d // 8 * 8 + (d % 8 + 4) % 8, d ^ 1
    rel = np.arange(WINDOW)[:, None] - np.arange(WINDOW)[None, :] + WINDOW - 1
    relpos = np.full((S, 16, S), NEG, np.float32)
    for k in range(0, S, WINDOW):
        relpos[k:k + WINDOW, :, k:k + WINDOW] = i["L1_attn_rel_bias"][rel].transpose(0, 2, 1)
    packs = {"const": constants()}
    packs["L0_attn"] = [("Wq", i["L0_attn_Wq"]), ("Wkv", i["L0_attn_Wkv"]), ("Wo", chunks(i["L0_attn_Wo"])),
                        ("bq", column(i["L0_attn_bq"])), ("bkv", column(i["L0_attn_bkv"]))]
    for n in ("L0_xattn", "L1_xattn"):
        packs[n] = [(k, i[f"{n}_{k}"]) for k in ("Wq", "Wk", "Wv", "Wo")] + [(k, column(i[f"{n}_{k}"])) for k in ("bq", "bk", "bv")] + [("bo", row(i[f"{n}_bo"]))]
    packs["L0_ffn"] = [("Wr", padded(i["L0_ffn_router_w"].T, 64)),
                       ("gate_w", i["L0_ffn_gate_w"].transpose(1, 0, 2).reshape(P, -1)), ("up_w", i["L0_ffn_up_w"].transpose(1, 0, 2).reshape(P, -1)),
                       ("down_w", chunks(i["L0_ffn_down_w"].reshape(-1, D))),
                       ("gate_b", column(i["L0_ffn_gate_b"].reshape(-1))), ("up_b", column(i["L0_ffn_up_b"].reshape(-1))), ("be", rows_below(i["L0_ffn_down_b"]))]
    qkv, qkv_b = i["L1_attn_qkv_w"], i["L1_attn_qkv_b"]
    packs["L1_attn"] = [("Wq", qkv[:, 0:D]), ("Wk", qkv[:, D:2 * D]), ("Wv", qkv[:, 2 * D:]), ("Wo", i["L1_attn_proj_w"]),
                        ("bq", column(qkv_b[0:D])), ("bk", column(qkv_b[D:2 * D])), ("bv", column(qkv_b[2 * D:])), ("bo", row(i["L1_attn_proj_b"])),
                        ("relpos", relpos.reshape(P, 4, 4, S).transpose(0, 2, 1, 3).reshape(P, -1))]
    packs["L1_ffn"] = [("Wr", padded(i["L1_ffn_Wg"], 64)), ("We", i["L1_ffn_We"].transpose(1, 0, 2).reshape(P, -1)), ("be", rows_below(i["L1_ffn_be"])), ("bg", row(i["L1_ffn_bg"]))]
    for n, turned, q, c, s in (("L2_attn", turn2, "W_", cos2, sin2), ("L3_attn", turn3, "W", cos3, sin3)):
        wq, wk, wv, wo = (i[f"{n}_{q}{k}"].T for k in (("Q", "K", "V", "O") if q == "W_" else ("q", "k", "v", "o")))
        packs[n] = [("Wq", wq), ("Wk", wk), ("Wv", wv), ("Wo", wo), ("Wq_turned", wq[:, turned]), ("Wk_turned", wk[:, turned]), ("cos", c), ("sin", s)]
    packs["L2_xattn"] = [("Wq", i["L2_xattn_Wq"]), ("Wk", i["L2_xattn_Wkv"][:, :1024]), ("Wv", i["L2_xattn_Wkv"][:, 1024:]), ("Wo", chunks(i["L2_xattn_Wo"])),
                         ("bo", row(i["L2_xattn_bo"]))]
    packs["L2_ffn"] = [("gate", chunks(i["L2_ffn_w_gate"])), ("up", chunks(i["L2_ffn_w_up"])), ("down", i["L2_ffn_w_down"])]
    packs["L3_xattn"] = [("Wq", i["L3_xattn_Wq"]), ("Wk", i["L3_xattn_Wkv"][:, :1024]), ("Wv", i["L3_xattn_Wkv"][:, 1024:]), ("Wo", chunks(i["L3_xattn_Wout"]))] + [
        (k, column(i[f"L3_xattn_{k}"])) for k in ("g1", "b1", "g2", "b2")]
    packs["L3_ffn"] = [("gamma", column(i["L3_ffn_ln_gamma"])), ("beta", column(i["L3_ffn_ln_beta"])), ("fc1_s", row(i["L3_ffn_fc1_scales"])),
                       ("fc1_b", column(i["L3_ffn_fc1_bias"])), ("fc2_s", row(i["L3_ffn_fc2_scales"])), ("fc2_b", row(i["L3_ffn_fc2_bias"]))]
    return packs


def kernel(**inputs):
    import concourse.bacc as bacc
    from concourse.bass_utils import run_bass_kernel_spmd

    i = {k: np.asarray(v) for k, v in inputs.items()}
    packs = laid_out(i)
    arrays, cols = {}, {}
    for name, parts in packs.items():
        cols[name], at = {}, 0
        for k, a in parts:
            cols[name][k] = (at, a.shape[1])
            at += a.shape[1]
        arrays[name] = np.ascontiguousarray(np.concatenate([a for _, a in parts], axis=1))
    tokens = lambda a: np.ascontiguousarray(a.reshape(NIT, G, S, D).transpose(0, 2, 1, 3).reshape(NIT, P, G * D))
    widths = lambda a: np.ascontiguousarray(a.reshape(NIT, G, S, D).transpose(0, 3, 1, 2).reshape(NIT, P, G * S))
    arrays["x"], arrays["xT"] = tokens(i["x"]), widths(i["x"])
    arrays["ctx"], arrays["ctxT"] = tokens(i["ctx_1024"]), widths(i["ctx_1024"])
    for k in ("bk0", "bk1"):
        arrays["mask_" + k] = np.ascontiguousarray(i["mask_BxS2_" + k]).reshape(NIT, G * S)
    arrays["fc1_q"] = np.ascontiguousarray(i["L3_ffn_fc1_q"])
    arrays["fc2_q"] = np.ascontiguousarray(i["L3_ffn_fc2_q"].reshape(4, P, D).transpose(1, 0, 2).reshape(P, 4 * D))

    nc = bacc.Bacc("TRN2", target_bir_lowering=False, num_devices=1)
    dram, feed = {}, {}
    for name, a in arrays.items():
        dram[name] = nc.dram_tensor("in_" + name, a.shape, mybir.dt.from_np(a.dtype), kind="ExternalInput").ap()
        feed["in_" + name] = a
    out = nc.dram_tensor("out", (B, S, D), F32, kind="ExternalOutput").ap()
    decoder_kernel(nc, dram, out, cols)
    r = run_bass_kernel_spmd(nc, [feed], core_ids=[0])
    return r.results[0]["out"]
```

```python
from contextlib import ExitStack

import numpy as np

import concourse.bass as bass
from concourse import mybir

F32 = mybir.dt.float32
BF16 = mybir.dt.bfloat16
I32 = mybir.dt.int32
U8 = mybir.dt.uint8
ALU = mybir.AluOpType
ACT = mybir.ActivationFunctionType
AX = mybir.AxisListType

B, S, D = 16, 128, 128
G = 8
NIT = B // G
P = 128
EPS = 1e-5
NEG = -1e30
MAGIC = 1.5 * 2.0 ** 23
NE = 8
N_PROJ = 3
CTX_SLOT = 6
AHEAD = 3
WINDOW = 64

EARLY = {
    "mqa": [("q0", 6, "dve"), ("q1", 6, "dve"), ("kv", 5, "dve")],
    "h8": [("qk", 8, "act"), ("v", 4, "dve")],
    "h8p": [("qk", 8, "act"), ("v", 4, "dve")],
    "h8r": [("qk", 8, "dve"), ("v", 4, "dve")],
    "moe": [("router", 24, "dve"), ("gateT", 6, "act"), ("biases", 5, "dve")],
    "lin": [("router", 24, "dve"), ("gateT", 6, "act"), ("biases", 5, "dve")],
    "h64c": [("q0", 7, "act"), ("q1", 7, "act"), ("k0", 6, "dve"), ("k1", 6, "dve"), ("v0", 4, "act"), ("v1", 4, "dve")],
    "h64m": [("c", 10, "act"), ("q0", 9, "act"), ("q1", 9, "dve"), ("q2", 8, "act"), ("q3", 8, "dve"),
             ("v0", 5, "act"), ("v1", 5, "dve"), ("v2", 4, "act"), ("v3", 4, "dve")],
    "ffn": [],
}
UNITS = {"mqa": 2, "h8": 4, "h8p": 4, "h8r": 4, "moe": 8, "lin": 2, "h64c": 4, "h64m": 8, "ffn": 2}
H8 = ("h8", "h8p", "h8r")
SOFTMAX = ("mqa", "h64m", "h64c") + H8
STAGES = {
    "scores": tuple(k for k in UNITS if k != "lin"),
    "negmax": ("mqa", "h64m") + H8,
    "moved": ("h64c", "h64m", "h8p"),
    "exp": SOFTMAX,
    "norm": SOFTMAX,
    "silu": ("moe", "ffn"),
    "gate": ("moe",),
    "second": SOFTMAX + ("moe", "lin", "ffn"),
    "acc": ("moe", "lin", "ffn"),
    "values": SOFTMAX,
}


PT_ACT = {"h8": (3,), "h8p": (2,), "h8r": (1, 3)}


class Layer:
    def __init__(self, name, kind, mask=None, ctx=False, bias=False, out_bias=False):
        self.name, self.kind, self.mask, self.ctx, self.bias, self.out_bias = name, kind, mask, ctx, bias, out_bias


LOOP_A = [
    Layer("L0_attn", "mqa", mask="causal"),
    Layer("L0_xattn", "h8", mask="causal", ctx=True, bias=True, out_bias=True),
    Layer("L0_ffn", "moe"),
    Layer("L1_attn", "h8p", mask="relpos", bias=True, out_bias=True),
    Layer("L1_xattn", "h8", ctx=True, bias=True, out_bias=True),
    Layer("L1_ffn", "lin"),
    Layer("L2_attn", "h8r", mask="causal"),
    Layer("L2_xattn", "h64c", ctx=True, out_bias=True),
]
LOOP_C = [
    Layer("L3_attn", "h8r", mask="causal"),
    Layer("L3_xattn", "h64m", mask="keys"),
    Layer("L3_ffn", "ffn"),
]


class Plan:

    def __init__(self, layers):
        self.layers = layers
        self.steps = [(L, b) for L in range(len(layers)) for b in range(G)]
        self.before = {s: self.steps.index((L - 1, b)) for s, (L, b) in enumerate(self.steps) if L}
        self.units, self.first, self.last = [], [], []
        for s, (L, b) in enumerate(self.steps):
            self.first.append(len(self.units))
            self.units += [(s, i) for i in range(UNITS[layers[L].kind])]
            self.last.append(len(self.units) - 1)
        self.n = len(self.units)
        self.spread = {}
        self.choice = {}
        self.early, self.after = {}, {}
        for s in range(len(self.steps)):
            for name, ahead, eng in EARLY[self.kind(s)]:
                made = self.last[self.before[s]] + dict(self.rest(self.before[s]))["turn"] // 2 if s in self.before else -8
                if name in ("gateT", "biases"):
                    made += 2 + (name == "biases")
                self.early.setdefault(max(self.first[s] - ahead, made), []).append((s, name, eng))
                if name == "qk":
                    at = max(self.first[s] - ahead, made)
                    self.spread.setdefault(max(at, min(at + 1, self.first[s] - AHEAD - 1)), []).append(s)
                if name == "gateT":
                    self.choice.setdefault(max(self.first[s] - ahead, made) - 2, []).append(s)
            for what, half in self.rest(s):
                self.after.setdefault(2 * self.last[s] + half, []).append((what, s))
        self.uses = []
        for n in self.slots():
            for half in (0, 1):
                for what, s in self.after.get(2 * n + half, []):
                    if what == "output" and self.kind(s) in SOFTMAX:
                        self.uses.append((s, "y", "dve"))
                    if what == "turn":
                        self.uses.append((s, "xT", "act"))
            self.uses += self.early.get(n, [])
        normalised = [(half, s) for half in self.after for what, s in self.after[half] if what == "normalise"]
        assert sorted(normalised) == sorted(normalised, key=lambda x: x[1])
        self.at = {(s, name): u for u, (s, name, _) in enumerate(self.uses)}

    def ring(self, s, n):
        return sum(self.kind(t) in SOFTMAX for t in range(s)) % n

    def layer(self, s):
        return self.layers[self.steps[s][0]]

    def kind(self, s):
        return self.layer(s).kind

    def next_kind(self, s):
        L = self.steps[s][0] + 1
        return self.layers[L].kind if L < len(self.layers) else None

    def affine_next(self, s):
        return self.next_kind(s) in ("h64m", "ffn")

    def rest(self, s):
        after = {before: first for first, before in self.before.items()}
        gap = self.first[after[s]] - self.last[s] if s in after else 0
        tight = gap < 13
        if tight:
            late = min(max(gap - (10 if self.next_kind(s) in H8 else 7), 0), 3)
            parts = [("output", 4 + late), ("normalise", 6 + late)]
        elif self.kind(s) not in SOFTMAX:
            parts = [("output", 6), ("normalise", 9)]
        elif self.affine_next(s):
            parts = [("output", 7), ("normalise", 9)]
        else:
            parts = [("output", 7), ("normalise", 10)]
        at = parts[-1][1]
        if self.affine_next(s):
            at += 2
            parts.append(("normalise_again", at))
        if self.next_kind(s):
            parts.append(("turn", at + (late if tight else 2)))
        return parts

    def slots(self):
        return range(-10, self.n + 7)

    def unit(self, n):
        s, i = self.units[n]
        return s, i, self.kind(s), self.steps[s][1]

    def count(self, stage, n):
        if stage in ("pt_act", "pt_dve"):
            return sum(self.copier(k) == stage for k in range(n + 1))
        return sum(self.kind(s) in STAGES[stage] for s, _ in self.units[:n + 1])

    def copier(self, n):
        s, i = self.units[n]
        if self.kind(s) not in SOFTMAX:
            return None
        return "pt_act" if self.kind(s) == "h64m" or i in PT_ACT.get(self.kind(s), ()) else "pt_dve"

    def used_by(self, eng, u):
        return sum(e == eng for _, _, e in self.uses[:u + 1])


def heads_view(ap, n):
    return ap.rearrange("p (n k) -> p n k", n=n)


def over(ap, n):
    return ap.unsqueeze(1).to_broadcast([ap.shape[0], n, ap.shape[1]])


def along(ap, n):
    return ap.unsqueeze(2).to_broadcast([ap.shape[0], ap.shape[1], n])


def quantised_ffn(nc, sb, sem, scope, w, w_in, dram, cols, state, state_t, ident, neg_half, banks, q_in, fc1_q, fc2_q):
    NT, FC = B * S, 3
    QMAX = 32767.0
    wq = sb("wq", [P, 9, D], scope=scope)
    wr = sb("wr", [P, 9, D], scope=scope)
    wt = sb("wt", [P, 9, D], scope=scope)
    bmax = sb("bmax", [P, 36], scope=scope)
    bscale = sb("bscale", [P, 36], scope=scope)
    binv = sb("binv", [P, 36], scope=scope)
    xq = sb("xq", [P, B, D], scope=scope)
    xqt = sb("xqt", [P, NT], scope=scope)
    hid = sb("hid", [P, 2 * FC, NT], scope=scope)
    sig = sb("sig", [P, FC, NT], scope=scope)
    cmax = sb("cmax", [P, 5, 12], scope=scope)
    pmax = sb("pmax", [P, 5], scope=scope)
    gmax = sb("gmax", [P, 5], scope=scope)
    scl = sb("scl", [P, 5], scope=scope)
    inv = sb("inv", [P, 5], scope=scope)
    prod_by = sb("prod_by", [P, 1], scope=scope)
    magic = sb("magic", [P, 1], scope=scope)
    R = sb("b_r", [P, B, D], scope=scope)
    st6 = sb("b_st6", [P, B, 6], scope=scope)
    mv = sb("b_mv", [P, B, 2], scope=scope)
    ve = sb("b_ve", [P, B], scope=scope)
    rstd = sb("b_rstd", [P, B], scope=scope)
    X_, GATE, UP, GATED, PROD = range(5)

    chain_dve, wq_ready, max_part, max_all, scale_ready, xq_ready = (sem("b_" + n) for n in ("chain", "wq_ready", "max_part", "max_all", "scale_ready", "xq_ready"))
    bank_full, bank_taken, down_taken, gate_ready, sig_ready, up_ready, up_rounded, gated_rounded, prod_rounded, prod_ready, var_ready, rstd_ready, x_ready = (
        sem("b_" + n) for n in ("bank_full", "bank_taken", "down_taken", "gate_ready", "sig_ready", "up_ready", "up_rounded", "gated_rounded", "prod_rounded", "prod_ready", "var_ready",
                                "rstd_ready", "x_ready"))
    N_W, N_X, N_H = 3, 4, 24

    with nc.Block() as block:
        @block.sync
        def _(sp):
            sp.dma_start(wq[:, :, :].rearrange("p c d -> p (c d)"), dram["L2_ffn"]).then_inc(w_in["L2_ffn"], 16)
            for layer in LOOP_C:
                sp.dma_start(w[layer.name][:, :], dram[layer.name]).then_inc(w_in[layer.name], 16)
            sp.dma_start(fc1_q[:, :], dram["fc1_q"]).then_inc(q_in, 16)
            sp.dma_start(fc2_q[:, :], dram["fc2_q"]).then_inc(q_in, 16)

        @block.vector
        def _(dve):
            done = [0]

            def link(op):
                done[0] += 1
                op.then_inc(chain_dve, 1)
                dve.wait_ge(chain_dve, done[0])

            def scale(k):
                dve.wait_ge(max_all, k + 1)
                link(dve.tensor_scalar(scl[:, k:k + 1], gmax[:, k:k + 1], 1.0 / QMAX, 1e-12, ALU.mult, ALU.max))
                op = dve.reciprocal(inv[:, k:k + 1], scl[:, k:k + 1])
                if k == PROD:
                    link(op)
                    op = dve.tensor_tensor(prod_by[:, :], scl[:, GATED:GATED + 1], inv[:, k:k + 1], ALU.mult)
                op.then_inc(scale_ready, 1)
                dve.wait_ge(scale_ready, k + 1)

            def quantise(to, of, k):
                link(dve.tensor_scalar(to, of, inv[:, k:k + 1], MAGIC, ALU.mult, ALU.add))
                return dve.tensor_scalar(to, to, -MAGIC, scl[:, k:k + 1], ALU.add, ALU.mult)

            def absmax(to, of):
                return dve.tensor_reduce(to, of, axis=AX.X, op=ALU.max, apply_absolute_value=True)

            dve.memset(magic[:, :], MAGIC)
            absmax(pmax[:, X_:X_ + 1], state[:, :, :].rearrange("p b d -> p (b d)")).then_inc(max_part, 1)
            dve.wait_ge(w_in["L2_ffn"], 16)
            blocks = wq[:, :, :].rearrange("p c (n k) -> p (c n) k", k=32)
            rounded = wr[:, :, :].rearrange("p c (n k) -> p (c n) k", k=32)
            link(absmax(bmax[:, :], blocks))
            link(dve.tensor_scalar(bscale[:, :], bmax[:, :], 1.0 / 7.0, 1e-12, ALU.mult, ALU.max))
            link(dve.reciprocal(binv[:, :], bscale[:, :]))
            link(dve.tensor_tensor(rounded, blocks, along(binv[:, :], 32), ALU.mult))
            link(dve.tensor_scalar(rounded, rounded, MAGIC, -MAGIC, ALU.add, ALU.add))
            dve.tensor_tensor(rounded, rounded, along(bscale[:, :], 32), ALU.mult).then_inc(wq_ready, 1)
            scale(X_)
            for t in range(N_X):
                four = slice(4 * t, 4 * t + 4)
                quantise(xq[:, four, :], state[:, four, :], X_).then_inc(xq_ready, 1)

            def chunk_max(k):
                dve.wait_ge(bank_taken, N_W + N_X + k + 1)
                op = absmax(cmax[:, GATE + k // 12, k % 12:k % 12 + 1], hid[:, k // 4, (k % 4) * 512:(k % 4 + 1) * 512])
                if k % 12 == 11:
                    link(op)
                    g = GATE + k // 12
                    absmax(pmax[:, g:g + 1], cmax[:, g, :]).then_inc(max_part, 1)

            for k in range(16):
                chunk_max(k)
            scale(GATE)
            for c in range(FC):
                quantise(hid[:, c, :], hid[:, c, :], GATE).then_inc(gate_ready, 1)
                if c < 2:
                    for k in range(16 + 4 * c, 20 + 4 * c):
                        chunk_max(k)
            for c in range(FC):
                dve.wait_ge(sig_ready, c + 1)
                link(dve.tensor_scalar(sig[:, c, :], sig[:, c, :], 65535.0 / 65536.0, 192.0, ALU.min, ALU.add))
                link(dve.scalar_tensor_tensor(hid[:, c, :], sig[:, c, :], -192.0, hid[:, c, :], ALU.add, ALU.mult))
                op = absmax(cmax[:, GATED, c:c + 1], hid[:, c, :])
                if c == 0:
                    scale(UP)
            link(op)
            absmax(pmax[:, GATED:GATED + 1], cmax[:, GATED, 0:FC]).then_inc(max_part, 1)
            scale(GATED)
            for c in range(FC):
                dve.wait_ge(gated_rounded, c + 1)
                dve.wait_ge(up_ready, c + 1)
                link(dve.scalar_tensor_tensor(hid[:, c, :], hid[:, c, :], -MAGIC, hid[:, FC + c, :], ALU.add, ALU.mult))
                op = absmax(cmax[:, PROD, c:c + 1], hid[:, c, :])
            link(op)
            link(absmax(pmax[:, PROD:PROD + 1], cmax[:, PROD, 0:FC]))
            dve.tensor_tensor(pmax[:, PROD:PROD + 1], pmax[:, PROD:PROD + 1], scl[:, GATED:GATED + 1], ALU.mult).then_inc(max_part, 1)
            scale(PROD)
            for c in range(FC):
                dve.wait_ge(prod_rounded, c + 1)
                dve.tensor_scalar(hid[:, c, :], hid[:, c, :], -MAGIC, scl[:, PROD:PROD + 1], ALU.add, ALU.mult).then_inc(prod_ready, 1)
            def stats(g):
                u = N_W + N_X + N_H + g
                dve.wait_ge(bank_full, u + 1)
                sl = slice(4 * g, 4 * g + 4)
                dve.tensor_tensor(R[:, sl, :], heads_view(banks[u % 8][:, :], 4), state[:, sl, :], ALU.add).then_inc(down_taken, 1)
                dve.wait_ge(down_taken, g + 1)
                for b in range(4 * g, 4 * g + 4):
                    op = dve.bn_stats(st6[:, b, :], R[:, b, :])
                link(op)
                for b in range(4 * g, 4 * g + 4):
                    op = dve.bn_aggr(mv[:, b, :], st6[:, b, :])
                link(op)
                dve.tensor_scalar(ve[:, sl], mv[:, sl, 1], EPS, None, ALU.add).then_inc(var_ready, 1)

            def normalise(g):
                dve.wait_ge(rstd_ready, g + 1)
                for b in range(4 * g, 4 * g + 4):
                    op = dve.tensor_scalar(state[:, b, :], R[:, b, :], mv[:, b, 0:1], rstd[:, b:b + 1], ALU.subtract, ALU.mult)
                op.then_inc(x_ready, 1)

            for g in range(4):
                stats(g)
                if g > 0:
                    normalise(g - 1)
            normalise(3)

        @block.gpsimd
        def _(pool):
            for k in range(3):
                pool.wait_ge(max_part, k + 1)
                pool.partition_all_reduce(gmax[:, k:k + 1], pmax[:, k:k + 1], P, bass.bass_isa.ReduceOp.max).then_inc(max_all, 1)
            for c in range(FC):
                up = hid[:, FC + c, :]
                pool.wait_ge(up_rounded, c + 1)
                pool.tensor_scalar(up, up, -MAGIC, scl[:, UP:UP + 1], ALU.add, ALU.mult).then_inc(up_ready, 1)
            for k in range(3, 5):
                pool.wait_ge(max_part, k + 1)
                pool.partition_all_reduce(gmax[:, k:k + 1], pmax[:, k:k + 1], P, bass.bass_isa.ReduceOp.max).then_inc(max_all, 1)
            for g in range(4):
                pool.wait_ge(var_ready, g + 1)
                pool.tensor_tensor(rstd[:, 4 * g:4 * g + 4], ve[:, 4 * g:4 * g + 4], neg_half[:, 0:4], ALU.pow).then_inc(rstd_ready, 1)

        @block.tensor
        def _(pe):
            pe.wait_ge(wq_ready, 1)
            for u in range(N_W):
                for j in range(3):
                    mm = pe.transpose(banks[u][:, j * P:(j + 1) * P], wr[:, 3 * u + j, :], ident)
                mm.then_inc(bank_full, 1)
            for t in range(N_X):
                pe.wait_ge(xq_ready, t + 1)
                for j in range(4):
                    mm = pe.transpose(banks[N_W + t][:, j * P:(j + 1) * P], xq[:, 4 * t + j, :], ident)
                mm.then_inc(bank_full, 1)
            pe.wait_ge(bank_taken, N_W + N_X)
            for k in range(N_H):
                u = N_W + N_X + k
                if u >= N_W + N_X + 1:
                    pe.wait_ge(bank_taken, max(u - 7, N_W + N_X))
                pe.matmul(banks[u % 8][:, :], wt[:, k // 4, :], xqt[:, (k % 4) * 512:(k % 4 + 1) * 512], start=True, stop=True).then_inc(bank_full, 1)
            pe.wait_ge(prod_ready, FC)
            pe.wait_ge(bank_taken, N_W + N_X + N_H)
            for g in range(4):
                u = N_W + N_X + N_H + g
                for j in range(4):
                    t = 4 * g + j
                    for c in range(FC):
                        mm = pe.matmul(banks[u % 8][:, j * D:(j + 1) * D], hid[:, c, t * S:(t + 1) * S], wt[:, 6 + c, :], start=c == 0, stop=c == FC - 1)
                mm.then_inc(bank_full, 1)
            for g in range(4):
                u = N_W + N_X + N_H + 4 + g
                pe.wait_ge(x_ready, g + 1)
                for j in range(4):
                    mm = pe.transpose(banks[u % 8][:, j * S:(j + 1) * S], state[:, 4 * g + j, :], ident)
                mm.then_inc(bank_full, 1)

        @block.scalar
        def _(act):
            for u in range(N_W):
                act.wait_ge(bank_full, u + 1)
                act.activation(wt[:, 3 * u:3 * u + 3, :], heads_view(banks[u][:, 0:3 * P], 3), ACT.Copy).then_inc(bank_taken, 1)
            for t in range(N_X):
                act.wait_ge(bank_full, N_W + t + 1)
                act.activation(xqt[:, t * 512:(t + 1) * 512], banks[N_W + t][:, :], ACT.Copy).then_inc(bank_taken, 1)
            for k in range(N_H):
                u = N_W + N_X + k
                act.wait_ge(bank_full, u + 1)
                act.activation(hid[:, k // 4, (k % 4) * 512:(k % 4 + 1) * 512], banks[u % 8][:, :], ACT.Copy).then_inc(bank_taken, 1)
            for c in range(FC):
                act.wait_ge(gate_ready, c + 1)
                act.activation(sig[:, c, :], hid[:, c, :], ACT.Sigmoid).then_inc(sig_ready, 1)

            def rounded(c, by):
                return act.activation(hid[:, c, :], hid[:, c, :], ACT.Identity, scale=by, bias=magic[:, :])

            act.wait_ge(scale_ready, UP + 1)
            for c in range(FC):
                rounded(FC + c, inv[:, UP:UP + 1]).then_inc(up_rounded, 1)
            act.wait_ge(scale_ready, GATED + 1)
            for c in range(FC):
                rounded(c, inv[:, GATED:GATED + 1]).then_inc(gated_rounded, 1)
            act.wait_ge(scale_ready, PROD + 1)
            for c in range(FC):
                rounded(c, prod_by[:, :]).then_inc(prod_rounded, 1)
            for g in range(4):
                u = N_W + N_X + N_H + 4 + g
                act.wait_ge(bank_full, u + 1)
                act.activation(state_t[:, 4 * g:4 * g + 4, :], heads_view(banks[u % 8][:, :], 4), ACT.Copy).then_inc(bank_taken, 1)


def decoder_kernel(nc, dram, out, cols):
    ctx = ExitStack()
    with ctx:
        def sb(name, shape, dt=F32, scope=ctx):
            return scope.enter_context(nc.sbuf_tensor(name, shape, dt))

        def sem(name):
            return ctx.enter_context(nc.semaphore(name))

        def part(tensor, pack, name):
            a, n = cols[pack][name]
            return tensor[:, a:a + n]

        w_in = {k: sem(f"w_in_{k}") for k in cols}
        body_names = ["next_in",
                      "ctx_in", "mask_in", "x_out",
                      "proj_ready",
                      "proj_by_act", "proj_by_dve",
                      "masked",
                      "rope_ready",
                      "scores_ready", "negmax_ready", "moved", "exp_done", "rsum_ready", "norm_done",
                      "second_ready", "pt_act", "pt_dve", "values_ready", "out_taken",
                      "silu_done", "gate_done", "acc_done", "acc_start",
                      "resid_ready",
                      "logits_ready", "route_exp", "route_ready",
                      "var_ready", "rstd_ready", "x_ready", "stat2_ready", "rstd2_ready", "norm2_ready",
                      "chain_dve", "chain_pool", "keymask_ready",
                      "ctx_stats", "ctx_rstd", "ctx_norm", "state_in_dve", "state_in_act"]
        sems = {n: sem("body_" + n) for n in body_names}
        nums = sorted(x.num for x in sems.values())
        assert nums == list(range(nums[0], nums[-1] + 1))
        body_range = range(nums[0], nums[-1] + 1)

        score_bank = [ctx.enter_context(nc.psum_tensor(f"score_bank{i}", [P, 512], F32)) for i in range(3)]
        second_bank = ctx.enter_context(nc.psum_tensor("second_bank", [P, 512], F32))
        value_bank = ctx.enter_context(nc.psum_tensor("value_bank", [P, 512], F32))
        proj_bank = [ctx.enter_context(nc.psum_tensor(f"proj_bank{i}", [P, 512], F32)) for i in range(N_PROJ)]

        const = sb("const", [P, sum(n for _, n in cols["const"].values())])
        ident = part(const, "const", "ident")
        head_scale = part(const, "const", "group")
        value_pick = part(const, "const", "vpick").rearrange("p (j d) -> p j d", j=4)
        lower = part(const, "const", "lower").rearrange("p (i j) -> p i j", i=NE)
        ident_b = sb("ident_b", [P, P], BF16)
        causal_b = sb("causal_b", [P, 4, P], BF16)
        neg_half = sb("neg_half", [P, G])
        state = sb("state", [P, B, D])

        def run_loop(tag, plan, w, scope, last_loop, state_t=None, score_w=None):
            X = sb(tag + "x", [P, G, D], scope=scope)
            XT = sb(tag + "xt", [P, G, S], scope=scope)
            R = sb(tag + "r", [P, G, D], scope=scope)
            st6 = sb(tag + "st6", [P, G, 6], scope=scope)
            mv = sb(tag + "mv", [P, G, 2], scope=scope)
            ve = sb(tag + "ve", [P, G], scope=scope)
            rstd = sb(tag + "rstd", [P, G], scope=scope)
            Pb = sb(tag + "probs", [P, 4, 512], scope=scope)
            PT = sb(tag + "probs_t", [P, 2, 512], scope=scope)
            negmax = sb(tag + "negmax", [P, 4, 4], scope=scope)
            rsum = sb(tag + "rsum", [P, 4, 4], scope=scope)
            rinv = sb(tag + "rinv", [P, 4, 4], scope=scope)
            OT = sb(tag + "ot", [P, 2, 8, S], scope=scope)
            QK = sb(tag + "qk", [P, 2, 2, S], scope=scope)
            RT2 = sb(tag + "rt", [P, 2, 2, S], scope=scope)
            Qg = sb(tag + "qg", [P, 2, 4, S], scope=scope)
            Km = sb(tag + "km", [P, 2, 4, S], scope=scope)
            Vm = sb(tag + "vm", [P, 2, 4, D], scope=scope)
            nkeys = 2 * S if last_loop else S
            V64 = sb(tag + "v64", [P, 2, nkeys // S, 1024], scope=scope)
            H = sb(tag + "h", [P, 4, 2, S], scope=scope)
            HS = sb(tag + "hs", [P, 3, 2, S], scope=scope)
            if last_loop:
                Q64 = sb(tag + "q64", [P, 2, 16, S], scope=scope)
                KV = sb(tag + "kv", [P, G, 2, S], scope=scope)
                CX = sb(tag + "cx", [P, G, D], scope=scope)
                LH = sb(tag + "lh", [P, G, D], scope=scope)
                st6b = sb(tag + "st6b", [P, G, 6], scope=scope)
                mv2 = sb(tag + "mv2", [P, G, 2], scope=scope)
                ve2 = sb(tag + "ve2", [P, G], scope=scope)
                rstd2 = sb(tag + "rstd2", [P, G], scope=scope)
                mask_u8 = sb(tag + "mask_u8", [P, G, S], U8, scope=scope)
                key_mask = sb(tag + "key_mask", [P, G, 2, S], scope=scope)
            else:
                Qz = sb(tag + "qz", [P, 2, 8, 2, S], scope=scope)
                K64 = sb(tag + "k64", [P, 2, 8, S], scope=scope)
                CT = sb(tag + "ct", [P, G, S], scope=scope)
                Q8 = sb(tag + "q8", [P, 3, 8, S], scope=scope)
                K8 = sb(tag + "k8", [P, 3, S], scope=scope)
                V8 = sb(tag + "v8", [P, 4, D], scope=scope)
                mask_u8 = sb(tag + "mask_u8", [P, G, S], U8, scope=scope)
                clip_hi = sb(tag + "clip_hi", [P, G, S], scope=scope)
                lg = sb(tag + "lg", [P, G, NE], scope=scope)
                lmax = sb(tag + "lmax", [P, G], scope=scope)
                lexp = sb(tag + "lexp", [P, G, NE], scope=scope)
                lsum = sb(tag + "lsum", [P, G], scope=scope)
                beat = sb(tag + "beat", [P, 2, NE, 2, NE], scope=scope)
                rank = sb(tag + "rank", [P, G, NE], scope=scope)
                pick = sb(tag + "pick", [P, G, NE], scope=scope)
                odd_sum = HS[:, 0, :, :]
                wsum = sb(tag + "wsum", [P, G], scope=scope)
                winv = sb(tag + "winv", [P, G], scope=scope)
                gatew = sb(tag + "gatew", [P, G, NE], scope=scope)
                gatewT = sb(tag + "gatew_t", [NE, 2, S], scope=scope)
            if not last_loop:
                first_in = sem("first_in")
                inputs = {"xT": XT, "x": X, "ctxT": CT, "mask_bk1": mask_u8}

                def load(name, iteration):
                    of = dram[name][bass.ds(iteration, 1)]
                    of = of.rearrange("a n -> (a n)").partition_broadcast(P) if name == "mask_bk1" else of.rearrange("a p n -> p (a n)")
                    return nc.sync.dma_start(inputs[name][:, :, :].rearrange("p a n -> p (a n)"), of)
            with nc.Block() as block:
                @block.vector
                def _(dve):
                    dve.memset(Km[:, :, :, :], 0.0)

                if not last_loop:
                    @block.sync
                    def _(sp):
                        for name in inputs:
                            load(name, 0).then_inc(first_in, 16)
                        for layer in plan.layers[1:]:
                            sp.dma_start(w[layer.name][:, :], dram[layer.name]).then_inc(w_in[layer.name], 16)
                        sp.wait_ge(first_in, 16 * len(inputs))

                    @block.gpsimd
                    def _(pool):
                        pool.memset(Qz[0:64, :, :, 1, :], 0.0)
                        pool.memset(Qz[64:128, :, :, 0, :], 0.0)
            iters = nc.Fori(0, NIT)
            it = iters.__enter__()

            names = [plan.layers[L].name for L, _ in plan.steps]

            def used(eng, s, name):
                u = plan.at[s, name]
                reader = plan.uses[u][2]
                return sems["proj_by_" + reader], plan.used_by(reader, u)

            passed = {}

            def wait_once(eng, semaphore, value):
                if passed.get((eng, semaphore.num), 0) < value:
                    passed[eng, semaphore.num] = value
                    eng.wait_ge(semaphore, value)

            def after_reader(eng, s, name):
                wait_once(eng, *used(eng, s, name))

            def state_t_ready(eng, s):
                if s in plan.before:
                    after_reader(eng, plan.before[s], "xT")
                elif last_loop:
                    wait_once(eng, sems["state_in_act"], 1)

            def state_ready(eng, s):
                if s in plan.before:
                    wait_once(eng, sems["x_ready"], plan.before[s] + 1)
                elif last_loop:
                    wait_once(eng, sems["state_in_dve"], 1)

            def weights(eng, s):
                wait_once(eng, w_in[names[s]], 16)

            def W(s, name):
                return part(w[names[s]], names[s], name)

            def routed(s):
                return sum(plan.kind(t) in ("moe", "lin") for t in range(s + 1))

            def second_of(n):
                s, i, kind, _ = plan.unit(n)
                return value_bank if kind in ("moe", "lin", "ffn") and i % 2 else second_bank

            def out_before(n):
                k = 0
                for m in range(min(n, plan.n)):
                    s, i, kind, _ = plan.unit(m)
                    k += kind in ("mqa", "h64c", "h64m") or (kind in H8 and i == 3)
                return k

            with nc.Block() as block:
                @block.sync
                def _(sp):
                    if last_loop:
                        sp.dma_start(CX[:, :, :].rearrange("p a n -> p (a n)"), dram["ctx"][bass.ds(it, 1)].rearrange("a p n -> p (a n)")).then_inc(sems["ctx_in"], 16)
                        sp.dma_start(mask_u8[:, :, :].rearrange("p a n -> p (a n)"), dram["mask_bk0"][bass.ds(it, 1)].rearrange("a n -> (a n)").partition_broadcast(P)).then_inc(sems["mask_in"], 16)
                        for b in range(G):
                            sp.wait_ge(sems["x_ready"], (len(plan.layers) - 1) * G + b + 1)
                            sp.dma_start(out[bass.ds(it * G + b, 1)].rearrange("a p d -> p (a d)"), X[:, b, :]).then_inc(sems["x_out"], 16)
                        sp.wait_ge(sems["x_out"], 16 * G)
                    else:
                        end = len(plan.steps) - 1
                        sp.wait_ge(sems["keymask_ready"], 1)
                        load("mask_bk1", it + 1).then_inc(sems["next_in"], 16)
                        sp.wait_ge(sems["proj_ready"], plan.at[end, "v1"] + 1)
                        load("xT", it + 1).then_inc(sems["next_in"], 16)
                        load("ctxT", it + 1).then_inc(sems["next_in"], 16)
                        sp.wait_ge(sems["resid_ready"], sum(plan.layer(s).out_bias for s in range(end + 1)))
                        load("x", it + 1).then_inc(sems["next_in"], 16)
                        sp.wait_ge(sems["next_in"], 4 * 16)

                @block.tensor
                def _(pe):
                    def open_use(s, name):
                        u = plan.at[s, name]
                        if u >= N_PROJ:
                            after_reader(pe, *plan.uses[u - N_PROJ][:2])
                        return proj_bank[u % N_PROJ]

                    def project(s, name):
                        kind, b = plan.kind(s), plan.steps[s][1]
                        bank = open_use(s, name)
                        if b == 0:
                            weights(pe, s)
                        if name not in ("gateT", "biases") and kind != "h64m":
                            state_t_ready(pe, s)
                        kv = XT
                        if plan.layer(s).ctx and name != "q0" and name != "q1":
                            kv = CT
                        xt = XT[:, b, :]
                        if kind == "mqa" and name != "kv":
                            for j in range(4):
                                h = 4 * int(name[1]) + j
                                mm = pe.matmul(bank[:, j * S:(j + 1) * S], W(s, "Wq")[:, h * P:(h + 1) * P], xt, start=True, stop=True)
                        elif kind == "mqa":
                            pe.matmul(bank[:, 0:S], W(s, "Wkv")[:, 0:P], xt, start=True, stop=True)
                            mm = pe.matmul(bank[:, S:2 * S], xt, W(s, "Wkv")[:, P:2 * P], start=True, stop=True)
                        elif name == "qk":
                            pe.matmul(bank[:, 0:S], W(s, "Wq"), xt, start=True, stop=True)
                            mm = pe.matmul(bank[:, S:2 * S], W(s, "Wk"), kv[:, b, :], start=True, stop=True)
                            if kind == "h8r":
                                pe.matmul(bank[:, 2 * S:3 * S], W(s, "Wq_turned"), xt, start=True, stop=True)
                                mm = pe.matmul(bank[:, 3 * S:4 * S], W(s, "Wk_turned"), xt, start=True, stop=True)
                        elif name == "v":
                            mm = pe.matmul(bank[:, 0:D], kv[:, b, :], W(s, "Wv"), start=True, stop=True)
                        elif name == "router":
                            mm = pe.matmul(bank[:, 0:64], xt, W(s, "Wr"), start=True, stop=True)
                        elif name == "gateT":
                            pe.wait_ge(sems["route_ready"], routed(s))
                            mm = pe.transpose(bank[0:NE, 0:P], gatew[:, b, :], ident)
                        elif name == "biases":
                            after_reader(pe, s, "gateT")
                            mm = pe.matmul(bank[:, 0:D], gatewT[:, b % 2, :], W(s, "be")[0:NE, :], start=True, stop=True)
                        elif kind == "h64c":
                            half = int(name[1])
                            for j in range(4):
                                c = 4 * half + j
                                to = bank[:, j * S:(j + 1) * S]
                                if name[0] == "q":
                                    mm = pe.matmul(to, W(s, "Wq")[:, c * P:(c + 1) * P], xt, start=True, stop=True)
                                if name[0] == "k":
                                    mm = pe.matmul(to, W(s, "Wk")[:, c * P:(c + 1) * P], CT[:, b, :], start=True, stop=True)
                            if name[0] == "v":
                                mm = pe.matmul(bank[:, :], CT[:, b, :], W(s, "Wv")[:, half * 512:(half + 1) * 512], start=True, stop=True)
                        else:
                            if name == "c":
                                pe.wait_ge(sems["ctx_norm"], 1)
                            else:
                                after_reader(pe, s, "c")
                                after_reader(pe, plan.before[s], "xT")
                                i = int(name[1])
                            if name == "c":
                                mm = pe.transpose(bank[:, 0:S], CX[:, b, :], ident)
                            elif name[0] == "q":
                                for j in range(4):
                                    mm = pe.matmul(bank[:, j * S:(j + 1) * S], score_w[:, 4 * i + j, :], KV[:, b, 1, :], start=True, stop=True)
                            else:
                                mm = pe.matmul(bank[:, :], KV[:, b, i // 2, :], W(s, "Wv")[:, (i % 2) * 512:(i % 2 + 1) * 512], start=True, stop=True)
                        mm.then_inc(sems["proj_ready"], 1)

                    def scores(n):
                        s, i, kind, b = plan.unit(n)
                        if kind == "lin":
                            return
                        bank = score_bank[n % 3]
                        last = [k for k in range(n) if k % 3 == n % 3 and plan.unit(k)[2] in STAGES["scores"]]
                        if last:
                            k3 = plan.unit(last[-1])[2]
                            done = {"moe": ("gate_done", "gate"), "ffn": ("silu_done", "silu")}.get(
                                k3, ("moved", "moved") if k3 in STAGES["moved"] else ("exp_done", "exp"))
                            wait_once(pe, sems[done[0]], plan.count(done[1], last[-1]))
                        if i == 0:
                            if kind in SOFTMAX:
                                for name, _, _ in EARLY[kind]:
                                    if name[0] != "v":
                                        after_reader(pe, s, name)
                            if kind == "moe":
                                if b == 0:
                                    weights(pe, s)
                                state_t_ready(pe, s)
                            if kind in H8:
                                pe.wait_ge(sems["masked"], (1 + sum(plan.kind(t) in H8 for t in range(s))))
                            if kind == "ffn":
                                if b == 0:
                                    weights(pe, s)
                                state_t_ready(pe, s)
                        mask = plan.layer(s).mask
                        if mask == "causal":
                            pe.matmul(bank[:, :], ident_b[:, :], causal_b[:, :, :].rearrange("p a k -> p (a k)"), start=True, stop=False)
                        if kind == "mqa":
                            for j in range(4):
                                mm = pe.matmul(bank[:, j * S:(j + 1) * S], Q8[:, plan.ring(s, 3), 4 * i + j, :], K8[:, plan.ring(s, 3), :], start=False, stop=j == 3)
                        elif kind in H8:
                            mm = pe.matmul(bank[:, :], Qg[:, plan.ring(s, 2), i, :], Km[:, plan.ring(s, 2), :, :].rearrange("p j k -> p (j k)"), start=mask != "causal", stop=True)
                        elif kind == "h64c":
                            for j in range(4):
                                mm = pe.matmul(bank[:, j * S:(j + 1) * S], Qz[:, plan.ring(s, 2), 2 * i + j // 2, j % 2, :], K64[:, plan.ring(s, 2), 2 * i + j // 2, :], start=True, stop=True)
                        elif kind == "h64m":
                            for j in range(2):
                                mm = pe.matmul(bank[:, j * 256:(j + 1) * 256], Q64[:, plan.ring(s, 2), 2 * i + j, :],
                                               KV[:, b, :, :].rearrange("p a k -> p (a k)"), start=True, stop=True)
                        elif kind == "moe":
                            for j in range(4):
                                c = (2 * i + j % 2) * P
                                mm = pe.matmul(bank[:, j * S:(j + 1) * S], W(s, "gate_w" if j < 2 else "up_w")[:, c:c + P], XT[:, b, :], start=True, stop=True)
                        elif kind == "ffn":
                            for j in range(2):
                                c = (2 * i + j) * P
                                mm = pe.matmul(bank[:, j * S:(j + 1) * S], fc1[:, c:c + P], XT[:, b, :], start=True, stop=True)
                        mm.then_inc(sems["scores_ready"], 1)

                    def second(n):
                        s, i, kind, b = plan.unit(n)
                        if kind not in STAGES["second"]:
                            return
                        bank = second_of(n)
                        before = [k for k in range(n) if plan.unit(k)[2] in STAGES["second"] and second_of(k) is bank]
                        if before:
                            stage = "acc" if plan.unit(before[-1])[2] in STAGES["acc"] else plan.copier(before[-1])
                            wait_once(pe, sems["acc_done" if stage == "acc" else stage], plan.count(stage, before[-1]))
                        if bank is value_bank and out_before(n):
                            wait_once(pe, sems["out_taken"], out_before(n))
                        if kind in SOFTMAX:
                            pe.wait_ge(sems["norm_done"], plan.count("norm", n))
                            for j in range(4):
                                mm = pe.transpose(bank[:, j * S:(j + 1) * S], Pb[:, n % 4, j * S:(j + 1) * S], ident)
                        elif kind == "lin":
                            if i == 0:
                                if b == 0:
                                    weights(pe, s)
                                state_t_ready(pe, s)
                            mm = pe.matmul(bank[:, :], XT[:, b, :], W(s, "We")[:, i * 512:(i + 1) * 512], start=True, stop=True)
                        elif kind == "moe":
                            pe.wait_ge(sems["gate_done"], plan.count("gate", n))
                            for j in range(2):
                                c = (2 * i + j) * D
                                mm = pe.matmul(bank[:, 0:D], H[:, n % 4, j, :], W(s, "down_w")[:, c:c + D], start=j == 0, stop=j == 1)
                        else:
                            pe.wait_ge(sems["silu_done"], plan.count("silu", n))
                            for j in range(2):
                                mm = pe.matmul(bank[:, 0:D], H[:, n % 4, j, :], fc2[:, 2 * i + j, :], start=j == 0, stop=j == 1)
                        mm.then_inc(sems["second_ready"], 1)

                    def values(n):
                        s, i, kind, b = plan.unit(n)
                        if kind not in SOFTMAX:
                            return
                        stage = plan.copier(n)
                        if i == 0:
                            for name, _, _ in EARLY[kind]:
                                if name[0] == "v":
                                    after_reader(pe, s, name)
                        wait_once(pe, sems[stage], plan.count(stage, n))
                        outs = out_before(n)
                        if outs:
                            wait_once(pe, sems["out_taken"], outs)
                        experts = [k for k in range(n) if second_of(k) is value_bank]
                        if experts:
                            wait_once(pe, sems["acc_done"], plan.count("acc", experts[-1]))
                        pt = PT[:, n % 2, :]
                        if kind == "mqa":
                            mm = pe.matmul(value_bank[:, :], V8[:, plan.ring(s, 4), :], pt, start=True, stop=True)
                        elif kind in H8:
                            for j in range(4):
                                mm = pe.matmul(value_bank[32 * j:32 * j + 32, 0:S], Vm[:, plan.ring(s, 2), i, 32 * j:32 * j + 32], pt[:, j * S:(j + 1) * S], start=i == 0, stop=i == 3)
                        elif kind == "h64c":
                            for j in range(4):
                                h = 4 * i + j
                                mm = pe.matmul(value_bank[64 * (j % 2):64 * (j % 2) + 64, (j // 2) * S:(j // 2 + 1) * S],
                                               V64[:, plan.ring(s, 2), 0, h * 64:(h + 1) * 64], pt[:, j * S:(j + 1) * S], start=True, stop=True)
                        else:
                            for c in range(2):
                                for j in range(2):
                                    h = 2 * i + j
                                    mm = pe.matmul(value_bank[64 * j:64 * j + 64, 0:S], V64[:, plan.ring(s, 2), c, h * 64:(h + 1) * 64],
                                                   pt[:, (2 * j + c) * S:(2 * j + c + 1) * S], start=c == 0, stop=c == 1)
                        mm.then_inc(sems["values_ready"], 1)

                    def output(s):
                        bank = open_use(s, "y")
                        wait_once(pe, sems["out_taken"], out_before(plan.last[s] + 1))
                        chunks = 1 if plan.kind(s) in H8 else 8
                        for c in range(chunks):
                            mm = pe.matmul(bank[:, 0:D], OT[:, plan.ring(s, 2), c, :], W(s, "Wo")[:, c * D:(c + 1) * D], start=c == 0, stop=c == chunks - 1)
                        mm.then_inc(sems["proj_ready"], 1)

                    def turn(s):
                        b = plan.steps[s][1]
                        bank = open_use(s, "xT")
                        if plan.affine_next(s):
                            pe.wait_ge(sems["norm2_ready"], 1 + sum(plan.affine_next(t) for t in range(s)))
                            mm = pe.transpose(bank[:, 0:S], LH[:, b, :], ident)
                        else:
                            pe.wait_ge(sems["x_ready"], s + 1)
                            mm = pe.transpose(bank[:, 0:S], X[:, b, :], ident)
                        mm.then_inc(sems["proj_ready"], 1)

                    def after(half):
                        for what, s in plan.after.get(half, []):
                            if what == "output" and plan.kind(s) in SOFTMAX:
                                output(s)
                            if what == "turn":
                                turn(s)

                    for n in plan.slots():
                        after(2 * n)
                        if 0 <= n + AHEAD < plan.n:
                            scores(n + AHEAD)
                        if 0 <= n < plan.n:
                            second(n)
                        if 0 <= n - 1 < plan.n:
                            values(n - 1)
                        after(2 * n + 1)
                        for s, name, _ in plan.early.get(n, []):
                            project(s, name)

                @block.scalar
                def _(act):
                    def take(s, name):
                        kind, b = plan.kind(s), plan.steps[s][1]
                        u = plan.at[s, name]
                        bank = proj_bank[u % N_PROJ]
                        act.wait_ge(sems["proj_ready"], u + 1)
                        if name == "qk":
                            if b == 0:
                                weights(act, s)
                            act.activation(QK[:, plan.ring(s, 2), 0, :], bank[:, 0:S], ACT.Identity, bias=W(s, "bq"))
                            for j in range(4):
                                rows = slice(32 * j, 32 * j + 32)
                                op = act.activation(Km[rows, plan.ring(s, 2), j, :], bank[rows, S:2 * S], ACT.Identity, bias=W(s, "bk")[rows, :])
                        elif name == "c":
                            if b == 0:
                                act.wait_ge(w_in["L3_xattn"], 16)
                            g, e = (part(w["L3_xattn"], "L3_xattn", k) for k in ("g1", "b1"))
                            op = act.activation(KV[:, b, 0, :], bank[:, 0:S], ACT.Identity, scale=g, bias=e)
                        elif name == "gateT":
                            op = act.activation(gatewT[:, b % 2, :], bank[0:NE, 0:P], ACT.Copy)
                        elif kind == "h64m" and name[0] == "q":
                            i = int(name[1])
                            op = act.activation(Q64[:, plan.ring(s, 2), 4 * i:4 * i + 4, :], heads_view(bank[:, :], 4), ACT.Copy)
                        elif name[0] == "q":
                            half = int(name[1])
                            for j in range(2):
                                op = act.activation(Qz[64 * j:64 * j + 64, plan.ring(s, 2), 4 * half:4 * half + 4, j, :],
                                                    heads_view(bank[64 * j:64 * j + 64, :], 4), ACT.Copy, scale=0.125)
                        elif name[0] == "v":
                            i = int(name[1])
                            op = act.activation(V64[:, plan.ring(s, 2), i // 2, (i % 2) * 512:(i % 2 + 1) * 512], bank[:, :], ACT.Copy)
                        else:
                            to = plan.next_kind(s)
                            if to == "h64m":
                                if b == 0:
                                    act.wait_ge(w_in["L3_xattn"], 16)
                                g, e = (part(w["L3_xattn"], "L3_xattn", k) for k in ("g2", "b2"))
                                op = act.activation(KV[:, b, 1, :], bank[:, 0:S], ACT.Identity, scale=g, bias=e)
                            elif to == "ffn":
                                if b == 0:
                                    act.wait_ge(w_in["L3_ffn"], 16)
                                g, e = (part(w["L3_ffn"], "L3_ffn", k) for k in ("gamma", "beta"))
                                op = act.activation(XT[:, b, :], bank[:, 0:S], ACT.Identity, scale=g, bias=e)
                            else:
                                op = act.activation(XT[:, b, :], bank[:, 0:S], ACT.Copy)
                        op.then_inc(sems["proj_by_act"], 1)

                    def front(n):
                        s, i, kind, b = plan.unit(n)
                        if kind in SOFTMAX:
                            heads, width = (2, 256) if kind == "h64m" else (4, S)
                            if kind == "h64c":
                                act.wait_ge(sems["moved"], plan.count("moved", n))
                            else:
                                act.wait_ge(sems["negmax_ready"], plan.count("negmax", n))
                            for j in range(heads):
                                p = Pb[:, n % 4, j * width:(j + 1) * width]
                                if kind == "h64c":
                                    op = act.activation(p, p, ACT.Exp, accum_out=rsum[:, n % 4, j:j + 1])
                                elif kind in STAGES["moved"]:
                                    op = act.activation(p, p, ACT.Exp, bias=negmax[:, n % 4, j:j + 1], accum_out=rsum[:, n % 4, j:j + 1])
                                else:
                                    op = act.activation(p, score_bank[n % 3][:, j * width:(j + 1) * width], ACT.Exp,
                                                        bias=negmax[:, n % 4, j:j + 1], accum_out=rsum[:, n % 4, j:j + 1])
                            op.then_inc(sems["exp_done"], 1)
                        elif kind == "moe":
                            if i == 0 and b == 0:
                                weights(act, s)
                            act.wait_ge(sems["scores_ready"], plan.count("scores", n))
                            for j in range(2):
                                op = act.activation(HS[:, n % 3, j, :], score_bank[n % 3][:, j * S:(j + 1) * S], ACT.Silu,
                                                    bias=W(s, "gate_b")[:, 2 * i + j:2 * i + j + 1])
                            op.then_inc(sems["silu_done"], 1)
                        elif kind == "ffn":
                            act.wait_ge(sems["scores_ready"], plan.count("scores", n))
                            for j in range(2):
                                op = act.activation(H[:, n % 4, j, :], score_bank[n % 3][:, j * S:(j + 1) * S], ACT.Silu,
                                                    bias=W(s, "fc1_b")[:, 2 * i + j:2 * i + j + 1])
                            op.then_inc(sems["silu_done"], 1)

                    def turned(n):
                        kind = plan.unit(n)[2]
                        if plan.copier(n) == "pt_act":
                            act.wait_ge(sems["second_ready"], plan.count("second", n))
                            m = plan.count("second", n) - 1
                            act.activation(PT[:, n % 2, :], second_of(n)[:, :], ACT.Copy).then_inc(sems["pt_act"], 1)

                    def outs(n):
                        s, i, kind, b = plan.unit(n)
                        if kind in H8 and i < 3 or kind not in SOFTMAX:
                            return
                        act.wait_ge(sems["values_ready"], plan.count("values", n))
                        if kind == "mqa":
                            if i == 0 and b == 0:
                                weights(act, s)
                            op = act.activation(OT[:, plan.ring(s, 2), 4 * i:4 * i + 4, :], heads_view(value_bank[:, :], 4), ACT.Identity, bias=W(s, "bkv")[:, 1:2])
                        elif kind in ("h8", "h8p"):
                            op = act.activation(OT[:, plan.ring(s, 2), 0, :], value_bank[:, 0:S], ACT.Identity, bias=W(s, "bv"))
                        elif kind == "h8r":
                            op = act.activation(OT[:, plan.ring(s, 2), 0, :], value_bank[:, 0:S], ACT.Copy)
                        elif kind == "h64c":
                            op = act.activation(OT[:, plan.ring(s, 2), 2 * i:2 * i + 2, :], heads_view(value_bank[:, 0:2 * S], 2), ACT.Copy)
                        else:
                            op = act.activation(OT[:, plan.ring(s, 2), i, :], value_bank[:, 0:S], ACT.Copy)
                        op.then_inc(sems["out_taken"], 1)

                    def route(s):
                        b = plan.steps[s][1]
                        act.wait_ge(sems["logits_ready"], routed(s))
                        act.activation(lexp[:, b, :], lg[:, b, :], ACT.Exp, bias=lmax[:, b:b + 1], accum_out=lsum[:, b:b + 1]).then_inc(sems["route_exp"], 1)

                    def after(half):
                        for what, s in plan.after.get(half, []):
                            if what == "turn":
                                take(s, "xT")

                    if last_loop:
                        act.activation(XT[:, :, :], state_t[:, bass.ds(it * G, G), :], ACT.Copy).then_inc(sems["state_in_act"], 1)
                    for n in plan.slots():
                        after(2 * n)
                        if 0 <= n < plan.n:
                            turned(n)
                        if 0 <= n - 1 < plan.n:
                            outs(n - 1)
                        if 0 <= n + AHEAD < plan.n:
                            front(n + AHEAD)
                        after(2 * n + 1)
                        for s, name, eng in plan.early.get(n, []):
                            if eng == "act":
                                take(s, name)
                            if name == "router":
                                route(s)

                @block.vector
                def _(dve):
                    chain = [0]

                    def link(op):
                        chain[0] += 1
                        op.then_inc(sems["chain_dve"], 1)
                        dve.wait_ge(sems["chain_dve"], chain[0])

                    def take(s, name):
                        kind, b = plan.kind(s), plan.steps[s][1]
                        u = plan.at[s, name]
                        bank = proj_bank[u % N_PROJ]
                        dve.wait_ge(sems["proj_ready"], u + 1)
                        if kind == "mqa" and name != "kv":
                            half = int(name[1])
                            op = dve.tensor_tensor(Q8[:, plan.ring(s, 3), 4 * half:4 * half + 4, :], heads_view(bank[:, :], 4), qpe[:, 4 * half:4 * half + 4, :], ALU.add)
                        elif kind == "mqa":
                            dve.scalar_tensor_tensor(K8[:, plan.ring(s, 3), :], bank[:, 0:S], D ** -0.5, kpe[:, :], ALU.mult, ALU.add)
                            op = dve.tensor_copy(V8[:, plan.ring(s, 4), :], bank[:, S:2 * S])
                        elif name == "qk":
                            if b == 0:
                                weights(dve, s)
                            dve.tensor_tensor(QK[:, plan.ring(s, 2), :, :], heads_view(bank[:, 0:2 * S], 2), over(W(s, "cos"), 2), ALU.mult)
                            op = dve.tensor_tensor(RT2[:, plan.ring(s, 2), :, :], heads_view(bank[:, 2 * S:4 * S], 2), over(W(s, "sin"), 2), ALU.mult)
                        elif name == "v":
                            op = dve.tensor_tensor(Vm[:, plan.ring(s, 2), :, :], over(bank[:, 0:D], 4), value_pick, ALU.mult)
                        elif name == "router":
                            if b == 0:
                                weights(dve, s)
                            if kind == "lin":
                                op = dve.tensor_tensor(lg[:, b, :], bank[:, 0:NE], W(s, "bg"), ALU.add)
                            else:
                                op = dve.tensor_copy(lg[:, b, :], bank[:, 0:NE])
                        elif name == "biases":
                            state_ready(dve, s)
                            op = dve.tensor_tensor(R[:, b, :], bank[:, 0:D], X[:, b, :], ALU.add)
                        elif name[0] == "k":
                            i = int(name[1])
                            n = 4
                            op = dve.tensor_copy(K64[:, plan.ring(s, 2), n * i:n * i + n, :], heads_view(bank[:, :], n))
                        elif kind == "h64m" and name[0] == "q":
                            i = int(name[1])
                            op = dve.tensor_copy(Q64[:, plan.ring(s, 2), 4 * i:4 * i + 4, :], heads_view(bank[:, :], 4))
                        elif name[0] == "v":
                            i = int(name[1])
                            op = dve.tensor_copy(V64[:, plan.ring(s, 2), i // 2, (i % 2) * 512:(i % 2 + 1) * 512], bank[:, :])
                        op.then_inc(sems["proj_by_dve"], 1)
                        if name == "qk":
                            after_reader(dve, s, name)
                            for j in range(4):
                                rows = slice(32 * j, 32 * j + 32)
                                dve.tensor_tensor(Km[rows, plan.ring(s, 2), j, :], QK[rows, plan.ring(s, 2), 1, :], RT2[rows, plan.ring(s, 2), 1, :], ALU.add)
                            dve.tensor_tensor(QK[:, plan.ring(s, 2), 0, :], QK[:, plan.ring(s, 2), 0, :], RT2[:, plan.ring(s, 2), 0, :], ALU.add).then_inc(sems["rope_ready"], 1)
                        if name == "router":
                            after_reader(dve, s, name)
                            dve.tensor_reduce(lmax[:, b:b + 1], lg[:, b, :], axis=AX.X, op=ALU.max, negate=True).then_inc(sems["logits_ready"], 1)

                    def rank_experts(s):
                        b = plan.steps[s][1]
                        mine, other = along(lg[:, b, :], NE), over(lg[:, b, :], NE)
                        dve.tensor_tensor(beat[:, b % 2, :, 0, :], other, mine, ALU.is_gt)
                        link(dve.tensor_tensor(beat[:, b % 2, :, 1, :], other, mine, ALU.is_equal))
                        link(dve.tensor_tensor(beat[:, b % 2, :, 1, :], beat[:, b % 2, :, 1, :], lower, ALU.mult))
                        link(dve.tensor_reduce(rank[:, b, :], beat[:, b % 2, :, :, :].rearrange("p i a j -> p i (a j)"), axis=AX.X, op=ALU.add))

                    def choose(s):
                        b, kind = plan.steps[s][1], plan.kind(s)
                        dve.wait_ge(sems["route_exp"], routed(s))
                        link(dve.scalar_tensor_tensor(pick[:, b, :], rank[:, b, :], 2.0, lexp[:, b, :], ALU.is_lt, ALU.mult))
                        link(dve.tensor_reduce(wsum[:, b:b + 1], pick[:, b, :], axis=AX.X, op=ALU.add))
                        if kind == "moe":
                            link(dve.scalar_tensor_tensor(wsum[:, b:b + 1], lsum[:, b:b + 1], 1e-9, wsum[:, b:b + 1], ALU.mult, ALU.add))
                        link(dve.reciprocal(winv[:, b:b + 1], wsum[:, b:b + 1]))
                        dve.tensor_scalar(gatew[:, b, :], pick[:, b, :], winv[:, b:b + 1], None, ALU.mult).then_inc(sems["route_ready"], 1)

                    def front(n):
                        s, i, kind, b = plan.unit(n)
                        bank = score_bank[n % 3]
                        if kind in STAGES["negmax"]:
                            heads = 2 if kind == "h64m" else 4
                            dve.wait_ge(sems["scores_ready"], plan.count("scores", n))
                            of = heads_view(bank[:, :], heads)
                            if kind in STAGES["moved"]:
                                of = heads_view(Pb[:, n % 4, :], heads)
                                if kind == "h8p":
                                    add = heads_view(W(s, "relpos")[:, i * 512:(i + 1) * 512], heads)
                                else:
                                    wait_once(dve, sems["keymask_ready"], 1)
                                    add = over(key_mask[:, b, :, :].rearrange("p a k -> p (a k)"), heads)
                                dve.tensor_tensor(of, heads_view(bank[:, :], heads), add, ALU.add).then_inc(sems["moved"], 1)
                                dve.wait_ge(sems["moved"], plan.count("moved", n))
                            dve.tensor_reduce(negmax[:, n % 4, 0:heads], of, axis=AX.X, op=ALU.max, negate=True).then_inc(sems["negmax_ready"], 1)
                        elif kind == "h64c":
                            if i == 0 and b == 0:
                                dve.wait_ge(sems["keymask_ready"], 1)
                            dve.wait_ge(sems["scores_ready"], plan.count("scores", n))
                            dve.scalar_tensor_tensor(heads_view(Pb[:, n % 4, :], 4), heads_view(bank[:, :], 4), -5.0, over(clip_hi[:, b, :], 4),
                                                     ALU.max, ALU.min).then_inc(sems["moved"], 1)
                        elif kind == "moe":
                            dve.wait_ge(sems["silu_done"], plan.count("silu", n))
                            for j in range(2):
                                op = dve.scalar_tensor_tensor(H[:, n % 4, j, :], bank[:, (2 + j) * S:(3 + j) * S], W(s, "up_b")[:, 2 * i + j:2 * i + j + 1],
                                                              HS[:, n % 3, j, :], ALU.add, ALU.mult)
                            op.then_inc(sems["gate_done"], 1)

                    def inverse(n):
                        s, i, kind, b = plan.unit(n)
                        if kind in SOFTMAX:
                            heads = 2 if kind == "h64m" else 4
                            dve.wait_ge(sems["exp_done"], plan.count("exp", n))
                            dve.reciprocal(rinv[:, n % 4, 0:heads], rsum[:, n % 4, 0:heads]).then_inc(sems["rsum_ready"], 1)

                    def back(n):
                        s, i, kind, b = plan.unit(n)
                        if plan.copier(n) == "pt_dve":
                            m = plan.count("second", n) - 1
                            dve.wait_ge(sems["second_ready"], m + 1)
                            dve.tensor_copy(PT[:, n % 2, :], second_of(n)[:, :]).then_inc(sems["pt_dve"], 1)
                        elif kind in STAGES["acc"]:
                            k = plan.count("acc", n)
                            if i == 0 and kind == "ffn":
                                dve.wait_ge(sems["acc_start"], 1 + sum(plan.kind(t) == "ffn" for t in range(s)))
                            elif i == 0:
                                after_reader(dve, s, "biases")
                            else:
                                dve.wait_ge(sems["acc_done"], k - 1)
                            if kind == "lin":
                                dve.wait_ge(sems["second_ready"], plan.count("second", n))
                                for j in range(4):
                                    e = 4 * i + j
                                    to = R[:, b, :] if j % 2 == 0 else odd_sum[:, b % 2, :]
                                    if j >= 2:
                                        dve.wait_ge(sems["chain_dve"], chain[0] - 1)
                                    if e == 1:
                                        op = dve.tensor_scalar(to, second_of(n)[:, j * D:(j + 1) * D], gatew[:, b, e:e + 1], None, ALU.mult)
                                    else:
                                        op = dve.scalar_tensor_tensor(to, second_of(n)[:, j * D:(j + 1) * D], gatew[:, b, e:e + 1], to, ALU.mult, ALU.add)
                                    if j < 3:
                                        chain[0] += 1
                                        op.then_inc(sems["chain_dve"], 1)
                                if e == NE - 1:
                                    link(op)
                                    op = dve.tensor_tensor(R[:, b, :], R[:, b, :], odd_sum[:, b % 2, :], ALU.add)
                            else:
                                m = plan.count("second", n) - 1
                                dve.wait_ge(sems["second_ready"], m + 1)
                                by = gatew[:, b, i:i + 1] if kind == "moe" else 0.5
                                op = dve.scalar_tensor_tensor(R[:, b, :], second_of(n)[:, 0:D], by, R[:, b, :], ALU.mult, ALU.add)
                            op.then_inc(sems["acc_done"], 1)

                    def add_and_stats(s):
                        b, kind = plan.steps[s][1], plan.kind(s)
                        if kind in SOFTMAX:
                            u = plan.at[s, "y"]
                            if plan.layer(s).out_bias:
                                dve.wait_ge(sems["resid_ready"], 1 + sum(plan.layer(t).out_bias for t in range(s)))
                            else:
                                state_ready(dve, s)
                            dve.wait_ge(sems["proj_ready"], u + 1)
                            dve.tensor_tensor(R[:, b, :], proj_bank[u % N_PROJ][:, 0:D], (R if plan.layer(s).out_bias else X)[:, b, :], ALU.add).then_inc(sems["proj_by_dve"], 1)
                            after_reader(dve, s, "y")
                        else:
                            dve.wait_ge(sems["acc_done"], plan.count("acc", plan.last[s]))
                        link(dve.bn_stats(st6[:, b, :], R[:, b, :]))
                        link(dve.bn_aggr(mv[:, b, :], st6[:, b, :]))
                        dve.tensor_scalar(ve[:, b:b + 1], mv[:, b, 1:2], EPS, None, ALU.add).then_inc(sems["var_ready"], 1)

                    def normalise(s):
                        b = plan.steps[s][1]
                        dve.wait_ge(sems["rstd_ready"], s + 1)
                        to = X[:, b, :]
                        if plan.next_kind(s) is None and not last_loop:
                            to = state[:, bass.ds(it * G + b, 1), :].rearrange("p a d -> p (a d)")
                        dve.tensor_scalar(to, R[:, b, :], mv[:, b, 0:1], rstd[:, b:b + 1], ALU.subtract, ALU.mult).then_inc(sems["x_ready"], 1)
                        if plan.affine_next(s):
                            dve.wait_ge(sems["x_ready"], s + 1)
                            link(dve.bn_stats(st6b[:, b, :], X[:, b, :]))
                            link(dve.bn_aggr(mv2[:, b, :], st6b[:, b, :]))
                            dve.tensor_scalar(ve2[:, b:b + 1], mv2[:, b, 1:2], EPS, None, ALU.add).then_inc(sems["stat2_ready"], 1)

                    def normalise_again(s):
                        b = plan.steps[s][1]
                        dve.wait_ge(sems["rstd2_ready"], 1 + sum(plan.affine_next(t) for t in range(s)))
                        dve.tensor_scalar(LH[:, b, :], X[:, b, :], mv2[:, b, 0:1], rstd2[:, b:b + 1], ALU.subtract, ALU.mult).then_inc(sems["norm2_ready"], 1)

                    def after(half):
                        for what, s in plan.after.get(half, []):
                            if what == "output":
                                add_and_stats(s)
                            if what == "normalise":
                                normalise(s)
                            if what == "normalise_again":
                                normalise_again(s)

                    def normalise_context():
                        dve.wait_ge(sems["ctx_in"], 16)
                        for b in range(G):
                            op = dve.bn_stats(st6b[:, b, :], CX[:, b, :])
                        link(op)
                        for b in range(G):
                            op = dve.bn_aggr(mv2[:, b, :], st6b[:, b, :])
                        link(op)
                        dve.tensor_scalar(ve2[:, :], mv2[:, :, 1], EPS, None, ALU.add).then_inc(sems["ctx_stats"], 1)
                        dve.wait_ge(sems["mask_in"], 16)
                        dve.memset(key_mask[:, :, 1, :], 0.0)
                        dve.tensor_scalar(key_mask[:, :, 0, :], mask_u8[:, :, :], -NEG, NEG, ALU.mult, ALU.add).then_inc(sems["keymask_ready"], 1)
                        dve.wait_ge(sems["ctx_rstd"], 1)
                        for b in range(G):
                            op = dve.tensor_scalar(CX[:, b, :], CX[:, b, :], mv2[:, b, 0:1], rstd2[:, b:b + 1], ALU.subtract, ALU.mult)
                        op.then_inc(sems["ctx_norm"], 1)

                    if last_loop:
                        dve.tensor_copy(X[:, :, :], state[:, bass.ds(it * G, G), :]).then_inc(sems["state_in_dve"], 1)
                    else:
                        dve.tensor_scalar(clip_hi[:, :, :], mask_u8[:, :, :], 10.0, -5.0, ALU.mult, ALU.add).then_inc(sems["keymask_ready"], 1)
                    for n in plan.slots():
                        if last_loop and n == CTX_SLOT:
                            normalise_context()
                        for s in plan.choice.get(n - 1, []):
                            choose(s)
                        after(2 * n)
                        if 0 <= n + AHEAD < plan.n:
                            front(n + AHEAD)
                        if 0 <= n + AHEAD - 1 < plan.n:
                            inverse(n + AHEAD - 1)
                        if 0 <= n < plan.n:
                            back(n)
                        after(2 * n + 1)
                        for s, name, eng in plan.early.get(n, []):
                            if eng == "dve":
                                take(s, name)
                        for s in plan.choice.get(n, []):
                            rank_experts(s)

                @block.gpsimd
                def _(pool):
                    chain = [0]

                    def link(op):
                        chain[0] += 1
                        op.then_inc(sems["chain_pool"], 1)
                        pool.wait_ge(sems["chain_pool"], chain[0])

                    def spread(s):
                        if plan.kind(s) == "h8r":
                            pool.wait_ge(sems["rope_ready"], 1 + sum(plan.kind(t) == "h8r" for t in range(s)))
                        else:
                            after_reader(pool, s, "qk")
                        pool.tensor_tensor(Qg[:, plan.ring(s, 2), :, :], over(QK[:, plan.ring(s, 2), 0, :], 4), along(head_scale, S), ALU.mult).then_inc(sems["masked"], 1)

                    def residual(s):
                        b = plan.steps[s][1]
                        if b == 0:
                            weights(pool, s)
                        state_ready(pool, s)
                        pool.tensor_tensor(R[:, b, :], X[:, b, :], W(s, "bo"), ALU.add).then_inc(sems["resid_ready"], 1)

                    def start_sum(s):
                        b = plan.steps[s][1]
                        state_ready(pool, s)
                        link(pool.tensor_tensor(R[:, b, :], X[:, b, :], half_b2[:, :], ALU.add))
                        pool.tensor_tensor(R[:, b, :], R[:, b, :], X[:, b, :], ALU.add).then_inc(sems["acc_start"], 1)

                    def probabilities(n):
                        s, i, kind, b = plan.unit(n)
                        if kind in SOFTMAX:
                            heads = 2 if kind == "h64m" else 4
                            pool.wait_ge(sems["rsum_ready"], plan.count("norm", n))
                            p = heads_view(Pb[:, n % 4, :], heads)
                            pool.tensor_tensor(p, p, along(rinv[:, n % 4, 0:heads], 512 // heads), ALU.mult).then_inc(sems["norm_done"], 1)

                    def after(half):
                        for what, s in plan.after.get(half, []):
                            b = plan.steps[s][1]
                            if what == "output":
                                pool.wait_ge(sems["var_ready"], s + 1)
                                pool.tensor_tensor(rstd[:, b:b + 1], ve[:, b:b + 1], neg_half[:, 0:1], ALU.pow).then_inc(sems["rstd_ready"], 1)
                            if what == "normalise" and plan.affine_next(s):
                                pool.wait_ge(sems["stat2_ready"], 1 + sum(plan.affine_next(t) for t in range(s)))
                                pool.tensor_tensor(rstd2[:, b:b + 1], ve2[:, b:b + 1], neg_half[:, 0:1], ALU.pow).then_inc(sems["rstd2_ready"], 1)

                    for n in plan.slots():
                        if last_loop and n == CTX_SLOT:
                            pool.wait_ge(sems["ctx_stats"], 1)
                            pool.tensor_tensor(rstd2[:, :], ve2[:, :], neg_half[:, :], ALU.pow).then_inc(sems["ctx_rstd"], 1)
                        after(2 * n)
                        for s in range(len(plan.steps)):
                            if plan.first[s] - AHEAD == n:
                                if plan.layer(s).out_bias:
                                    residual(s)
                                if plan.kind(s) == "ffn":
                                    start_sum(s)
                        if 0 <= n + AHEAD - 1 < plan.n:
                            probabilities(n + AHEAD - 1)
                        after(2 * n + 1)
                        for s in plan.spread.get(n, []):
                            spread(s)

            nc.all_engine_barrier(sems_to_clear=body_range)
            iters.__exit__(None, None, None)

        with ExitStack() as scope:
            w = {}
            for layer in LOOP_A:
                w[layer.name] = sb("w_" + layer.name, [P, sum(n for _, n in cols[layer.name].values())], scope=scope)
            qpe = sb("qpe", [P, 8, S], scope=scope)
            kpe = sb("kpe", [P, S], scope=scope)
            with nc.Block() as block:
                @block.sync
                def _(sp):
                    sp.dma_start(const[:, :], dram["const"]).then_inc(w_in["const"], 16)
                    first = LOOP_A[0].name
                    sp.dma_start(w[first][:, :], dram[first]).then_inc(w_in[first], 16)

                @block.vector
                def _(dve):
                    dve.wait_ge(w_in["const"], 16)
                    dve.tensor_copy(ident_b[:, :], ident)
                    dve.tensor_copy(causal_b[:, :, :], over(part(const, "const", "causal"), 4))

                @block.gpsimd
                def _(pool):
                    pool.memset(neg_half[:, :], -0.5)
                    pool.wait_ge(w_in["const"], 16)
                    pool.wait_ge(w_in["L0_attn"], 16)
                    pe_t = part(const, "const", "pe")
                    pool.tensor_tensor(qpe[:, :, :], over(pe_t, 8), along(part(w["L0_attn"], "L0_attn", "bq"), S), ALU.add)
                    pool.tensor_scalar(kpe[:, :], pe_t, part(w["L0_attn"], "L0_attn", "bkv")[:, 0:1], D ** -0.5, ALU.add, ALU.mult)
            run_loop("a_", Plan(LOOP_A), w, scope, False)

        with ExitStack() as scope:
            w = {}
            for layer in LOOP_C:
                w[layer.name] = sb("w_" + layer.name, [P, sum(n for _, n in cols[layer.name].values())], scope=scope)
            q_in = sem("q_in")
            fc1_q = sb("fc1_q", [P, 512], I32, scope=scope)
            fc2_q = sb("fc2_q", [P, 512], I32, scope=scope)
            fc1 = sb("fc1", [P, 512], scope=scope)
            fc2 = sb("fc2", [P, 4, D], scope=scope)
            half_b2 = sb("half_b2", [P, D], scope=scope)
            state_t = sb("state_t", [P, B, S], scope=scope)
            with ExitStack() as own:
                quantised_ffn(nc, sb, sem, own, w, w_in, dram, cols, state, state_t, ident, neg_half,
                              score_bank + [second_bank, value_bank] + proj_bank, q_in, fc1_q, fc2_q)
            score_w = sb("score_w", [P, 16, D], scope=scope)
            score_w_full, score_w_taken = sem("score_w_full"), sem("score_w_taken")
            with nc.Block() as block:
                @block.tensor
                def _(pe):
                    pe.wait_ge(w_in["L3_xattn"], 16)
                    q, k = (part(w["L3_xattn"], "L3_xattn", n) for n in ("WqT", "WkT"))
                    for h in range(16):
                        rows, c = slice(64 * (h % 2), 64 * (h % 2) + 64), h // 2
                        pe.matmul(score_bank[h % 2][:, (h // 2 % 4) * D:(h // 2 % 4 + 1) * D] if h < 8 else
                                  (score_bank[2], second_bank)[h % 2][:, (h // 2 % 4) * D:(h // 2 % 4 + 1) * D],
                                  q[rows, c * D:(c + 1) * D], k[rows, c * D:(c + 1) * D], start=True, stop=True).then_inc(score_w_full, 1)

                @block.scalar
                def _(act):
                    act.wait_ge(score_w_full, 16)
                    for half in range(2):
                        for odd in range(2):
                            bank = (score_bank[:2], (score_bank[2], second_bank))[half][odd]
                            heads = score_w[:, 8 * half:8 * half + 8, :].rearrange("p (c o) d -> p c o d", o=2)[:, :, odd, :]
                            act.activation(heads, heads_view(bank[:, :], 4), ACT.Copy, scale=0.125).then_inc(score_w_taken, 1)

                @block.vector
                def _(dve):
                    dve.wait_ge(w_in["L3_ffn"], 16)
                    dve.wait_ge(q_in, 32)
                    ffn = w["L3_ffn"]
                    dve.scalar_tensor_tensor(fc1[:, :], fc1_q[:, :], -128.0, part(ffn, "L3_ffn", "fc1_s"), ALU.add, ALU.mult)
                    dve.scalar_tensor_tensor(fc2[:, :, :].rearrange("p c d -> p (c d)"), fc2_q[:, :], -128.0, part(ffn, "L3_ffn", "fc2_s"), ALU.add, ALU.mult)
                    dve.tensor_scalar(half_b2[:, :], part(ffn, "L3_ffn", "fc2_b"), 0.5, None, ALU.mult)
            run_loop("c_", Plan(LOOP_C), w, scope, True, state_t, score_w)


def rope_tables():
    f = np.float32
    pos = np.arange(S, dtype=f)
    freq2 = (f(1.0) / f(10000.0) ** (np.arange(0, 8, 2, dtype=f) / f(8))).astype(f)
    freq3 = (f(10000.0) ** (-np.arange(0, 8, 2, dtype=f) / f(8))).astype(f)
    a2 = (freq2[np.arange(8) % 4][:, None] * pos[None, :]).astype(f)
    a3 = (freq3[np.arange(8) // 2][:, None] * pos[None, :]).astype(f)
    sign2 = np.where(np.arange(8) < 4, -1, 1).astype(f)[:, None]
    sign3 = np.where(np.arange(8) % 2 == 0, -1, 1).astype(f)[:, None]
    rows = lambda a: np.tile(a.astype(f), (16, 1))
    return rows(np.cos(a2)), rows(np.sin(a2) * sign2), rows(np.cos(a3)), rows(np.sin(a3) * sign3)


def constants():
    f = np.float32
    p = np.arange(P)
    pick = (p[:, None] % 32 // 8 == np.arange(4)[None, :]).astype(f)
    group = np.where(pick > 0, f(1.0 / np.sqrt(f(8.0))), f(0))
    vpick = np.broadcast_to(pick.T.reshape(1, 4 * P), (P, 4 * P))
    lower = np.broadcast_to(np.tril(np.ones((NE, NE), f), -1).reshape(1, NE * NE), (P, NE * NE))
    causal = np.where(np.tril(np.ones((S, S), bool)), 0, NEG).astype(f)
    pos = np.arange(S, dtype=f)[:, None]
    ang = pos * np.exp(f(-np.log(10000.0)) * np.arange(0, D, 2, dtype=f) / f(D))[None, :]
    pe = np.zeros((S, D), f)
    pe[:, 0::2], pe[:, 1::2] = np.sin(ang), np.cos(ang)
    return [("ident", np.eye(P, dtype=f)), ("group", group), ("vpick", vpick), ("lower", lower), ("causal", causal), ("pe", pe.T)]


def laid_out(i):
    def column(v):
        return v.reshape(-1, P).T

    def row(v):
        return np.broadcast_to(v.reshape(1, -1), (P, v.size))

    def chunks(m):
        return m.reshape(-1, P, m.shape[1]).transpose(1, 0, 2).reshape(P, -1)

    def rows_below(m):
        return np.concatenate([m, np.zeros((P - m.shape[0], m.shape[1]), m.dtype)], axis=0)

    def padded(m, n):
        return np.concatenate([m, np.zeros((P, n - m.shape[1]), m.dtype)], axis=1)

    cos2, sin2, cos3, sin3 = rope_tables()
    d = np.arange(P)
    turn2, turn3 = d // 8 * 8 + (d % 8 + 4) % 8, d ^ 1
    rel = np.arange(WINDOW)[:, None] - np.arange(WINDOW)[None, :] + WINDOW - 1
    relpos = np.full((S, 16, S), NEG, np.float32)
    for k in range(0, S, WINDOW):
        relpos[k:k + WINDOW, :, k:k + WINDOW] = i["L1_attn_rel_bias"][rel].transpose(0, 2, 1)
    packs = {"const": constants()}
    packs["L0_attn"] = [("Wq", i["L0_attn_Wq"]), ("Wkv", i["L0_attn_Wkv"]), ("Wo", chunks(i["L0_attn_Wo"])),
                        ("bq", column(i["L0_attn_bq"])), ("bkv", column(i["L0_attn_bkv"]))]
    for n in ("L0_xattn", "L1_xattn"):
        packs[n] = [(k, i[f"{n}_{k}"]) for k in ("Wq", "Wk", "Wv", "Wo")] + [(k, column(i[f"{n}_{k}"])) for k in ("bq", "bk", "bv")] + [("bo", row(i[f"{n}_bo"]))]
    packs["L0_ffn"] = [("Wr", padded(i["L0_ffn_router_w"].T, 64)),
                       ("gate_w", i["L0_ffn_gate_w"].transpose(1, 0, 2).reshape(P, -1)), ("up_w", i["L0_ffn_up_w"].transpose(1, 0, 2).reshape(P, -1)),
                       ("down_w", chunks(i["L0_ffn_down_w"].reshape(-1, D))),
                       ("gate_b", column(i["L0_ffn_gate_b"].reshape(-1))), ("up_b", column(i["L0_ffn_up_b"].reshape(-1))), ("be", rows_below(i["L0_ffn_down_b"]))]
    qkv, qkv_b = i["L1_attn_qkv_w"], i["L1_attn_qkv_b"]
    packs["L1_attn"] = [("Wq", qkv[:, 0:D]), ("Wk", qkv[:, D:2 * D]), ("Wv", qkv[:, 2 * D:]), ("Wo", i["L1_attn_proj_w"]),
                        ("bq", column(qkv_b[0:D])), ("bk", column(qkv_b[D:2 * D])), ("bv", column(qkv_b[2 * D:])), ("bo", row(i["L1_attn_proj_b"])),
                        ("relpos", relpos.reshape(P, 4, 4, S).transpose(0, 2, 1, 3).reshape(P, -1))]
    packs["L1_ffn"] = [("Wr", padded(i["L1_ffn_Wg"], 64)), ("We", i["L1_ffn_We"].transpose(1, 0, 2).reshape(P, -1)), ("be", rows_below(i["L1_ffn_be"])), ("bg", row(i["L1_ffn_bg"]))]
    for n, turned, q, c, s in (("L2_attn", turn2, "W_", cos2, sin2), ("L3_attn", turn3, "W", cos3, sin3)):
        wq, wk, wv, wo = (i[f"{n}_{q}{k}"].T for k in (("Q", "K", "V", "O") if q == "W_" else ("q", "k", "v", "o")))
        packs[n] = [("Wq", wq), ("Wk", wk), ("Wv", wv), ("Wo", wo), ("Wq_turned", wq[:, turned]), ("Wk_turned", wk[:, turned]), ("cos", c), ("sin", s)]
    packs["L2_xattn"] = [("Wq", i["L2_xattn_Wq"]), ("Wk", i["L2_xattn_Wkv"][:, :1024]), ("Wv", i["L2_xattn_Wkv"][:, 1024:]), ("Wo", chunks(i["L2_xattn_Wo"])),
                         ("bo", row(i["L2_xattn_bo"]))]
    packs["L2_ffn"] = [("gate", chunks(i["L2_ffn_w_gate"])), ("up", chunks(i["L2_ffn_w_up"])), ("down", i["L2_ffn_w_down"])]
    packs["L3_xattn"] = [("WqT", chunks(i["L3_xattn_Wq"].T)), ("WkT", chunks(i["L3_xattn_Wkv"][:, :1024].T)), ("Wv", i["L3_xattn_Wkv"][:, 1024:]), ("Wo", chunks(i["L3_xattn_Wout"]))] + [
        (k, column(i[f"L3_xattn_{k}"])) for k in ("g1", "b1", "g2", "b2")]
    packs["L3_ffn"] = [("gamma", column(i["L3_ffn_ln_gamma"])), ("beta", column(i["L3_ffn_ln_beta"])), ("fc1_s", row(i["L3_ffn_fc1_scales"])),
                       ("fc1_b", column(i["L3_ffn_fc1_bias"])), ("fc2_s", row(i["L3_ffn_fc2_scales"])), ("fc2_b", row(i["L3_ffn_fc2_bias"]))]
    return packs


def kernel(**inputs):
    import concourse.bacc as bacc
    from concourse.bass_utils import run_bass_kernel_spmd

    i = {k: np.asarray(v) for k, v in inputs.items()}
    packs = laid_out(i)
    arrays, cols = {}, {}
    for name, parts in packs.items():
        cols[name], at = {}, 0
        for k, a in parts:
            cols[name][k] = (at, a.shape[1])
            at += a.shape[1]
        arrays[name] = np.ascontiguousarray(np.concatenate([a for _, a in parts], axis=1))
    tokens = lambda a: np.ascontiguousarray(a.reshape(NIT, G, S, D).transpose(0, 2, 1, 3).reshape(NIT, P, G * D))
    widths = lambda a: np.ascontiguousarray(a.reshape(NIT, G, S, D).transpose(0, 3, 1, 2).reshape(NIT, P, G * S))
    arrays["x"], arrays["xT"] = tokens(i["x"]), widths(i["x"])
    arrays["ctx"], arrays["ctxT"] = tokens(i["ctx_1024"]), widths(i["ctx_1024"])
    for k in ("bk0", "bk1"):
        arrays["mask_" + k] = np.ascontiguousarray(i["mask_BxS2_" + k]).reshape(NIT, G * S)
    for k in ("x", "xT", "ctxT", "mask_bk1"):
        arrays[k] = np.concatenate([arrays[k], np.zeros_like(arrays[k][:1])])
    arrays["fc1_q"] = np.ascontiguousarray(i["L3_ffn_fc1_q"])
    arrays["fc2_q"] = np.ascontiguousarray(i["L3_ffn_fc2_q"].reshape(4, P, D).transpose(1, 0, 2).reshape(P, 4 * D))

    nc = bacc.Bacc("TRN2", target_bir_lowering=False, num_devices=1)
    dram, feed = {}, {}
    for name, a in arrays.items():
        dram[name] = nc.dram_tensor("in_" + name, a.shape, mybir.dt.from_np(a.dtype), kind="ExternalInput").ap()
        feed["in_" + name] = a
    out = nc.dram_tensor("out", (B, S, D), F32, kind="ExternalOutput").ap()
    decoder_kernel(nc, dram, out, cols)
    r = run_bass_kernel_spmd(nc, [feed], core_ids=[0])
    return r.results[0]["out"]
```
